# Optimizing a Trainium2 kernel written in Bass

```python
import numpy as np
import jax
import jax.numpy as jnp

def _softmax(x, axis=-1):
    return jax.nn.softmax(x, axis=axis)

def _gelu(x):
    return jax.nn.gelu(x, approximate=True)

def _silu(x):
    return jax.nn.silu(x)

def _sigmoid(x):
    return jax.nn.sigmoid(x)

def _layernorm(x, axis=-1, eps=1e-05):
    m = jnp.mean(x, axis=axis, keepdims=True)
    v = jnp.var(x, axis=axis, keepdims=True)
    return (x - m) / jnp.sqrt(v + eps)

def _scatter_add(tgt, idx, src, axis=0):
    return tgt.at[idx].add(src)

def _segment_sum(src, seg, n):
    return jax.ops.segment_sum(src, seg, n)
kernel_name = 'mk_early_fusion_d1_tok_img1024_r4_e7c503'

def setup_inputs(seed: int=0):
    np.random.seed(seed)
    _w = jnp.asarray

    def _rec_inputs():
        import jax
        import jax.numpy as jnp
        _rk = jax.random.key(seed)
        x = -0.000356955 + 1 * jax.random.normal(jax.random.fold_in(_rk, 1), (32, 3, 224, 224), jnp.float32)
        txt = 0.000100671 + 0.999662 * jax.random.normal(jax.random.fold_in(_rk, 2), (32, 128, 256), jnp.float32)
        return (x, txt)
    x, txt = _rec_inputs()

    def _L0_tok_setup():
        import jax, jax.numpy as jnp
        import numpy as np
        EMBED_DIM = 256
        PATCH = 14
        GRID = 16
        PATCH_DIM = 3 * PATCH * PATCH
        key = jax.random.key(seed)
        k1, k2, k3 = jax.random.split(key, 3)
        x = jax.random.normal(k1, (128, 3, 224, 224), dtype=jnp.float32)
        W = jax.random.normal(k2, (EMBED_DIM, PATCH_DIM), dtype=jnp.float32) * (1.0 / np.sqrt(PATCH_DIM))
        b = jax.random.normal(k3, (EMBED_DIM,), dtype=jnp.float32) * 0.01
        return {'x': x, 'W': W, 'b': b}
    _L0_tok_all = _L0_tok_setup()
    _L0_tok_in = {k: v for k, v in _L0_tok_all.items() if k in ('W', 'b')}
    del _L0_tok_all

    def _L0_attn_setup():
        import jax, jax.numpy as jnp
        import numpy as np
        DIM = 256
        HEADS = 16
        HIDDEN = 512
        EPS = 1e-06

        def _rmsnorm(x, scale):
            norm = jnp.linalg.norm(x, axis=-1, keepdims=True)
            return x * (scale * (x.shape[-1] ** 0.5 + EPS) / norm)
        key = jax.random.key(seed)
        ks = jax.random.split(key, 8)
        B, N, C = (4, 1024, DIM)
        s = 0.02
        return {'x': jax.random.normal(ks[0], (B, N, C), dtype=jnp.float32), 'scale1': jnp.ones((C,), jnp.float32), 'scale2': jnp.ones((C,), jnp.float32), 'gamma': jnp.ones((C,), jnp.float32), 'qkv_w': jax.random.normal(ks[1], (3 * C, C), jnp.float32) * s, 'proj_w': jax.random.normal(ks[2], (C, C), jnp.float32) * s, 'proj_b': jnp.zeros((C,), jnp.float32), 'conv1_w': jax.random.normal(ks[3], (HIDDEN, C), jnp.float32) * s, 'conv1_b': jnp.zeros((HIDDEN,), jnp.float32), 'conv2_w': jax.random.normal(ks[4], (C, HIDDEN), jnp.float32) * s, 'conv2_b': jnp.zeros((C,), jnp.float32)}
    _L0_attn_all = _L0_attn_setup()
    _L0_attn_in = {k: v for k, v in _L0_attn_all.items() if k in ('scale1', 'scale2', 'gamma', 'qkv_w', 'proj_w', 'proj_b', 'conv1_w', 'conv1_b', 'conv2_w', 'conv2_b')}
    del _L0_attn_all

    def _L0_ffn_setup():
        import jax, jax.numpy as jnp
        import numpy as np
        EPS = 1e-06
        LN_EPS = 1e-05

        def _absmean_core(W):
            gamma = jnp.mean(jnp.abs(W)) + EPS
            Ws = W / gamma
            Wq = jnp.sign(Ws) * jnp.minimum(jnp.round(jnp.abs(Ws)), 1.0)
            return (Wq, gamma)

        @jax.custom_vjp
        def absmean(W):
            return _absmean_core(W)[0]

        def _absmean_fwd(W):
            Wq, gamma = _absmean_core(W)
            return (Wq, gamma)

        def _absmean_bwd(gamma, g):
            return (g / gamma,)
        absmean.defvjp(_absmean_fwd, _absmean_bwd)

        def layernorm(x, w, b, eps=LN_EPS):
            mu = jnp.mean(x, axis=-1, keepdims=True)
            var = jnp.mean((x - mu) ** 2, axis=-1, keepdims=True)
            return (x - mu) * jax.lax.rsqrt(var + eps) * w + b
        key = jax.random.key(seed)
        k1, k2, k3 = jax.random.split(key, 3)
        d, h = (256, 1024)
        B, T = (8, 512)
        return {'x': jax.random.normal(k1, (B, T, d), jnp.float32), 'W_fc': jax.random.normal(k2, (h, d), jnp.float32), 'ln_w': jnp.ones((h,), jnp.float32), 'ln_b': jnp.zeros((h,), jnp.float32), 'W_proj': jax.random.normal(k3, (d, h), jnp.float32)}
    _L0_ffn_all = _L0_ffn_setup()
    _L0_ffn_in = {k: v for k, v in _L0_ffn_all.items() if k in ('W_fc', 'ln_w', 'ln_b', 'W_proj')}
    del _L0_ffn_all
    return {'x': x, 'txt': txt, 'L0_tok_W': _L0_tok_in['W'], 'L0_tok_b': _L0_tok_in['b'], 'L0_attn_scale1': _L0_attn_in['scale1'], 'L0_attn_scale2': _L0_attn_in['scale2'], 'L0_attn_gamma': _L0_attn_in['gamma'], 'L0_attn_qkv_w': _L0_attn_in['qkv_w'], 'L0_attn_proj_w': _L0_attn_in['proj_w'], 'L0_attn_proj_b': _L0_attn_in['proj_b'], 'L0_attn_conv1_w': _L0_attn_in['conv1_w'], 'L0_attn_conv1_b': _L0_attn_in['conv1_b'], 'L0_attn_conv2_w': _L0_attn_in['conv2_w'], 'L0_attn_conv2_b': _L0_attn_in['conv2_b'], 'L0_ffn_W_fc': _L0_ffn_in['W_fc'], 'L0_ffn_ln_w': _L0_ffn_in['ln_w'], 'L0_ffn_ln_b': _L0_ffn_in['ln_b'], 'L0_ffn_W_proj': _L0_ffn_in['W_proj']}

def reference(x, txt, L0_tok_W, L0_tok_b, L0_attn_scale1, L0_attn_scale2, L0_attn_gamma, L0_attn_qkv_w, L0_attn_proj_w, L0_attn_proj_b, L0_attn_conv1_w, L0_attn_conv1_b, L0_attn_conv2_w, L0_attn_conv2_b, L0_ffn_W_fc, L0_ffn_ln_w, L0_ffn_ln_b, L0_ffn_W_proj):
    import jax
    import jax.numpy as jnp

    def _L0_tok_ref(x, W, b):
        import jax, jax.numpy as jnp
        import numpy as np
        EMBED_DIM = 256
        PATCH = 14
        GRID = 16
        PATCH_DIM = 3 * PATCH * PATCH
        B, C, H, Wd = x.shape
        patches = x.reshape(B, C, GRID, PATCH, GRID, PATCH)
        patches = patches.transpose(0, 2, 4, 1, 3, 5)
        patches = patches.reshape(B, GRID * GRID, PATCH_DIM)
        return jnp.einsum('bpk,ek->bpe', patches, W) + b

    def _L0_attn_ref(x, scale1, scale2, gamma, qkv_w, proj_w, proj_b, conv1_w, conv1_b, conv2_w, conv2_b):
        import jax, jax.numpy as jnp
        import numpy as np
        DIM = 256
        HEADS = 16
        HIDDEN = 512
        EPS = 1e-06

        def _rmsnorm(x, scale):
            norm = jnp.linalg.norm(x, axis=-1, keepdims=True)
            return x * (scale * (x.shape[-1] ** 0.5 + EPS) / norm)
        B, N, C = x.shape
        h, d = (HEADS, C // HEADS)
        xn = _rmsnorm(x, scale1)
        qkv = jnp.einsum('bnc,fc->bnf', xn, qkv_w)
        qkv = qkv.reshape(B, N, 3, h, d).transpose(2, 0, 3, 1, 4)
        q, k, v = (qkv[0], qkv[1], qkv[2])
        phi = lambda t: jnp.exp(-0.5 * t * t)
        q, k = (phi(q), phi(k))
        kv = jnp.einsum('bhnd,bhne->bhde', k, v)
        z = 1.0 / (jnp.einsum('bhnd,bhd->bhn', q, k.sum(2)) + 1e-06)
        out = jnp.einsum('bhnd,bhde,bhn->bhne', q, kv, z)
        out = out.transpose(0, 2, 1, 3).reshape(B, N, C)
        attn = jnp.einsum('bnc,oc->bno', out, proj_w) + proj_b
        x = x + gamma * attn
        xn2 = _rmsnorm(x, scale2)
        hdd = jax.nn.gelu(jnp.einsum('bnc,hc->bnh', xn2, conv1_w) + conv1_b, approximate=False)
        mlp = jnp.einsum('bnh,ch->bnc', hdd, conv2_w) + conv2_b
        return x + gamma * mlp

    def _L0_ffn_ref(x, W_fc, ln_w, ln_b, W_proj):
        import jax, jax.numpy as jnp
        import numpy as np
        EPS = 1e-06
        LN_EPS = 1e-05

        def _absmean_core(W):
            gamma = jnp.mean(jnp.abs(W)) + EPS
            Ws = W / gamma
            Wq = jnp.sign(Ws) * jnp.minimum(jnp.round(jnp.abs(Ws)), 1.0)
            return (Wq, gamma)

        @jax.custom_vjp
        def absmean(W):
            return _absmean_core(W)[0]

        def _absmean_fwd(W):
            Wq, gamma = _absmean_core(W)
            return (Wq, gamma)

        def _absmean_bwd(gamma, g):
            return (g / gamma,)
        absmean.defvjp(_absmean_fwd, _absmean_bwd)

        def layernorm(x, w, b, eps=LN_EPS):
            mu = jnp.mean(x, axis=-1, keepdims=True)
            var = jnp.mean((x - mu) ** 2, axis=-1, keepdims=True)
            return (x - mu) * jax.lax.rsqrt(var + eps) * w + b
        h = jnp.einsum('btd,hd->bth', x, absmean(W_fc))
        h = jax.nn.gelu(h, approximate=False)
        h = layernorm(h, ln_w, ln_b)
        return jnp.einsum('bth,dh->btd', h, absmean(W_proj))
    h = _L0_tok_ref(x, L0_tok_W, L0_tok_b)
    h = jnp.concatenate([h, txt], axis=1)
    h = h + _L0_attn_ref(_layernorm(h, axis=-1), L0_attn_scale1, L0_attn_scale2, L0_attn_gamma, L0_attn_qkv_w, L0_attn_proj_w, L0_attn_proj_b, L0_attn_conv1_w, L0_attn_conv1_b, L0_attn_conv2_w, L0_attn_conv2_b)
    h = h + _L0_ffn_ref(_layernorm(h, axis=-1), L0_ffn_W_fc, L0_ffn_ln_w, L0_ffn_ln_b, L0_ffn_W_proj)
    return h

_drawn_inputs = setup_inputs


def setup_inputs(seed=0):
    import zlib

    import numpy as np

    out = dict(_drawn_inputs(seed))
    spreads = {'L0_attn_scale1': (1.0, 0.6),
     'L0_attn_scale2': (1.0, 0.6),
     'L0_attn_gamma': (1.0, 0.6),
     'L0_attn_proj_b': (0.0, 0.1),
     'L0_attn_conv1_b': (0.0, 0.535),
     'L0_attn_conv2_b': (0.0, 0.1),
     'L0_ffn_ln_w': (1.0, 0.2),
     'L0_ffn_ln_b': (0.0, 0.1)}
    factors = {'L0_tok_b': 5.374, 'L0_attn_qkv_w': 8.0, 'L0_attn_proj_w': 8.0}
    for name, (base, spread) in spreads.items():
        noise = np.random.default_rng([zlib.crc32(name.encode()), seed]).standard_normal(out[name].shape)
        drawn = base * np.exp(spread * noise) if base else spread * noise
        out[name] = jnp.asarray(drawn.astype(out[name].dtype))
    for name, factor in factors.items():
        out[name] = (out[name] * factor).astype(out[name].dtype)
    return out
```

```python
import numpy as np
from contextlib import ExitStack

import concourse.bass as bass
from concourse import mybir

P = 128
BATCHES = 32
GRID, PATCH, CHANNELS = 16, 14, 3
PATCHES = GRID * GRID
PIXELS = CHANNELS * PATCH * PATCH
TEXT = 128
TOKENS = PATCHES + TEXT
TILES = TOKENS // P
IMAGE_TILES = PATCHES // P
DIM = 256
GROUPS = DIM // P
HEADS, HEAD = 16, 16
GROUP_HEADS = P // HEAD
HIDDEN = 512
HIDDEN_TILES = HIDDEN // P
WIDE = 1024
WIDE_TILES = WIDE // P
FULL = PIXELS // P
REST = PIXELS - FULL * P
LN_EPS = 1e-5
RMS_EPS = 1e-6

WEIGHT_SCALE = 64.0
KV_SCALE = 1.0 / 64
Q_SCALE = 16384.0
OUT_SCALE = 8.0
GELU_SCALE = 16.0
ATTN_SCALE = OUT_SCALE * WEIGHT_SCALE
MLP_SCALE = GELU_SCALE * WEIGHT_SCALE
RMS_FACTOR = (DIM ** 0.5 + RMS_EPS) / DIM ** 0.5
DEN_EPS = 1e-6 * Q_SCALE * KV_SCALE

FIRST_LOOPED, LAST_LOOPED = 4, 29


def build(nc, image, text, tok_w, tok_b, scale1, scale2, gamma, qkv_w, proj_w, proj_b, conv1_w,
          conv1_b, conv2_w, conv2_b, fc_w, ln_w, ln_b, ffn_w, out):
    fp32, fp16, bf16 = mybir.dt.float32, mybir.dt.float16, mybir.dt.bfloat16
    ALU, ACT, AX = mybir.AluOpType, mybir.ActivationFunctionType, mybir.AxisListType

    text_v = text.rearrange("b p e -> b p e")
    out_v = out.rearrange("b (t p) e -> b p t e", p=P)

    ctx = ExitStack()
    with ctx:
        def sb(name, shape, dt=fp32):
            return ctx.enter_context(nc.sbuf_tensor(name, shape, dt))

        def sem(name):
            return ctx.enter_context(nc.semaphore(name))

        tok_wT = sb("tok_wT", [P, FULL + 1, DIM])
        qkv_hi, qkv_lo = (sb(f"qkv_{s}", [P, GROUPS, 3 * DIM], fp16) for s in ("hi", "lo"))
        proj_hi, proj_lo = (sb(f"proj_{s}", [P, GROUPS, DIM], fp16) for s in ("hi", "lo"))
        conv1_hi, conv1_lo = (sb(f"conv1_{s}", [P, GROUPS, HIDDEN], fp16) for s in ("hi", "lo"))
        conv2_hi, conv2_lo = (sb(f"conv2_{s}", [P, HIDDEN_TILES, DIM], fp16) for s in ("hi", "lo"))
        fc_q = sb("fc_q", [P, GROUPS, WIDE], fp16)
        ffn_q = sb("ffn_q", [P, WIDE_TILES, DIM], fp16)
        attn_bias, mlp_bias = (sb(f"{s}_bias", [P, DIM], bf16) for s in ("attn", "mlp"))
        ones_bf = sb("ones_bf", [P, P], bf16)
        conv1_bias = sb("conv1_bias", [P, HIDDEN_TILES])
        ln_w_all = sb("ln_w_all", [P, WIDE])
        ln_shift = sb("ln_shift", [P, DIM])
        identity = sb("identity", [P, P])
        head_mask = sb("head_mask", [P, GROUP_HEADS])
        block_mask = sb("block_mask", [P, GROUP_HEADS, HEAD])
        minus_half = sb("minus_half", [P, 8])
        minus_inv_wide, inv_wide, eps, attn_scale = (
            sb(s, [P, 8]) for s in ("minus_inv_wide", "inv_wide", "eps", "attn_scale"))
        spacer = sb("spacer", [P, 1])

        scales = sb("scales", [P, 2 * GROUPS])
        gamma_all = sb("gamma_all", [P, DIM])
        bias_all = sb("bias_all", [P, 2, DIM])
        bias_rest = sb("bias_rest", [P, DIM])
        absolute = sb("absolute", [P, 32])
        absolute_sum = sb("absolute_sum", [P, 2])
        ones_f = sb("ones_f", [P, P])
        threshold = sb("threshold", [P, 4])
        ln_b_cols = sb("ln_b_cols", [P, WIDE_TILES])

        pixels = [sb(f"pixels{p}", [P, FULL + 1, PATCHES]) for p in range(2)]
        h = [sb(f"h{p}", [P, TILES, DIM]) for p in range(2)]
        a = [sb(f"a{p}", [P, TILES, DIM]) for p in range(2)]
        ratio = [sb(f"ratio{p}", [P, TILES]) for p in range(2)]
        stats1 = sb("stats1", [P, TILES, 6])
        mv1 = sb("mv1", [P, TILES, 2])
        var1 = sb("var1", [P, TILES])
        rstd1 = sb("rstd1", [P, 2 * TILES])
        ratio_part = sb("ratio_part", [P, 2 * TILES])
        aT_hi, aT_lo = (sb(f"aT_{s}", [P, GROUPS, TOKENS], fp16) for s in ("hi", "lo"))
        k_square = sb("k_square", [P, TILES, DIM])
        k = sb("k", [P, TILES, DIM])
        v = sb("v", [P, TILES, GROUPS, P + 1])
        q_square = sb("q_square", [P, GROUPS, TOKENS])
        q = sb("q", [P, GROUPS, TOKENS])
        q_hi, q_lo = (sb(f"q_{s}", [P, GROUPS, TOKENS], fp16) for s in ("hi", "lo"))
        kv = sb("kv", [P, GROUPS, P + GROUP_HEADS])
        kv_hi, kv_lo = (sb(f"kv_{s}", [P, GROUPS, P + GROUP_HEADS], fp16) for s in ("hi", "lo"))
        den = sb("den", [P, GROUPS, TILES, GROUP_HEADS])
        z = sb("z", [P, GROUPS, TILES, GROUP_HEADS])
        read = sb("read", [P, TILES, DIM])
        readT_hi, readT_lo = (sb(f"readT_{s}", [P, GROUPS, TOKENS], fp16) for s in ("hi", "lo"))
        x1 = sb("x1", [P, TILES, DIM])
        unread1, unread_g = sb("unread1", [P, TILES, DIM], bf16), sb("unread_g", [P, TILES, WIDE], bf16)
        squares1 = sb("squares1", [P, TILES])
        rms = sb("rms", [P, TILES])
        xn = sb("xn", [P, TILES, DIM])
        hx = sb("hx", [P, TILES, DIM])
        xT_hi, xT_lo = (sb(f"xT_{s}", [P, GROUPS, TOKENS], fp16) for s in ("hi", "lo"))
        hid = sb("hid", [P, HIDDEN_TILES, TOKENS])
        hid_hi, hid_lo = (sb(f"hid_{s}", [P, HIDDEN_TILES, TOKENS], fp16) for s in ("hi", "lo"))
        h2 = sb("h2", [P, TILES, DIM])
        h2s = [sb(f"h2s{p}", [P, TILES, DIM]) for p in range(2)]
        stats2 = sb("stats2", [P, TILES, 6])
        mv2 = sb("mv2", [P, TILES, 2])
        var2 = sb("var2", [P, TILES])
        rstd2 = sb("rstd2", [P, TILES])
        hn = sb("hn", [P, TILES, DIM])
        hT_hi, hT_lo = (sb(f"hT_{s}", [P, GROUPS, TOKENS], fp16) for s in ("hi", "lo"))
        g = sb("g", [P, TILES, WIDE])
        g_sum = sb("g_sum", [P, TILES])
        g_minus_mean = sb("g_minus_mean", [P, TILES])
        g_squares = sb("g_squares", [P, TILES])
        g_meansq = sb("g_meansq", [P, TILES])
        g_var = sb("g_var", [P, TILES])
        g_rstd = sb("g_rstd", [P, TILES])
        gc = sb("gc", [P, TILES, WIDE])
        gT_hi, gT_lo = (sb(f"gT_{s}", [P, TILES, WIDE_TILES, P], fp16) for s in ("hi", "lo"))
        result = [sb(f"result{p}", [P, TILES, DIM]) for p in range(2)]

        raw = gc[:, 0:2, :].rearrange("p t n -> p (t n)")
        ln_b_wide = gc[:, 2, :].rearrange("p (n f) -> p n f", n=WIDE_TILES)
        scaled = g[:, 0:2, :].rearrange("p t n -> p (t n)")
        ffn_q32 = scaled.rearrange("p (n f) -> p n f", n=WIDE_TILES)
        sign_lo = gT_hi[:, 0:2, :, :].rearrange("p t n f -> p (t n f)")

        BANK = 512
        A, B, C, D = (ctx.enter_context(nc.psum_tensor(f"pair_{s}", [P, 2 * BANK], fp32)) for s in "ABCD")

        def rows(pair):
            return pair[:, 0:TILES * DIM].rearrange("p (t e) -> p t e", t=TILES)

        def cols(pair):
            return pair[:, :].rearrange("p (g n) -> p g n", g=2)[:, :, 0:TOKENS]

        kv01_ps = A[:, :].rearrange("p (t n) -> p t n", t=2)
        kv2_ps = D[:, BANK:2 * BANK]
        xT_ps, q_ps, hT_ps = cols(B), cols(C), cols(A)
        hid01_ps, hid23_ps = cols(B), cols(C)
        g_ps = [D, B, B]
        kv_ps = A[:, 0:GROUPS * (P + 1)].rearrange("p (g n) -> p g n", g=GROUPS)
        mlp_ps = rows(C)
        gT_ps = [A, A, B]
        ND = P + GROUP_HEADS
        read_ps = D[:, :].rearrange("p (g n) -> p g n", g=2)[:, :, 0:TILES * ND].rearrange(
            "p g (t n) -> p g t n", t=TILES)
        tok_ps = C[:, 0:BANK].rearrange("p (t e) -> p t e", t=IMAGE_TILES)
        readT_ps, aT_ps = cols(D), cols(B)
        attn_ps = rows(A)
        ffn_ps = [C[:, BANK:BANK + DIM], C[:, 0:DIM], D[:, 0:DIM]]

        weights_loaded = [sem(f"weights_loaded{n}") for n in range(7)]
        setup_done = sem("setup_done")
        ones_row_set = sem("ones_row_set")
        setup_chain = sem("setup_chain")
        pool_chain = sem("pool_chain")
        raw_used = sem("raw_used")
        sums_on_pe = sem("sums_on_pe")
        weights_ready = sem("weights_ready")
        pixels_loaded = [sem(f"pixels_loaded{p}") for p in range(2)]
        text_loaded = [sem(f"text_loaded{p}") for p in range(2)]
        stored = [sem(f"stored{p}") for p in range(2)]
        (pe_kv01, pe_kv2, pe_xT, pe_q, pe_hT, pe_hid01, pe_hid23, pe_kv, pe_mlp, pe_read, pe_tok,
         pe_readT, pe_aT, pe_attn) = (sem(f"pe_{s}") for s in (
             "kv01", "kv2", "xT", "q", "hT", "hid01", "hid23", "kv", "mlp", "read", "tok",
             "readT", "aT", "attn"))
        pe_g, pe_gT, pe_ffn = ([sem(f"pe_{s}{t}") for t in range(TILES)] for s in ("g", "gT", "ffn"))
        (act_k01, act_k2, act_k, act_xT, act_q_square, act_q, act_hT, act_hid01, act_hid23, act_h,
         act_readT, act_squares1, act_aT) = (sem(f"act_{s}") for s in (
             "k01", "k2", "k", "xT", "q_square", "q", "hT", "hid01", "hid23", "h", "readT",
             "squares1", "aT"))
        act_g, act_g_squares, act_gT = ([sem(f"act_{s}{t}") for t in range(TILES)]
                                        for s in ("g", "g_squares", "gT"))
        (dve_v01, dve_v2, dve_xT, dve_q_hi, dve_q, dve_hT, dve_hid01_hi, dve_hid01, dve_hid23_hi,
         dve_hid23, dve_kv_masked, dve_kv_hi, dve_kv, dve_h2, dve_stats2, dve_mv2, dve_den, dve_z,
         dve_read, dve_hn, dve_stats1, dve_mv1, dve_readT, dve_a, dve_aT, dve_x1, dve_hx,
         dve_xn) = (sem(f"dve_{s}") for s in (
             "v01", "v2", "xT", "q_hi", "q", "hT", "hid01_hi", "hid01", "hid23_hi", "hid23",
             "kv_masked", "kv_hi", "kv", "h2", "stats2", "mv2", "den", "z", "read", "hn",
             "stats1", "mv1", "readT", "a", "aT", "x1", "hx", "xn"))
        dve_gc, dve_gT, dve_result = ([sem(f"dve_{s}{t}") for t in range(TILES)]
                                      for s in ("gc", "gT", "result"))
        (pool_var2, pool_rstd2, pool_h2s, pool_var1, pool_rstd1, pool_ratio_a, pool_ratio_b,
         pool_ratio, pool_g_meansq, pool_g_var, pool_g_rstd, pool_rms, pool_rstd1_eps) = (sem(f"pool_{s}") for s in (
             "var2", "rstd2", "h2s", "var1", "rstd1", "ratio_a", "ratio_b", "ratio",
             "g_meansq", "g_var", "g_rstd", "rms", "rstd1_eps"))
        pool_g_mean = [sem(f"pool_g_mean{t}") for t in range(TILES)]

        def reached(engine, semaphore, count):
            if not isinstance(count, int) or count > 0:
                engine.wait_ge(semaphore, count)

        class Step:

            def __init__(self, pair, parity):
                self.looped = not isinstance(pair, int)
                step = 2 * pair + parity
                self.parity = parity
                self.embed, self.attn, self.mlp, self.ffn, self.fetch = (
                    step + d if self.looped or 0 <= step + d < BATCHES else None
                    for d in (1, 0, -1, -2, 2))
                if self.looped:
                    self.pair = pair
                else:
                    self.pair = step // 2

        def run(engine, body):
            for step in range(-1, FIRST_LOOPED):
                body(Step(step // 2, step % 2))
            with engine.Fori(FIRST_LOOPED // 2, (LAST_LOOPED + 1) // 2) as pair:
                for parity in range(2):
                    body(Step(pair, parity))
            for step in range(LAST_LOOPED + 1, BATCHES + 2):
                body(Step(step // 2, step % 2))

        block = ctx.enter_context(nc.Block())

        @block.sync
        def _(sp):
            def columns(src, n):
                return src.rearrange("(n p) f -> p n f", p=P)

            sp.dma_start(tok_wT[:, 0:FULL, :], columns(tok_w[0:FULL * P, :], FULL)).then_inc(weights_loaded[0], 16)
            sp.dma_start(tok_wT[0:REST, FULL, :], tok_w[FULL * P:PIXELS, :]).then_inc(weights_loaded[0], 16)
            sp.dma_start(tok_wT[REST:REST + 1, FULL, :], tok_b[None, :]).then_inc(weights_loaded[0], 16)

            def fetch_pixels(b, parity, b_number):
                sp.dma_start(pixels[parity][:, 0:FULL, :],
                             image[b_number, 0:FULL * P, :].rearrange("(n p) f -> p n f", p=P)
                             ).then_inc(pixels_loaded[parity], 16)
                sp.dma_start(pixels[parity][0:REST, FULL, :],
                             image[b_number, FULL * P:PIXELS, :]).then_inc(pixels_loaded[parity], 16)

            sp.wait_ge(ones_row_set, 1)
            fetch_pixels(0, 0, 0)
            fetch_pixels(1, 1, 1)
            for i, col in enumerate((scale1, scale2)):
                for n in range(GROUPS):
                    sp.dma_start(scales[:, 2 * i + n:2 * i + n + 1],
                                 col[n * P:(n + 1) * P, None]).then_inc(weights_loaded[1], 16)
            sp.dma_start(gamma_all[:, :], gamma[None, :].to_broadcast([P, DIM])).then_inc(weights_loaded[1], 16)
            sp.dma_start(bias_all[:, 0, :], proj_b[None, :].to_broadcast([P, DIM])).then_inc(weights_loaded[1], 16)
            sp.dma_start(bias_all[:, 1, :], conv2_b[None, :].to_broadcast([P, DIM])).then_inc(weights_loaded[1], 16)
            sp.dma_start(raw[:, 0:GROUPS * 3 * DIM].rearrange("p (n f) -> p n f", n=GROUPS),
                         columns(qkv_w, GROUPS)).then_inc(weights_loaded[1], 16)
            sp.dma_start(ln_w_all[:, :], ln_w[None, :].to_broadcast([P, WIDE])).then_inc(weights_loaded[0], 16)
            for n in range(HIDDEN_TILES):
                sp.dma_start(conv1_bias[:, n:n + 1], conv1_b[n * P:(n + 1) * P, None]).then_inc(weights_loaded[0], 16)
            for n in range(WIDE_TILES):
                sp.dma_start(ln_b_cols[:, n:n + 1], ln_b[n * P:(n + 1) * P, None]).then_inc(weights_loaded[0], 16)
            for n, (src, groups) in enumerate(((proj_w, GROUPS), (conv1_w, GROUPS), (conv2_w, HIDDEN_TILES),
                                               (fc_w, GROUPS), (ffn_w, WIDE_TILES))):
                sp.wait_ge(raw_used, n + 1)
                width = src.shape[1]
                sp.dma_start(raw[:, 0:groups * width].rearrange("p (n f) -> p n f", n=groups),
                             columns(src, groups)).then_inc(weights_loaded[n + 2], 16)

            def body(s):
                if s.embed is not None:
                    p = 1 - s.parity
                    reached(sp, dve_hx, s.embed - 1)
                    sp.dma_start(h[p][:, IMAGE_TILES, :], text_v[s.embed, :, :]).then_inc(text_loaded[p], 16)
                if s.fetch is not None and not (isinstance(s.fetch, int) and s.fetch < 2):
                    reached(sp, pe_tok, s.fetch - 1)
                    fetch_pixels(s.fetch, s.parity, s.fetch)
                if s.ffn is not None:
                    for t in range(TILES):
                        reached(sp, dve_result[t], s.ffn + 1)
                    sp.dma_start(out_v[s.ffn, :, :, :], result[s.parity][:, :, :]).then_inc(stored[s.parity], 16)

            run(sp, body)
            for p in range(2):
                sp.wait_ge(stored[p], 16 * (BATCHES // 2))

        @block.gpsimd
        def _(pool):
            G = nc.gpsimd
            G.memset(identity[:, :], 0.0)
            G.memset(head_mask[:, :], 1.0)
            G.memset(minus_half[:, :], -0.5)
            G.memset(minus_inv_wide[:, :], -1.0 / WIDE)
            G.memset(inv_wide[:, :], 1.0 / WIDE)
            G.memset(eps[:, :], LN_EPS)
            G.memset(attn_scale[:, :], ATTN_SCALE)
            G.memset(ones_f[:, :], 1.0)
            G.memset(ones_bf[:, :], 1.0)
            G.memset(attn_bias[:, :], 0.0)
            G.memset(mlp_bias[:, :], 0.0)
            G.memset(v[:, :, :, P:P + 1], 1.0).then_inc(pool_chain, 1)
            pool.wait_ge(pool_chain, 1)
            G.affine_select(out=identity[:, :], in_=identity[:, :], compare_op=ALU.not_equal, fill=1.0,
                            base=0, pattern=[[-1, P]], channel_multiplier=1)
            G.affine_select(out=head_mask[:, :], in_=head_mask[:, :], compare_op=ALU.is_ge, fill=0.0,
                            base=0, pattern=[[-HEAD, GROUP_HEADS]], channel_multiplier=1).then_inc(pool_chain, 1)
            pool.wait_ge(pool_chain, 2)
            G.affine_select(out=head_mask[:, :], in_=head_mask[:, :], compare_op=ALU.is_ge, fill=0.0,
                            base=HEAD - 1, pattern=[[HEAD, GROUP_HEADS]], channel_multiplier=-1).then_inc(pool_chain, 1)
            pool.wait_ge(pool_chain, 3)
            G.tensor_copy(block_mask[:, :, :], head_mask[:, :, None].to_broadcast([P, GROUP_HEADS, HEAD])
                          ).then_inc(setup_done, 1)

            def power(dst, src, n, done):
                return G.tensor_tensor(dst, src, minus_half[:, 0:n], ALU.pow).then_inc(done, 1)

            def body(s):
                def g_mean(t):
                    reached(pool, act_g[t], s.ffn + 1)
                    reached(pool, dve_gc[t], s.ffn)
                    reached(pool, act_g_squares[t], s.ffn)
                    G.tensor_tensor(g_minus_mean[:, t:t + 1], g_sum[:, t:t + 1], minus_inv_wide[:, 0:1],
                                    ALU.mult).then_inc(pool_g_mean[t], 1)

                if s.ffn is not None:
                    g_mean(0)
                    g_mean(1)
                if s.mlp is not None:
                    b = s.mlp
                    reached(pool, dve_mv2, b + 1)
                    G.tensor_tensor(var2[:, :], mv2[:, :, 1], eps[:, 0:TILES], ALU.add).then_inc(pool_var2, 1)
                    reached(pool, pool_var2, b + 1)
                    reached(pool, dve_hn, b)
                    power(rstd2[:, :], var2[:, :], TILES, pool_rstd2)
                if s.ffn is not None:
                    g_mean(2)
                if s.mlp is not None:
                    b = s.mlp
                    for t in range(TILES):
                        reached(pool, dve_result[t], b - 1)
                    G.tensor_tensor(h2s[1 - s.parity][:, :, :], h2[:, :, :],
                                    ln_shift[:, None, :].to_broadcast([P, TILES, DIM]), ALU.add).then_inc(pool_h2s, 1)
                if s.embed is not None:
                    b, p = s.embed, 1 - s.parity
                    reached(pool, dve_mv1, b + 1)
                    reached(pool, dve_a, b)
                    power(rstd1[:, 0:TILES], mv1[:, :, 1], TILES, pool_rstd1)
                    G.tensor_tensor(var1[:, :], mv1[:, :, 1], eps[:, 0:TILES], ALU.add).then_inc(pool_var1, 1)
                    reached(pool, pool_var1, b + 1)
                    power(rstd1[:, TILES:2 * TILES], var1[:, :], TILES, pool_rstd1_eps)
                    reached(pool, pool_rstd1, b + 1)
                    G.tensor_tensor(ratio_part[:, 0:TILES], mv1[:, :, 1], rstd1[:, 0:TILES],
                                    ALU.mult).then_inc(pool_ratio_a, 1)
                    reached(pool, pool_rstd1_eps, b + 1)
                    reached(pool, pool_ratio_a, b + 1)
                    G.tensor_tensor(ratio_part[:, TILES:2 * TILES], ratio_part[:, 0:TILES],
                                    rstd1[:, TILES:2 * TILES], ALU.mult).then_inc(pool_ratio_b, 1)
                    reached(pool, pool_ratio_b, b + 1)
                    reached(pool, dve_x1, b - 1)
                    G.tensor_tensor(ratio[p][:, :], ratio_part[:, TILES:2 * TILES], attn_scale[:, 0:TILES],
                                    ALU.mult).then_inc(pool_ratio, 1)
                if s.ffn is not None:
                    b = s.ffn
                    for t in range(TILES):
                        reached(pool, act_g_squares[t], b + 1)
                    G.tensor_tensor(g_meansq[:, :], g_squares[:, :], inv_wide[:, 0:TILES], ALU.mult).then_inc(pool_g_meansq, 1)
                    reached(pool, pool_g_meansq, b + 1)
                    G.tensor_tensor(g_var[:, :], g_meansq[:, :], eps[:, 0:TILES], ALU.add).then_inc(pool_g_var, 1)
                    reached(pool, pool_g_var, b + 1)
                    for t in range(TILES):
                        reached(pool, dve_result[t], b)
                    power(g_rstd[:, :], g_var[:, :], TILES, pool_g_rstd)
                if s.attn is not None:
                    b = s.attn
                    reached(pool, act_squares1, b + 1)
                    reached(pool, dve_xn, b)
                    power(rms[:, :], squares1[:, :], TILES, pool_rms)

            run(pool, body)

        @block.vector
        def _(dve):
            V = nc.vector
            links = [0]

            def link(ins):
                links[0] += 1
                ins.then_inc(setup_chain, 1)
                dve.wait_ge(setup_chain, links[0])

            def split(hi, lo, src):
                link(V.tensor_copy(hi, src))
                link(V.tensor_tensor(lo, src, hi, ALU.subtract))

            def staged(n, groups):
                return raw[:, 0:n].rearrange("p (n f) -> p n f", n=groups)

            def staged_scaled(n, groups):
                return scaled[:, 0:n].rearrange("p (n f) -> p n f", n=groups)

            V.memset(pixels[0][64:P, FULL, :], 1.0)
            V.memset(pixels[1][64:P, FULL, :], 1.0).then_inc(ones_row_set, 1)
            dve.wait_ge(setup_done, 1)
            dve.wait_ge(weights_loaded[1], 16 * 8)
            for i in range(GROUPS):
                link(V.tensor_scalar(staged_scaled(1536, GROUPS)[:, i, :], staged(1536, GROUPS)[:, i, :],
                                     scales[:, i:i + 1], RMS_FACTOR * WEIGHT_SCALE, ALU.mult, ALU.mult))
            V.tensor_copy(bias_rest[0:1, 0:1], raw[0:1, 0:1]).then_inc(raw_used, 1)
            split(qkv_hi[:, :, :], qkv_lo[:, :, :], staged_scaled(1536, GROUPS))
            for which, (bias, dst, scale) in enumerate(((0, attn_bias, ATTN_SCALE), (1, mlp_bias, MLP_SCALE))):
                link(V.scalar_tensor_tensor(bias_rest[:, :], bias_all[:, bias, :], scale, gamma_all[:, :],
                                            ALU.mult, ALU.mult))
                for part in range(3):
                    at = slice(32 * part, 32 * part + 1)
                    link(V.tensor_copy(dst[at, :], bias_rest[at, :]))
                    if part < 2:
                        lower = [32 * r for r in range(part + 1, 3)]
                        for r in lower:
                            link(V.tensor_copy(sign_lo[r:r + 1, 0:2 * DIM].bitcast(bf16)[:, 0:DIM],
                                               bias_rest[r:r + 1, :]))
                            link(V.tensor_tensor(bias_rest[r:r + 1, :], bias_rest[r:r + 1, :],
                                                 sign_lo[r:r + 1, 0:2 * DIM].bitcast(bf16)[:, 0:DIM], ALU.subtract))
            dve.wait_ge(weights_loaded[2], 16)
            for i in range(GROUPS):
                link(V.scalar_tensor_tensor(staged_scaled(512, GROUPS)[:, i, :], staged(512, GROUPS)[:, i, :],
                                            WEIGHT_SCALE, gamma_all[:, :], ALU.mult, ALU.mult))
            V.tensor_copy(bias_rest[0:1, 0:1], raw[0:1, 0:1]).then_inc(raw_used, 1)
            split(proj_hi[:, :, :], proj_lo[:, :, :], staged_scaled(512, GROUPS))
            dve.wait_ge(weights_loaded[3], 16)
            for i in range(GROUPS):
                link(V.tensor_scalar(staged_scaled(1024, GROUPS)[:, i, :], staged(1024, GROUPS)[:, i, :],
                                     scales[:, GROUPS + i:GROUPS + i + 1], RMS_FACTOR * WEIGHT_SCALE,
                                     ALU.mult, ALU.mult))
            V.tensor_copy(bias_rest[0:1, 0:1], raw[0:1, 0:1]).then_inc(raw_used, 1)
            split(conv1_hi[:, :, :], conv1_lo[:, :, :], staged_scaled(1024, GROUPS))
            dve.wait_ge(weights_loaded[4], 16)
            for i in range(HIDDEN_TILES):
                link(V.scalar_tensor_tensor(staged_scaled(1024, HIDDEN_TILES)[:, i, :],
                                            staged(1024, HIDDEN_TILES)[:, i, :],
                                            WEIGHT_SCALE, gamma_all[:, :], ALU.mult, ALU.mult))
            V.tensor_copy(bias_rest[0:1, 0:1], raw[0:1, 0:1]).then_inc(raw_used, 1)
            split(conv2_hi[:, :, :], conv2_lo[:, :, :], staged_scaled(1024, HIDDEN_TILES))
            for which, (dst, n) in enumerate(((fc_q, 5), (ffn_q, 6))):
                dve.wait_ge(weights_loaded[n], 16)
                link(V.tensor_reduce(out=absolute[:, :], in_=raw[:, :].rearrange("p (n f) -> p n f", f=64),
                                     op=ALU.add, axis=AX.X, apply_absolute_value=True))
                link(V.tensor_reduce(out=absolute_sum[:, which:which + 1], in_=absolute[:, :], op=ALU.add, axis=AX.X))
                dve.wait_ge(sums_on_pe, which + 1)
                link(V.tensor_scalar(threshold[:, 0:1], A[:, which:which + 1], 1.0 / (WIDE * DIM), 1e-6,
                                     ALU.mult, ALU.add))
                link(V.tensor_scalar(threshold[:, 1:2], threshold[:, 0:1], 0.5, None, ALU.mult))
                link(V.tensor_scalar(threshold[:, 2:3], threshold[:, 0:1], -0.5, None, ALU.mult))
                flat = dst[:, :, :].rearrange("p n f -> p (n f)")
                link(V.tensor_scalar(sign_lo[:, :], raw[:, :], threshold[:, 2:3], None, ALU.is_lt))
                link(V.tensor_scalar(flat, raw[:, :], threshold[:, 1:2], None, ALU.is_gt))
                V.tensor_copy(bias_rest[0:1, 0:1], raw[0:1, 0:1]).then_inc(raw_used, 1)
                link(V.tensor_tensor(flat, flat, sign_lo[:, :], ALU.subtract))
            dve.wait_ge(weights_loaded[0], 16 * (4 + HIDDEN_TILES + WIDE_TILES))
            link(V.tensor_copy(ffn_q32[:, :, :], ffn_q[:, :, :]))
            link(V.tensor_copy(ln_b_wide[:, :, :], ln_b_cols[:, :, None].to_broadcast([P, WIDE_TILES, P])))
            dve.wait_ge(sums_on_pe, 3)
            link(V.tensor_copy(ln_shift[:, :], B[:, 0:DIM]))
            V.memset(absolute[:, 0:1], 0.0).then_inc(weights_ready, 1)

            def body(s):
                def low(dst, ps, hi, b, ready, war, war_count, done):
                    reached(dve, ready, b + 1)
                    reached(dve, war, war_count)
                    V.tensor_tensor(dst, ps, hi, ALU.subtract).then_inc(done, 1)

                def centre(t):
                    reached(dve, pool_g_mean[t], s.ffn + 1)
                    reached(dve, pe_gT[t], s.ffn)
                    V.scalar_tensor_tensor(gc[:, t, :], g[:, t, :], g_minus_mean[:, t:t + 1], ln_w_all[:, :],
                                           ALU.add, ALU.mult).then_inc(dve_gc[t], 1)

                def gT_low(t):
                    low(gT_lo[:, t, :, :].rearrange("p n f -> p (n f)"), gT_ps[t][:, :],
                        gT_hi[:, t, :, :].rearrange("p n f -> p (n f)"), s.ffn, act_gT[t],
                        pe_ffn[t], s.ffn, dve_gT[t])

                def finish(t):
                    b, p = s.ffn, s.parity
                    reached(dve, pe_ffn[t], b + 1)
                    reached(dve, pool_g_rstd, b + 1)
                    if t == 0:
                        if s.looped:
                            dve.wait_ge(stored[p], 16 * (s.pair - 1))
                        elif s.pair > 1:
                            dve.wait_ge(stored[p], 16 * (s.pair - 1))
                    V.scalar_tensor_tensor(result[p][:, t, :], ffn_ps[t], g_rstd[:, t:t + 1], h2s[p][:, t, :],
                                           ALU.mult, ALU.add).then_inc(dve_result[t], 1)

                if s.attn is not None:
                    b = s.attn
                    reached(dve, act_k01, b + 1)
                    reached(dve, pe_kv, b)
                    V.tensor_scalar(v[:, 0:2, :, 0:P].rearrange("p t g n -> p (t g) n"),
                                    kv01_ps[:, :, DIM:2 * DIM].rearrange("p t (g n) -> p t g n", g=GROUPS),
                                    1.0 / WEIGHT_SCALE, None, ALU.mult).then_inc(dve_v01, 1)
                    reached(dve, act_k2, b + 1)
                    V.tensor_scalar(v[:, 2, :, 0:P], kv2_ps[:, DIM:2 * DIM].rearrange("p (g n) -> p g n", g=GROUPS),
                                    1.0 / WEIGHT_SCALE, None, ALU.mult).then_inc(dve_v2, 1)
                if s.mlp is not None:
                    low(xT_lo[:, :, :], xT_ps, xT_hi[:, :, :], s.mlp, act_xT, pe_hid23, s.mlp, dve_xT)
                if s.attn is not None:
                    b = s.attn
                    reached(dve, act_q, b + 1)
                    reached(dve, pe_read, b)
                    V.tensor_scalar(q_hi[:, :, :], q[:, :, :], Q_SCALE, None, ALU.mult).then_inc(dve_q_hi, 1)
                    reached(dve, dve_q_hi, b + 1)
                    V.scalar_tensor_tensor(q_lo[:, :, :], q[:, :, :], Q_SCALE, q_hi[:, :, :], ALU.mult,
                                           ALU.subtract).then_inc(dve_q, 1)
                if s.ffn is not None:
                    low(hT_lo[:, :, :], hT_ps, hT_hi[:, :, :], s.ffn, act_hT, pe_g[2], s.ffn, dve_hT)
                if s.mlp is not None:
                    b = s.mlp
                    for at, ready, hi_done, done in ((0, act_hid01, dve_hid01_hi, dve_hid01),
                                                     (2, act_hid23, dve_hid23_hi, dve_hid23)):
                        reached(dve, ready, b + 1)
                        reached(dve, pe_mlp, b)
                        V.tensor_scalar(hid_hi[:, at:at + 2, :], hid[:, at:at + 2, :], GELU_SCALE, None,
                                        ALU.mult).then_inc(hi_done, 1)
                        reached(dve, hi_done, b + 1)
                        V.scalar_tensor_tensor(hid_lo[:, at:at + 2, :], hid[:, at:at + 2, :], GELU_SCALE,
                                               hid_hi[:, at:at + 2, :], ALU.mult, ALU.subtract).then_inc(done, 1)
                if s.attn is not None:
                    b = s.attn
                    reached(dve, pe_kv, b + 1)
                    reached(dve, dve_kv, b)
                    for n in range(GROUPS):
                        V.scalar_tensor_tensor(kv[:, n, 0:P], kv_ps[:, n, 0:P], KV_SCALE,
                                               block_mask[:, :, :].rearrange("p a b -> p (a b)"),
                                               ALU.mult, ALU.mult)
                        last = V.tensor_scalar(kv[:, n, P:P + GROUP_HEADS], head_mask[:, :],
                                               kv_ps[:, n, P:P + 1], KV_SCALE, ALU.mult, ALU.mult)
                    last.then_inc(dve_kv_masked, 1)
                    reached(dve, dve_kv_masked, b + 1)
                    V.tensor_copy(kv_hi[:, :, :], kv[:, :, :]).then_inc(dve_kv_hi, 1)
                    reached(dve, dve_kv_hi, b + 1)
                    V.tensor_tensor(kv_lo[:, :, :], kv[:, :, :], kv_hi[:, :, :], ALU.subtract).then_inc(dve_kv, 1)
                if s.ffn is not None:
                    centre(0)
                    centre(1)
                if s.mlp is not None:
                    b = s.mlp
                    reached(dve, pe_mlp, b + 1)
                    reached(dve, pool_h2s, b)
                    V.scalar_tensor_tensor(h2[:, :, :], mlp_ps, 1.0 / MLP_SCALE, hx[:, :, :], ALU.mult,
                                           ALU.add).then_inc(dve_h2, 1)
                    reached(dve, dve_h2, b + 1)
                    for t in range(TILES):
                        last = V.bn_stats(stats2[:, t, :], h2[:, t, :])
                    last.then_inc(dve_stats2, 1)
                    reached(dve, dve_stats2, b + 1)
                    V.memset(spacer[:, :], 0.0)
                    for t in range(TILES):
                        last = V.bn_aggr(mv2[:, t, :], stats2[:, t, :])
                    last.then_inc(dve_mv2, 1)
                if s.ffn is not None:
                    gT_low(0)
                if s.attn is not None:
                    b = s.attn
                    reached(dve, pe_read, b + 1)
                    V.tensor_scalar(den[:, :, :, :], read_ps[:, :, :, P:ND], DEN_EPS, 1.0 / OUT_SCALE,
                                    ALU.add, ALU.mult).then_inc(dve_den, 1)
                    reached(dve, dve_den, b + 1)
                    V.reciprocal(z[:, :, :, :], den[:, :, :, :]).then_inc(dve_z, 1)
                    reached(dve, dve_z, b + 1)
                    reached(dve, pe_readT, b)
                    for n in range(GROUPS):
                        last = V.tensor_tensor(
                            read[:, :, n * P:(n + 1) * P].rearrange("p t (a c) -> p t a c", c=HEAD),
                            read_ps[:, n, :, 0:P].rearrange("p t (a c) -> p t a c", c=HEAD),
                            z[:, n, :, :][:, :, :, None].to_broadcast([P, TILES, GROUP_HEADS, HEAD]), ALU.mult)
                    last.then_inc(dve_read, 1)
                if s.mlp is not None:
                    b = s.mlp
                    reached(dve, pool_rstd2, b + 1)
                    reached(dve, pe_hT, b)
                    for t in range(TILES):
                        last = V.tensor_scalar(hn[:, t, :], h2[:, t, :], mv2[:, t, 0:1], rstd2[:, t:t + 1],
                                               ALU.subtract, ALU.mult)
                    last.then_inc(dve_hn, 1)
                if s.ffn is not None:
                    centre(2)
                if s.embed is not None:
                    b, p = s.embed, 1 - s.parity
                    reached(dve, act_h, b + 1)
                    dve.wait_ge(text_loaded[p], 16 * (s.pair + 1 if s.parity == 0 else s.pair + 2))
                    for t in range(TILES):
                        last = V.bn_stats(stats1[:, t, :], h[p][:, t, :])
                    last.then_inc(dve_stats1, 1)
                    reached(dve, dve_stats1, b + 1)
                    reached(dve, pool_ratio_a, b)
                    V.memset(spacer[:, :], 0.0)
                    for t in range(TILES):
                        last = V.bn_aggr(mv1[:, t, :], stats1[:, t, :])
                    last.then_inc(dve_mv1, 1)
                if s.attn is not None:
                    low(readT_lo[:, :, :], readT_ps, readT_hi[:, :, :], s.attn, act_readT, pe_attn, s.attn, dve_readT)
                if s.ffn is not None:
                    gT_low(1)
                if s.embed is not None:
                    b, p = s.embed, 1 - s.parity
                    reached(dve, pool_rstd1, b + 1)
                    reached(dve, pe_aT, b - 1)
                    for t in range(TILES):
                        last = V.tensor_scalar(a[p][:, t, :], h[p][:, t, :], mv1[:, t, 0:1], rstd1[:, t:t + 1],
                                               ALU.subtract, ALU.mult)
                    last.then_inc(dve_a, 1)
                if s.ffn is not None:
                    gT_low(2)
                    finish(0)
                    finish(1)
                if s.embed is not None:
                    low(aT_lo[:, :, :], aT_ps, aT_hi[:, :, :], s.embed, act_aT, pe_q, s.embed, dve_aT)
                if s.attn is not None:
                    b, p = s.attn, s.parity
                    reached(dve, pe_attn, b + 1)
                    reached(dve, pool_ratio, b + 1)
                    reached(dve, act_squares1, b)
                    for t in range(TILES):
                        last = V.scalar_tensor_tensor(x1[:, t, :], a[p][:, t, :], ratio[p][:, t:t + 1],
                                                      attn_ps[:, t, :], ALU.mult, ALU.add)
                    last.then_inc(dve_x1, 1)
                    reached(dve, dve_x1, b + 1)
                    V.scalar_tensor_tensor(hx[:, :, :], x1[:, :, :], 1.0 / ATTN_SCALE, h[p][:, :, :], ALU.mult,
                                           ALU.add).then_inc(dve_hx, 1)
                if s.ffn is not None:
                    finish(2)
                if s.attn is not None:
                    b = s.attn
                    reached(dve, pool_rms, b + 1)
                    reached(dve, pe_xT, b)
                    for t in range(TILES):
                        last = V.tensor_scalar(xn[:, t, :], x1[:, t, :], rms[:, t:t + 1], DIM ** 0.5, ALU.mult, ALU.mult)
                    last.then_inc(dve_xn, 1)

            run(dve, body)

        @block.scalar
        def _(act):
            S = nc.scalar
            act.wait_ge(weights_ready, 1)

            def body(s):
                def high(dst, ps, b, ready, war, war_count, done):
                    reached(act, ready, b + 1)
                    reached(act, war, war_count)
                    S.activation(dst, ps, ACT.Copy).then_inc(done, 1)

                def gelu(t):
                    b = s.ffn
                    reached(act, pe_g[t], b + 1)
                    reached(act, dve_gc[t], b)
                    reached(act, act_g_squares[t], b)
                    S.activation(g[:, t, :], g_ps[t][:, :], ACT.Gelu, accum_out=g_sum[:, t:t + 1]).then_inc(act_g[t], 1)

                def spread(t):
                    b = s.ffn
                    reached(act, pool_g_mean[t], b + 1)
                    reached(act, pool_g_var, b)
                    S.activation(unread_g[:, t, :], g[:, t, :], ACT.Square, bias=g_minus_mean[:, t:t + 1],
                                 accum_out=g_squares[:, t:t + 1]).then_inc(act_g_squares[t], 1)

                def gT_high(t):
                    high(gT_hi[:, t, :, :].rearrange("p n f -> p (n f)"), gT_ps[t][:, :], s.ffn, pe_gT[t],
                         pe_ffn[t], s.ffn, act_gT[t])

                if s.attn is not None:
                    b = s.attn
                    reached(act, pe_kv01, b + 1)
                    reached(act, act_k, b)
                    S.activation(k_square[:, 0:2, :], kv01_ps[:, :, 0:DIM], ACT.Square,
                                 scale=1.0 / WEIGHT_SCALE).then_inc(act_k01, 1)
                    reached(act, pe_kv2, b + 1)
                    S.activation(k_square[:, 2, :], kv2_ps[:, 0:DIM], ACT.Square,
                                 scale=1.0 / WEIGHT_SCALE).then_inc(act_k2, 1)
                if s.mlp is not None:
                    high(xT_hi[:, :, :], xT_ps, s.mlp, pe_xT, pe_hid23, s.mlp, act_xT)
                if s.attn is not None:
                    b = s.attn
                    reached(act, act_k2, b + 1)
                    reached(act, pe_kv, b)
                    S.activation(k[:, :, :], k_square[:, :, :], ACT.Exp, scale=-0.5).then_inc(act_k, 1)
                    reached(act, pe_q, b + 1)
                    S.activation(q_square[:, :, :], q_ps, ACT.Square, scale=1.0 / WEIGHT_SCALE
                                 ).then_inc(act_q_square, 1)
                    reached(act, act_q_square, b + 1)
                    reached(act, dve_q, b)
                    S.activation(q[:, :, :], q_square[:, :, :], ACT.Exp, scale=-0.5).then_inc(act_q, 1)
                if s.ffn is not None:
                    high(hT_hi[:, :, :], hT_ps, s.ffn, pe_hT, pe_g[2], s.ffn, act_hT)
                if s.mlp is not None:
                    b = s.mlp
                    for at, ps, ready, split_done, done in ((0, hid01_ps, pe_hid01, dve_hid01, act_hid01),
                                                            (2, hid23_ps, pe_hid23, dve_hid23, act_hid23)):
                        reached(act, ready, b + 1)
                        reached(act, split_done, b)
                        for n in range(2):
                            last = S.activation(hid[:, at + n, :], ps[:, n, :], ACT.Gelu,
                                                bias=conv1_bias[:, at + n:at + n + 1], scale=1.0 / WEIGHT_SCALE)
                        last.then_inc(done, 1)
                if s.ffn is not None:
                    gelu(0)
                    gelu(1)
                    spread(0)
                    gT_high(0)
                    gelu(2)
                    spread(1)
                if s.embed is not None:
                    b, p = s.embed, 1 - s.parity
                    reached(act, pe_tok, b + 1)
                    reached(act, dve_hx, b - 1)
                    S.activation(h[p][:, 0:IMAGE_TILES, :], tok_ps, ACT.Copy).then_inc(act_h, 1)
                if s.attn is not None:
                    high(readT_hi[:, :, :], readT_ps, s.attn, pe_readT, pe_attn, s.attn, act_readT)
                if s.ffn is not None:
                    gT_high(1)
                    spread(2)
                    gT_high(2)
                if s.embed is not None:
                    high(aT_hi[:, :, :], aT_ps, s.embed, pe_aT, pe_q, s.embed, act_aT)
                if s.attn is not None:
                    b = s.attn
                    reached(act, dve_x1, b + 1)
                    reached(act, pool_rms, b)
                    for t in range(TILES):
                        last = S.activation(unread1[:, t, :], x1[:, t, :], ACT.Square, accum_out=squares1[:, t:t + 1])
                    last.then_inc(act_squares1, 1)

            run(act, body)

        @block.tensor
        def _(pe):
            T = nc.tensor
            pe.wait_ge(setup_done, 1)
            for which, steps in enumerate(SETUP_STEPS):
                pe.wait_ge(setup_chain, steps)
                T.matmul(A[:, which:which + 1], ones_f[:, :], absolute_sum[:, which:which + 1],
                         start=True, stop=True).then_inc(sums_on_pe, 1)
            pe.wait_ge(setup_chain, SETUP_SHIFT)
            for n in range(WIDE_TILES):
                last = T.matmul(B[:, 0:DIM], ln_b_wide[:, n, :], ffn_q32[:, n, :], start=n == 0,
                                stop=n == WIDE_TILES - 1)
            last.then_inc(sums_on_pe, 1)
            pe.wait_ge(weights_ready, 1)

            def three(dst, moving, pairs, bias=None):
                products = []
                for (s_hi, s_lo), (m_hi, m_lo) in pairs:
                    products += [(s_hi, m_hi), (s_hi, m_lo), (s_lo, m_hi)]
                if bias is not None:
                    products.append((ones_bf[:, :], bias))
                for n, (stationary, mov) in enumerate(products):
                    last = T.matmul(dst, stationary, mov, start=n == 0, stop=n == len(products) - 1)
                return last

            def tile(x, c, t):
                return x[:, c, t * P:(t + 1) * P]

            def turn(ps, src):
                for c in range(GROUPS):
                    for t in range(TILES):
                        last = T.transpose(ps[:, c, t * P:(t + 1) * P], src[:, t, c * P:(c + 1) * P], identity[:, :])
                return last

            def body(s):
                def keys_values(t, ps):
                    return three(ps, None, [((tile(aT_hi, c, t), tile(aT_lo, c, t)),
                                             (qkv_hi[:, c, DIM:], qkv_lo[:, c, DIM:])) for c in range(GROUPS)])

                def wide(t):
                    for half in range(2):
                        n = 0
                        for c in range(GROUPS):
                            for part in (hT_hi, hT_lo):
                                last = T.matmul(g_ps[t][:, half * BANK:(half + 1) * BANK], tile(part, c, t),
                                                fc_q[:, c, half * BANK:(half + 1) * BANK], start=n == 0, stop=n == 3)
                                n += 1
                    last.then_inc(pe_g[t], 1)

                def turn_wide(t):
                    reached(pe, dve_gc[t], s.ffn + 1)
                    for n in range(WIDE_TILES):
                        last = T.transpose(gT_ps[t][:, n * P:(n + 1) * P], gc[:, t, n * P:(n + 1) * P], identity[:, :])
                    last.then_inc(pe_gT[t], 1)

                def narrow(t):
                    reached(pe, dve_gT[t], s.ffn + 1)
                    n = 0
                    for w in range(WIDE_TILES):
                        for part in (gT_hi, gT_lo):
                            last = T.matmul(ffn_ps[t], part[:, t, w, :], ffn_q[:, w, :], start=n == 0,
                                            stop=n == 2 * WIDE_TILES - 1)
                            n += 1
                    last.then_inc(pe_ffn[t], 1)

                if s.attn is not None:
                    b = s.attn
                    reached(pe, dve_aT, b + 1)
                    reached(pe, dve_x1, b)
                    for t in range(2):
                        last = keys_values(t, kv01_ps[:, t, :])
                    last.then_inc(pe_kv01, 1)
                    reached(pe, dve_readT, b)
                    keys_values(2, kv2_ps).then_inc(pe_kv2, 1)
                if s.mlp is not None:
                    b = s.mlp
                    reached(pe, dve_xn, b + 1)
                    if s.attn is not None:
                        reached(pe, dve_aT, s.attn + 1)
                    turn(xT_ps, xn).then_inc(pe_xT, 1)
                if s.attn is not None:
                    b = s.attn
                    reached(pe, act_h, b + 1)
                    if s.ffn is not None:
                        for t in range(2):
                            reached(pe, dve_result[t], s.ffn)
                    for c in range(GROUPS):
                        w = slice(c * P, (c + 1) * P)
                        last = three(q_ps[:, c, :], None, [((qkv_hi[:, d, w], qkv_lo[:, d, w]),
                                                            (aT_hi[:, d, :], aT_lo[:, d, :])) for d in range(GROUPS)])
                    last.then_inc(pe_q, 1)
                if s.ffn is not None:
                    b = s.ffn
                    reached(pe, dve_hn, b + 1)
                    if s.attn is not None:
                        reached(pe, act_k01, s.attn + 1)
                        reached(pe, dve_v01, s.attn + 1)
                    else:
                        reached(pe, dve_x1, BATCHES)
                    turn(hT_ps, hn).then_inc(pe_hT, 1)
                if s.mlp is not None:
                    b = s.mlp
                    reached(pe, dve_xT, b + 1)
                    if s.attn is not None:
                        reached(pe, act_q_square, s.attn + 1)
                    elif s.ffn is not None:
                        for t in range(2):
                            reached(pe, dve_result[t], s.ffn)
                    for n, (ps, done) in enumerate(((hid01_ps, pe_hid01), (hid23_ps, pe_hid23))):
                        for m in range(2):
                            w = slice((2 * n + m) * P, (2 * n + m + 1) * P)
                            last = three(ps[:, m, :], None, [((conv1_hi[:, c, w], conv1_lo[:, c, w]),
                                                              (xT_hi[:, c, :], xT_lo[:, c, :])) for c in range(GROUPS)])
                        last.then_inc(done, 1)
                if s.ffn is not None:
                    b = s.ffn
                    reached(pe, dve_hT, b + 1)
                    if s.attn is not None:
                        reached(pe, act_k2, s.attn + 1)
                        reached(pe, dve_v2, s.attn + 1)
                    reached(pe, dve_result[2], b)
                    wide(0)
                if s.attn is not None:
                    b = s.attn
                    reached(pe, act_k, b + 1)
                    reached(pe, dve_v2, b + 1)
                    reached(pe, dve_v01, b + 1)
                    if s.ffn is not None:
                        reached(pe, dve_hT, s.ffn + 1)
                    for n in range(GROUPS):
                        for t in range(TILES):
                            last = T.matmul(kv_ps[:, n, :], k[:, t, n * P:(n + 1) * P], v[:, t, n, :],
                                            start=t == 0, stop=t == TILES - 1)
                    last.then_inc(pe_kv, 1)
                if s.ffn is not None:
                    if s.mlp is not None:
                        reached(pe, act_hid01, s.mlp + 1)
                    wide(1)
                if s.mlp is not None:
                    b = s.mlp
                    reached(pe, dve_hid01, b + 1)
                    reached(pe, dve_hid23, b + 1)
                    for t in range(TILES):
                        last = three(mlp_ps[:, t, :], None,
                                     [((tile(hid_hi, n, t), tile(hid_lo, n, t)), (conv2_hi[:, n, :], conv2_lo[:, n, :]))
                                      for n in range(HIDDEN_TILES)], bias=mlp_bias[:, :])
                    last.then_inc(pe_mlp, 1)
                if s.ffn is not None:
                    if s.attn is not None:
                        reached(pe, dve_kv, s.attn + 1)
                    turn_wide(0)
                if s.attn is not None:
                    b = s.attn
                    reached(pe, dve_kv, b + 1)
                    reached(pe, dve_q, b + 1)
                    if s.ffn is not None:
                        reached(pe, act_g[0], s.ffn + 1)
                    for t in range(TILES):
                        for n in range(GROUPS):
                            last = three(read_ps[:, n, t, :], None,
                                         [((tile(q_hi, n, t), tile(q_lo, n, t)), (kv_hi[:, n, :], kv_lo[:, n, :]))])
                    last.then_inc(pe_read, 1)
                if s.ffn is not None:
                    reached(pe, act_g[1], s.ffn + 1)
                    wide(2)
                if s.embed is not None:
                    b, p = s.embed, 1 - s.parity
                    pe.wait_ge(pixels_loaded[p], 32 * (s.pair + 1 if s.parity == 0 else s.pair + 2))
                    if s.mlp is not None:
                        reached(pe, dve_h2, s.mlp + 1)
                    elif s.attn is not None:
                        reached(pe, act_q_square, s.attn + 1)
                    for t in range(IMAGE_TILES):
                        for n in range(FULL + 1):
                            rows_n = P if n < FULL else REST + 1
                            last = T.matmul(tok_ps[:, t, :], pixels[p][0:rows_n, n, t * P:(t + 1) * P],
                                            tok_wT[0:rows_n, n, :], start=n == 0, stop=n == FULL)
                    last.then_inc(pe_tok, 1)
                if s.attn is not None:
                    b = s.attn
                    reached(pe, dve_read, b + 1)
                    turn(readT_ps, read).then_inc(pe_readT, 1)
                if s.ffn is not None:
                    reached(pe, dve_gT[0], s.ffn + 1)
                    turn_wide(1)
                    reached(pe, act_g[2], s.ffn + 1)
                    turn_wide(2)
                    if s.mlp is not None:
                        reached(pe, dve_h2, s.mlp + 1)
                    narrow(0)
                    if s.embed is not None:
                        reached(pe, act_h, s.embed + 1)
                    narrow(1)
                if s.embed is not None:
                    b, p = s.embed, 1 - s.parity
                    reached(pe, dve_a, b + 1)
                    if s.ffn is not None:
                        reached(pe, dve_gT[2], s.ffn + 1)
                    elif s.mlp is not None:
                        reached(pe, act_hid01, s.mlp + 1)
                    turn(aT_ps, a[p]).then_inc(pe_aT, 1)
                if s.attn is not None:
                    b = s.attn
                    reached(pe, dve_readT, b + 1)
                    if s.ffn is not None:
                        reached(pe, dve_gT[1], s.ffn + 1)
                    for t in range(TILES):
                        last = three(attn_ps[:, t, :], None,
                                     [((tile(readT_hi, c, t), tile(readT_lo, c, t)), (proj_hi[:, c, :], proj_lo[:, c, :]))
                                      for c in range(GROUPS)], bias=attn_bias[:, :])
                    last.then_inc(pe_attn, 1)
                if s.ffn is not None:
                    if s.attn is not None:
                        reached(pe, dve_readT, s.attn + 1)
                    narrow(2)

            run(pe, body)


def _setup_counts():
    split = 2
    bias = 1 + 3 + 2 * (2 + 1)
    first = GROUPS + split + 2 * bias + GROUPS + split + GROUPS + split + HIDDEN_TILES + split
    ternary = 2 + 3 + 3
    return (first + 2, first + ternary + 2), first + 2 * ternary + 2


SETUP_STEPS, SETUP_SHIFT = _setup_counts()

_INS = ["image", "text", "tok_w", "tok_b", "scale1", "scale2", "gamma", "qkv_w", "proj_w", "proj_b",
        "conv1_w", "conv1_b", "conv2_w", "conv2_b", "fc_w", "ln_w", "ln_b", "ffn_w"]


def kernel(x, txt, L0_tok_W, L0_tok_b, L0_attn_scale1, L0_attn_scale2, L0_attn_gamma, L0_attn_qkv_w,
           L0_attn_proj_w, L0_attn_proj_b, L0_attn_conv1_w, L0_attn_conv1_b, L0_attn_conv2_w,
           L0_attn_conv2_b, L0_ffn_W_fc, L0_ffn_ln_w, L0_ffn_ln_b, L0_ffn_W_proj):
    import concourse.bacc as _bacc
    from concourse.bass_utils import run_bass_kernel_spmd as _run

    image = np.asarray(x).reshape(BATCHES, CHANNELS, GRID, PATCH, GRID, PATCH).transpose(0, 1, 3, 5, 2, 4)
    image = image.reshape(BATCHES, PIXELS, PATCHES)
    given = [image, txt, np.asarray(L0_tok_W).T, L0_tok_b, L0_attn_scale1, L0_attn_scale2, L0_attn_gamma,
             np.asarray(L0_attn_qkv_w).T, np.asarray(L0_attn_proj_w).T, L0_attn_proj_b,
             np.asarray(L0_attn_conv1_w).T, L0_attn_conv1_b, np.asarray(L0_attn_conv2_w).T, L0_attn_conv2_b,
             np.asarray(L0_ffn_W_fc).T, L0_ffn_ln_w, L0_ffn_ln_b, np.asarray(L0_ffn_W_proj).T]
    nc = _bacc.Bacc("TRN2", target_bir_lowering=False, num_devices=1)
    arrays, args = {}, []
    for name, array in zip(_INS, given):
        array = np.ascontiguousarray(array)
        arrays[f"in_{name}"] = array
        args.append(nc.dram_tensor(f"in_{name}", array.shape, mybir.dt.from_np(array.dtype),
                                   kind="ExternalInput").ap())
    out = nc.dram_tensor("out", (BATCHES, TOKENS, DIM), mybir.dt.float32, kind="ExternalOutput").ap()
    build(nc, *args, out)
    r = _run(nc, [arrays], core_ids=[0])
    return r.results[0]["out"]
```

```python
import numpy as np
from contextlib import ExitStack

import concourse.bass as bass
from concourse import mybir

P = 128
BATCHES = 32
GRID, PATCH, CHANNELS = 16, 14, 3
PATCHES = GRID * GRID
PIXELS = CHANNELS * PATCH * PATCH
TEXT = 128
TOKENS = PATCHES + TEXT
TILES = TOKENS // P
IMAGE_TILES = PATCHES // P
DIM = 256
GROUPS = DIM // P
HEADS, HEAD = 16, 16
GROUP_HEADS = P // HEAD
HIDDEN = 512
HIDDEN_TILES = HIDDEN // P
WIDE = 1024
WIDE_TILES = WIDE // P
PAIRS = WIDE_TILES // 2
FULL = PIXELS // P
REST = PIXELS - FULL * P
LN_EPS = 1e-5
RMS_EPS = 1e-6

WEIGHT_SCALE = 64.0
KV_SCALE = 1.0 / 64
Q_SCALE = 16384.0
OUT_SCALE = 8.0
GELU_SCALE = 16.0
ATTN_SCALE = OUT_SCALE * WEIGHT_SCALE
MLP_SCALE = GELU_SCALE * WEIGHT_SCALE
SQUARE_SCALE = 1.0 / 16
RMS_FACTOR = (DIM ** 0.5 + RMS_EPS) / DIM ** 0.5
DEN_EPS = 1e-6 * Q_SCALE * KV_SCALE

FIRST_LOOPED, LAST_LOOPED = 6, 29


def build(nc, image, text, tok_w, tok_b, columns, rows, qkv_w, proj_w, conv1_w, conv2_w, fc_w,
          ffn_w, out):
    fp32, fp16, bf16 = mybir.dt.float32, mybir.dt.float16, mybir.dt.bfloat16
    ALU, ACT, AX = mybir.AluOpType, mybir.ActivationFunctionType, mybir.AxisListType

    out_v = out.rearrange("b (t p) e -> b p t e", p=P)

    ctx = ExitStack()
    with ctx:
        def sb(name, shape, dt=fp32):
            return ctx.enter_context(nc.sbuf_tensor(name, shape, dt))

        def sem(name):
            return ctx.enter_context(nc.semaphore(name))

        tok_hi, tok_lo = (sb(f"tok_{s}", [P, FULL + 1, DIM], fp16) for s in ("hi", "lo"))
        qkv_hi, qkv_lo = (sb(f"qkv_{s}", [P, GROUPS, 3 * DIM], fp16) for s in ("hi", "lo"))
        proj_hi, proj_lo = (sb(f"proj_{s}", [P, GROUPS, DIM], fp16) for s in ("hi", "lo"))
        conv1_hi, conv1_lo = (sb(f"conv1_{s}", [P, GROUPS, HIDDEN], fp16) for s in ("hi", "lo"))
        conv2_hi, conv2_lo = (sb(f"conv2_{s}", [P, HIDDEN_TILES, DIM], fp16) for s in ("hi", "lo"))
        fc_q = sb("fc_q", [P, GROUPS, WIDE], fp16)
        ffn_q = sb("ffn_q", [P, WIDE_TILES, DIM], fp16)
        attn_bias = sb("attn_bias", [P, DIM], bf16)
        ones_bf = sb("ones_bf", [P, P], bf16)
        mlp_bias = sb("mlp_bias", [P, DIM])
        ln_shift = sb("ln_shift", [P, DIM])
        identity = sb("identity", [P, P])
        head_mask = sb("head_mask", [P, GROUP_HEADS])
        block_mask = sb("block_mask", [P, GROUP_HEADS, HEAD])
        ln_weight_sum = sb("ln_weight_sum", [P, DIM])
        minus_half, eps, attn_scale = (sb(s, [P, 8]) for s in ("minus_half", "eps", "attn_scale"))
        spacer = sb("spacer", [P, 1])
        cols_all = sb("cols_all", [P, columns.shape[1]])
        scale1_cols, scale2_cols = cols_all[:, 0:GROUPS], cols_all[:, GROUPS:2 * GROUPS]
        conv1_bias = cols_all[:, 2 * GROUPS:2 * GROUPS + HIDDEN_TILES]
        ln_b_cols, ln_w_cols = (cols_all[:, 2 * GROUPS + HIDDEN_TILES + n * WIDE_TILES:][:, 0:WIDE_TILES]
                                for n in range(2))
        rows_all = sb("rows_all", [P, 3 * DIM])
        gamma_all, proj_b_all, conv2_b_all = (rows_all[:, n * DIM:(n + 1) * DIM] for n in range(3))

        tok_raw = sb("tok_raw", [P, FULL + 1, DIM])
        proj_raw = sb("proj_raw", [P, GROUPS, DIM])
        bias_rest = sb("bias_rest", [P, DIM])
        bias_part = sb("bias_part", [P, DIM], bf16)
        absolute_sum = sb("absolute_sum", [P, 2])
        ones_f = sb("ones_f", [P, P])
        ones_16 = sb("ones_16", [P, 2], fp16)
        threshold = sb("threshold", [P, 2, 3])

        pixels = [sb(f"pixels{p}", [P, FULL + 1, PATCHES]) for p in range(2)]
        pixels_hi, pixels_lo = (sb(f"pixels_{s}", [P, FULL + 1, PATCHES], fp16) for s in ("hi", "lo"))
        h = [sb(f"h{p}", [P, TILES, DIM]) for p in range(2)]
        a = [sb(f"a{p}", [P, TILES, DIM]) for p in range(2)]
        ratio = [sb(f"ratio{p}", [P, TILES]) for p in range(2)]
        stats1 = sb("stats1", [P, TILES, 6])
        mv1 = sb("mv1", [P, TILES, 2])
        var1 = sb("var1", [P, TILES])
        rstd1 = sb("rstd1", [P, 2 * TILES])
        ratio_part = sb("ratio_part", [P, 2 * TILES])
        aT_hi, aT_lo = (sb(f"aT_{s}", [P, GROUPS, TOKENS], fp16) for s in ("hi", "lo"))
        k_square = sb("k_square", [P, TILES, DIM])
        k = sb("k", [P, TILES, DIM])
        v = sb("v", [P, TILES, GROUPS, P + 1])
        q_square = sb("q_square", [P, GROUPS, TOKENS])
        q = sb("q", [P, GROUPS, TOKENS])
        q_hi, q_lo = (sb(f"q_{s}", [P, GROUPS, TOKENS], fp16) for s in ("hi", "lo"))
        kv = sb("kv", [P, GROUPS, P + GROUP_HEADS])
        kv_hi, kv_lo = (sb(f"kv_{s}", [P, GROUPS, P + GROUP_HEADS], fp16) for s in ("hi", "lo"))
        den = sb("den", [P, GROUPS, TILES, GROUP_HEADS])
        z = sb("z", [P, GROUPS, TILES, GROUP_HEADS])
        read = sb("read", [P, TILES, DIM])
        readT_hi, readT_lo = (sb(f"readT_{s}", [P, GROUPS, TOKENS], fp16) for s in ("hi", "lo"))
        x1 = sb("x1", [P, TILES, DIM])
        unread_exp = sb("unread_exp", [P, 1])
        unread1 = sb("unread1", [P, TILES, DIM], bf16)
        squares1 = sb("squares1", [P, TILES])
        rms = sb("rms", [P, TILES])
        xn = sb("xn", [P, TILES, DIM])
        hx = sb("hx", [P, TILES, DIM])
        hxb = sb("hxb", [P, TILES, DIM])
        xT_hi, xT_lo = (sb(f"xT_{s}", [P, GROUPS, TOKENS], fp16) for s in ("hi", "lo"))
        hid = sb("hid", [P, HIDDEN_TILES, TOKENS])
        hid_hi, hid_lo = (sb(f"hid_{s}", [P, HIDDEN_TILES, TOKENS], fp16) for s in ("hi", "lo"))
        h2 = sb("h2", [P, TILES, DIM])
        h2s = [sb(f"h2s{p}", [P, TILES, DIM]) for p in range(2)]
        stats2 = sb("stats2", [P, TILES, 6])
        mv2 = sb("mv2", [P, TILES, 2])
        var2 = sb("var2", [P, TILES])
        rstd2 = sb("rstd2", [P, TILES])
        hn = sb("hn", [P, TILES, DIM])
        hT_hi, hT_lo = (sb(f"hT_{s}", [P, GROUPS, TOKENS], fp16) for s in ("hi", "lo"))
        g = sb("g", [P, WIDE_TILES, TOKENS])
        g_square = sb("g_square", [P, WIDE_TILES, TOKENS])
        g_part, square_part = (sb(f"{s}_part", [P, 2, TOKENS]) for s in ("g", "square"))
        g_total, square_total = (sb(f"{s}_total", [P, TOKENS]) for s in ("g", "square"))
        total_hi, total_lo = (sb(f"total_{s}", [P, 2, TOKENS], fp16) for s in ("hi", "lo"))
        g_mean = sb("g_mean", [P, TILES])
        g_minus_mean = sb("g_minus_mean", [P, TILES])
        g_square_mean = sb("g_square_mean", [P, TILES])
        g_mean_square = sb("g_mean_square", [P, TILES])
        g_var = sb("g_var", [P, TILES])
        g_rstd = sb("g_rstd", [P, TILES])
        gw_hi, gw_lo = (sb(f"gw_{s}", [P, WIDE_TILES, TOKENS], fp16) for s in ("hi", "lo"))
        product = sb("product", [P, TILES, DIM])
        result = [sb(f"result{p}", [P, TILES, DIM]) for p in range(2)]

        g_flat, g_square_flat, gw_hi_flat, gw_lo_flat = (
            x[:, :, :].rearrange("p n f -> p (n f)") for x in (g, g_square, gw_hi, gw_lo))
        RAW = GROUPS * WIDE
        fc_raw, ffn_raw = g_flat[:, 0:RAW], g_square_flat[:, 0:RAW]
        conv1_raw = g_flat[:, RAW:RAW + GROUPS * HIDDEN].rearrange("p (n f) -> p n f", n=GROUPS)
        conv2_raw = g_square_flat[:, RAW:RAW + HIDDEN_TILES * DIM].rearrange("p (n f) -> p n f", n=HIDDEN_TILES)
        ffn_q32 = ffn_raw.rearrange("p (n f) -> p n f", n=WIDE_TILES)
        unread_abs = [x[:, 0:RAW] for x in (gw_hi_flat, gw_lo_flat)]
        below = gw_hi_flat[:, 0:RAW]
        hid_flat = hid[:, :, :].rearrange("p n f -> p (n f)")
        qkv_raw = hid_flat.rearrange("p (n f) -> p n f", n=GROUPS)
        ln_b_wide, ln_w_wide = (x[:, 0:WIDE].rearrange("p (n f) -> p n f", n=WIDE_TILES) for x in (hid_flat, fc_raw))

        BANK = 512
        A, B, C, D = (ctx.enter_context(nc.psum_tensor(f"pair_{s}", [P, 2 * BANK], fp32)) for s in "ABCD")

        def by_token(pair):
            return pair[:, 0:TILES * DIM].rearrange("p (t e) -> p t e", t=TILES)

        def by_channel(pair):
            return pair[:, :].rearrange("p (g n) -> p g n", g=2)[:, :, 0:TOKENS]

        kv01_ps = A[:, :].rearrange("p (t n) -> p t n", t=2)
        kv2_ps = D[:, BANK:2 * BANK]
        xT_ps, q_ps, hT_ps = by_channel(B), by_channel(C), by_channel(A)
        hid01_ps, hid23_ps = by_channel(B), by_channel(C)
        g_ps = [by_channel(pair) for pair in (D, B, A, B)]
        kv_ps = A[:, 0:GROUPS * (P + 1)].rearrange("p (g n) -> p g n", g=GROUPS)
        mlp_ps = by_token(C)
        ND = P + GROUP_HEADS
        read_ps = D[:, :].rearrange("p (g n) -> p g n", g=2)[:, :, 0:TILES * ND].rearrange(
            "p g (t n) -> p g t n", t=TILES)
        tok_ps = C[:, 0:BANK].rearrange("p (t e) -> p t e", t=IMAGE_TILES)
        readT_ps, aT_ps = by_channel(D), by_channel(B)
        attn_ps = by_token(A)
        ffn_ps = [C[:, BANK:BANK + DIM], C[:, 0:DIM], D[:, 0:DIM]]
        sums_ps = B[:, TOKENS:TOKENS + 2 * TILES]

        (tok_loaded, columns_loaded, qkv_loaded, rows_loaded, proj_loaded, conv1_loaded, conv2_loaded,
         fc_loaded, ffn_loaded) = (sem(f"{s}_loaded") for s in (
             "tok", "columns", "qkv", "rows", "proj", "conv1", "conv2", "fc", "ffn"))
        setup_done = sem("setup_done")
        ones_row_set = sem("ones_row_set")
        setup_chain = sem("setup_chain")
        pool_chain = sem("pool_chain")
        tok_ready, qkv_ready, ternary_ready, shift_ready = (
            sem(f"{s}_ready") for s in ("tok", "qkv", "ternary", "shift"))
        absolute_summed = sem("absolute_summed")
        pe_absolute, pe_shift = sem("pe_absolute"), sem("pe_shift")
        pixels_loaded = [sem(f"pixels_loaded{p}") for p in range(2)]
        text_loaded = [sem(f"text_loaded{p}") for p in range(2)]
        stored = [sem(f"stored{p}") for p in range(2)]
        (pe_kv01, pe_kv2, pe_xT, pe_q, pe_hT, pe_hid01, pe_hid23, pe_kv, pe_mlp, pe_read, pe_tok,
         pe_readT, pe_attn) = (sem(f"pe_{s}") for s in (
             "kv01", "kv2", "xT", "q", "hT", "hid01", "hid23", "kv", "mlp", "read", "tok",
             "readT", "attn"))
        pe_aT, act_aT, dve_aT = ([sem(f"{s}_aT{c}") for c in range(GROUPS)] for s in ("pe", "act", "dve"))
        pe_g = [sem(f"pe_g{j}") for j in range(PAIRS)]
        pe_ffn = [sem(f"pe_ffn{t}") for t in range(TILES)]
        pe_sums = sem("pe_sums")
        (act_k01, act_k2, act_k, act_xT, act_q_square, act_q, act_hT, act_hid01, act_hid23, act_h,
         act_readT, act_squares1, act_pixels) = (sem(f"act_{s}") for s in (
             "k01", "k2", "k", "xT", "q_square", "q", "hT", "hid01", "hid23", "h", "readT",
             "squares1", "pixels"))
        act_product = [sem(f"act_product{t}") for t in range(TILES)]
        act_g, act_g_square = ([sem(f"act_{s}{j}") for j in range(PAIRS)] for s in ("g", "g_square"))
        (dve_v01, dve_v2, dve_xT, dve_q_hi, dve_q, dve_hT, dve_hid01_hi, dve_hid01, dve_hid23_hi,
         dve_hid23, dve_kv_masked, dve_kv_hi, dve_kv, dve_h2, dve_stats2, dve_mv2, dve_den, dve_z,
         dve_read, dve_hn, dve_stats1, dve_mv1, dve_readT, dve_a, dve_x1, dve_hx,
         dve_xn, dve_pixels) = (sem(f"dve_{s}") for s in (
             "v01", "v2", "xT", "q_hi", "q", "hT", "hid01_hi", "hid01", "hid23_hi", "hid23",
             "kv_masked", "kv_hi", "kv", "h2", "stats2", "mv2", "den", "z", "read", "hn",
             "stats1", "mv1", "readT", "a", "x1", "hx", "xn", "pixels"))
        dve_gw_hi, dve_gw = ([sem(f"dve_{s}{j}") for j in range(PAIRS)] for s in ("gw_hi", "gw"))
        dve_g_means, dve_centred, dve_result = (sem(f"dve_{s}") for s in ("g_means", "centred", "result"))
        (pool_var2, pool_rstd2, pool_h2s, pool_var1, pool_rstd1, pool_ratio_a, pool_ratio_b,
         pool_ratio, pool_g_mean_square, pool_g_var, pool_g_rstd, pool_rms, pool_rstd1_eps,
         pool_hxb) = (sem(f"pool_{s}") for s in (
             "var2", "rstd2", "h2s", "var1", "rstd1", "ratio_a", "ratio_b", "ratio",
             "g_mean_square", "g_var", "g_rstd", "rms", "rstd1_eps", "hxb"))
        pool_g_part, pool_square_part = ([None] + [sem(f"pool_{s}_part{j}") for j in range(1, PAIRS)]
                                         for s in ("g", "square"))
        pool_g_total, pool_square_total = (sem(f"pool_{s}_total") for s in ("g", "square"))
        act_total_hi, pool_total = ([sem(f"{s}{n}") for n in range(2)] for s in ("act_total_hi", "pool_total"))

        def reached(engine, semaphore, count):
            if not isinstance(count, int) or count > 0:
                engine.wait_ge(semaphore, count)

        class Step:

            def __init__(self, pair, parity):
                self.looped = not isinstance(pair, int)
                step = 2 * pair + parity
                self.parity = parity
                self.embed, self.attn, self.mlp, self.ffn, self.finish, self.fetch = (
                    step + d if self.looped or 0 <= step + d < BATCHES else None
                    for d in (1, 0, -1, -2, -3, 2))
                if self.looped:
                    self.pair = pair
                else:
                    self.pair = step // 2

        def run(engine, body, ahead=None):
            for step in range(-1, FIRST_LOOPED):
                if ahead and step in ahead:
                    ahead[step]()
                body(Step(step // 2, step % 2))
            with engine.Fori(FIRST_LOOPED // 2, (LAST_LOOPED + 1) // 2) as pair:
                for parity in range(2):
                    body(Step(pair, parity))
            for step in range(LAST_LOOPED + 1, BATCHES + 3):
                body(Step(step // 2, step % 2))

        block = ctx.enter_context(nc.Block())

        @block.sync
        def _(sp):
            def fetch_pixels(parity, b):
                sp.dma_start(pixels[parity][:, 0:FULL, :],
                             image[b, 0:FULL * P, :].rearrange("(n p) f -> p n f", p=P)
                             ).then_inc(pixels_loaded[parity], 16)
                sp.dma_start(pixels[parity][0:REST, FULL, :],
                             image[b, FULL * P:PIXELS, :]).then_inc(pixels_loaded[parity], 16)

            sp.dma_start(tok_raw[:, 0:FULL, :], tok_w[0:FULL * P, :].rearrange("(n p) f -> p n f", p=P)
                         ).then_inc(tok_loaded, 16)
            sp.wait_ge(ones_row_set, 1)
            sp.dma_start(tok_raw[0:REST, FULL, :], tok_w[FULL * P:PIXELS, :]).then_inc(tok_loaded, 16)
            sp.dma_start(tok_raw[REST:REST + 1, FULL, :], tok_b[None, :]).then_inc(tok_loaded, 16)
            fetch_pixels(0, 0)
            fetch_pixels(1, 1)
            sp.dma_start(fc_raw.rearrange("p (n f) -> p n f", n=GROUPS),
                         fc_w.rearrange("(n p) f -> p n f", p=P)).then_inc(fc_loaded, 16)
            sp.dma_start(ffn_raw.rearrange("p (n f) -> p n f", n=WIDE_TILES),
                         ffn_w.rearrange("(n p) f -> p n f", p=P)).then_inc(ffn_loaded, 16)

            def body(s):
                if s.embed is not None:
                    p = 1 - s.parity
                    reached(sp, dve_hx, s.embed - 1)
                    sp.dma_start(h[p][:, IMAGE_TILES, :], text[s.embed, :, :]).then_inc(text_loaded[p], 16)
                if s.fetch is not None and not (isinstance(s.fetch, int) and s.fetch < 2):
                    reached(sp, act_pixels, s.fetch - 1)
                    reached(sp, dve_pixels, s.fetch - 1)
                    fetch_pixels(s.parity, s.fetch)
                if s.finish is not None:
                    p = 1 - s.parity
                    reached(sp, dve_result, s.finish + 1)
                    sp.dma_start(out_v[s.finish, :, :, :], result[p][:, :, :]).then_inc(stored[p], 16)

            run(sp, body)
            for p in range(2):
                sp.wait_ge(stored[p], 16 * (BATCHES // 2))

        @block.gpsimd
        def _(pool):
            G = nc.gpsimd
            G.memset(identity[:, :], 0.0)
            G.memset(head_mask[:, :], 1.0)
            G.memset(minus_half[:, :], -0.5)
            G.memset(eps[:, :], LN_EPS)
            G.memset(attn_scale[:, :], ATTN_SCALE)
            G.memset(ones_f[:, :], 1.0)
            G.memset(ones_bf[:, :], 1.0)
            G.memset(ones_16[:, :], 1.0)
            G.memset(attn_bias[:, :], 0.0)
            G.memset(v[:, :, :, P:P + 1], 1.0).then_inc(pool_chain, 1)
            pool.wait_ge(pool_chain, 1)
            G.affine_select(out=identity[:, :], in_=identity[:, :], compare_op=ALU.not_equal, fill=1.0,
                            base=0, pattern=[[-1, P]], channel_multiplier=1)
            G.affine_select(out=head_mask[:, :], in_=head_mask[:, :], compare_op=ALU.is_ge, fill=0.0,
                            base=0, pattern=[[-HEAD, GROUP_HEADS]], channel_multiplier=1).then_inc(pool_chain, 1)
            pool.wait_ge(pool_chain, 2)
            G.affine_select(out=head_mask[:, :], in_=head_mask[:, :], compare_op=ALU.is_ge, fill=0.0,
                            base=HEAD - 1, pattern=[[HEAD, GROUP_HEADS]], channel_multiplier=-1).then_inc(pool_chain, 1)
            pool.wait_ge(pool_chain, 3)
            G.tensor_copy(block_mask[:, :, :], head_mask[:, :, None].to_broadcast([P, GROUP_HEADS, HEAD])
                          ).then_inc(setup_done, 1)

            def power(dst, src, n, done):
                return G.tensor_tensor(dst, src, minus_half[:, 0:n], ALU.pow).then_inc(done, 1)

            def body(s):
                def add_pair(src, part, done, ready, j):
                    b = s.ffn
                    reached(pool, ready[j], b + 1)
                    if j == 1:
                        reached(pool, ready[0], b + 1)
                        first = src[:, 0:2, :]
                    else:
                        reached(pool, done[j - 1], b + 1)
                        first = part[:, :, :]
                    G.tensor_tensor(part[:, :, :], first, src[:, 2 * j:2 * j + 2, :], ALU.add).then_inc(done[j], 1)

                def add_halves(part, total, parts_done, done):
                    b = s.ffn
                    reached(pool, parts_done[PAIRS - 1], b + 1)
                    G.tensor_tensor(total[:, :], part[:, 0, :], part[:, 1, :], ALU.add).then_inc(done, 1)

                def low_total(n):
                    b = s.ffn
                    reached(pool, act_total_hi[n], b + 1)
                    G.tensor_tensor(total_lo[:, n, :], (g_total, square_total)[n][:, :], total_hi[:, n, :],
                                    ALU.subtract).then_inc(pool_total[n], 1)

                def add_g(j):
                    if j == 1:
                        reached(pool, pool_g_total, s.ffn)
                    add_pair(g, g_part, pool_g_part, act_g, j)

                def add_square(j):
                    if j == 1:
                        reached(pool, pool_square_total, s.ffn)
                    add_pair(g_square, square_part, pool_square_part, act_g_square, j)

                if s.finish is not None:
                    b = s.finish
                    reached(pool, dve_g_means, b + 1)
                    G.tensor_tensor(g_mean_square[:, :], g_mean[:, :], g_mean[:, :], ALU.mult).then_inc(pool_g_mean_square, 1)
                    reached(pool, pool_g_mean_square, b + 1)
                    G.tensor_tensor(g_var[:, :], g_square_mean[:, :], g_mean_square[:, :],
                                    ALU.subtract).then_inc(pool_g_var, 1)
                    reached(pool, pool_g_var, b + 1)
                    reached(pool, dve_result, b)
                    power(g_rstd[:, :], g_var[:, :], TILES, pool_g_rstd)
                if s.ffn is not None:
                    add_g(1)
                    add_square(1)
                if s.mlp is not None:
                    b = s.mlp
                    reached(pool, dve_mv2, b + 1)
                    G.tensor_tensor(var2[:, :], mv2[:, :, 1], eps[:, 0:TILES], ALU.add).then_inc(pool_var2, 1)
                    reached(pool, pool_var2, b + 1)
                    reached(pool, dve_hn, b)
                    power(rstd2[:, :], var2[:, :], TILES, pool_rstd2)
                if s.ffn is not None:
                    add_g(2)
                    add_square(2)
                    add_g(3)
                    add_halves(g_part, g_total, pool_g_part, pool_g_total)
                if s.embed is not None:
                    b, p = s.embed, 1 - s.parity
                    reached(pool, dve_mv1, b + 1)
                    reached(pool, dve_a, b)
                    power(rstd1[:, 0:TILES], mv1[:, :, 1], TILES, pool_rstd1)
                    G.tensor_tensor(var1[:, :], mv1[:, :, 1], eps[:, 0:TILES], ALU.add).then_inc(pool_var1, 1)
                    reached(pool, pool_var1, b + 1)
                    power(rstd1[:, TILES:2 * TILES], var1[:, :], TILES, pool_rstd1_eps)
                    reached(pool, pool_rstd1, b + 1)
                    G.tensor_tensor(ratio_part[:, 0:TILES], mv1[:, :, 1], rstd1[:, 0:TILES],
                                    ALU.mult).then_inc(pool_ratio_a, 1)
                    reached(pool, pool_rstd1_eps, b + 1)
                    reached(pool, pool_ratio_a, b + 1)
                    G.tensor_tensor(ratio_part[:, TILES:2 * TILES], ratio_part[:, 0:TILES],
                                    rstd1[:, TILES:2 * TILES], ALU.mult).then_inc(pool_ratio_b, 1)
                    reached(pool, pool_ratio_b, b + 1)
                    reached(pool, dve_x1, b - 1)
                    G.tensor_tensor(ratio[p][:, :], ratio_part[:, TILES:2 * TILES], attn_scale[:, 0:TILES],
                                    ALU.mult).then_inc(pool_ratio, 1)
                if s.ffn is not None:
                    add_square(3)
                if s.attn is not None:
                    b = s.attn
                    reached(pool, act_squares1, b + 1)
                    reached(pool, dve_xn, b)
                    power(rms[:, :], squares1[:, :], TILES, pool_rms)
                if s.ffn is not None:
                    add_halves(square_part, square_total, pool_square_part, pool_square_total)
                    low_total(0)
                    low_total(1)
                if s.mlp is not None:
                    b = s.mlp
                    reached(pool, dve_h2, b + 1)
                    reached(pool, dve_result, b - 1)
                    G.tensor_tensor(h2s[1 - s.parity][:, :, :], h2[:, :, :],
                                    ln_shift[:, None, :].to_broadcast([P, TILES, DIM]), ALU.add).then_inc(pool_h2s, 1)
                if s.attn is not None:
                    b = s.attn
                    reached(pool, dve_hx, b + 1)
                    reached(pool, dve_h2, b)
                    G.tensor_tensor(hxb[:, :, :], hx[:, :, :], mlp_bias[:, None, :].to_broadcast([P, TILES, DIM]),
                                    ALU.add).then_inc(pool_hxb, 1)

            def shift_known():
                pool.wait_ge(shift_ready, 1)

            run(pool, body, {1: shift_known})

        @block.vector
        def _(dve):
            V = nc.vector
            links = [0]

            def link(ins):
                links[0] += 1
                ins.then_inc(setup_chain, 1)
                dve.wait_ge(setup_chain, links[0])

            def split(hi, lo, src):
                link(V.tensor_copy(hi, src))
                link(V.tensor_tensor(lo, src, hi, ALU.subtract))

            V.memset(pixels[0][64:P, FULL, :], 1.0)
            V.memset(pixels[1][64:P, FULL, :], 1.0)
            V.memset(tok_raw[64:P, FULL, :], 1.0).then_inc(ones_row_set, 1)

            def embedding_weights():
                dve.wait_ge(tok_loaded, 16 * 3)
                link(V.tensor_scalar(tok_raw[:, :, :], tok_raw[:, :, :], WEIGHT_SCALE, None, ALU.mult))
                split(tok_hi[:, :, :], tok_lo[:, :, :], tok_raw[:, :, :])
                V.memset(spacer[:, :], 0.0).then_inc(tok_ready, 1)
                split_pixels(0, 0)
                dve.wait_ge(columns_loaded, 16)
                dve.wait_ge(qkv_loaded, 16)
                for i in range(GROUPS):
                    last = V.tensor_scalar(qkv_raw[:, i, :], qkv_raw[:, i, :], scale1_cols[:, i:i + 1],
                                           RMS_FACTOR * WEIGHT_SCALE, ALU.mult, ALU.mult)
                link(last)
                split(qkv_hi[:, :, :], qkv_lo[:, :, :], qkv_raw[:, :, :])
                V.tensor_copy(spacer[:, :], qkv_lo[:, 0, 0:1]).then_inc(qkv_ready, 1)

            def attention_weights():
                dve.wait_ge(setup_done, 1)
                dve.wait_ge(rows_loaded, 16)
                dve.wait_ge(proj_loaded, 16)
                for i in range(GROUPS):
                    last = V.scalar_tensor_tensor(proj_raw[:, i, :], proj_raw[:, i, :], WEIGHT_SCALE,
                                                  gamma_all, ALU.mult, ALU.mult)
                link(last)
                split(proj_hi[:, :, :], proj_lo[:, :, :], proj_raw[:, :, :])
                V.tensor_tensor(mlp_bias[:, :], conv2_b_all, gamma_all, ALU.mult)
                link(V.scalar_tensor_tensor(bias_rest[:, :], proj_b_all, ATTN_SCALE, gamma_all,
                                            ALU.mult, ALU.mult))
                for part in range(3):
                    at = slice(32 * part, 32 * part + 1)
                    link(V.tensor_copy(attn_bias[at, :], bias_rest[at, :]))
                    for row in range(32 * (part + 1), 96, 32):
                        link(V.tensor_copy(bias_part[row:row + 1, :], bias_rest[row:row + 1, :]))
                        link(V.tensor_tensor(bias_rest[row:row + 1, :], bias_rest[row:row + 1, :],
                                             bias_part[row:row + 1, :], ALU.subtract))
                dve.wait_ge(fc_loaded, 16)
                dve.wait_ge(ffn_loaded, 16)
                dve.wait_ge(pe_absolute, 1)
                link(V.tensor_scalar(threshold[:, :, 0], D[:, 0:2], 1.0 / (WIDE * DIM), 1e-6, ALU.mult, ALU.add))
                V.tensor_scalar(threshold[:, :, 1], threshold[:, :, 0], 0.5, None, ALU.mult)
                link(V.tensor_scalar(threshold[:, :, 2], threshold[:, :, 0], -0.5, None, ALU.mult))
                for which, (raw, dst) in enumerate(((fc_raw, fc_q), (ffn_raw, ffn_q))):
                    flat = dst[:, :, :].rearrange("p n f -> p (n f)")
                    V.tensor_scalar(below, raw, threshold[:, which, 2:3], None, ALU.is_lt)
                    link(V.tensor_scalar(flat, raw, threshold[:, which, 1:2], None, ALU.is_gt))
                    link(V.tensor_tensor(flat, flat, below, ALU.subtract))
                V.tensor_copy(ffn_q32, ffn_q[:, :, :])
                V.tensor_copy(ln_w_wide, ln_w_cols[:, :, None].to_broadcast([P, WIDE_TILES, P]))
                V.tensor_copy(ln_b_wide, ln_b_cols[:, :, None].to_broadcast([P, WIDE_TILES, P])
                              ).then_inc(ternary_ready, 1)

            def mlp_weights():
                dve.wait_ge(conv1_loaded, 16)
                dve.wait_ge(conv2_loaded, 16)
                for i in range(GROUPS):
                    last = V.tensor_scalar(conv1_raw[:, i, :], conv1_raw[:, i, :], scale2_cols[:, i:i + 1],
                                           RMS_FACTOR * WEIGHT_SCALE, ALU.mult, ALU.mult)
                link(last)
                split(conv1_hi[:, :, :], conv1_lo[:, :, :], conv1_raw)
                for i in range(HIDDEN_TILES):
                    last = V.scalar_tensor_tensor(conv2_raw[:, i, :], conv2_raw[:, i, :], WEIGHT_SCALE, gamma_all,
                                                  ALU.mult, ALU.mult)
                link(last)
                split(conv2_hi[:, :, :], conv2_lo[:, :, :], conv2_raw)
                dve.wait_ge(pe_shift, 1)
                V.tensor_copy(ln_weight_sum[:, :], D[:, DIM:2 * DIM])
                V.tensor_copy(ln_shift[:, :], D[:, 0:DIM]).then_inc(shift_ready, 1)

            def split_pixels(b, p):
                reached(dve, act_pixels, b + 1)
                reached(dve, pe_tok, b)
                V.tensor_tensor(pixels_lo[:, :, :], pixels[p][:, :, :], pixels_hi[:, :, :],
                                ALU.subtract).then_inc(dve_pixels, 1)

            def body(s):
                def low(dst, ps, hi, b, ready, war, war_count, done):
                    reached(dve, ready, b + 1)
                    reached(dve, war, war_count)
                    V.tensor_tensor(dst, ps, hi, ALU.subtract).then_inc(done, 1)

                def split_g(j):
                    b = s.ffn
                    reached(dve, act_g[j], b + 1)
                    reached(dve, pe_ffn[TILES - 1], b)
                    for n in (2 * j, 2 * j + 1):
                        last = V.tensor_scalar(gw_hi[:, n, :], g[:, n, :], ln_w_cols[:, n:n + 1], None, ALU.mult)
                    last.then_inc(dve_gw_hi[j], 1)
                    reached(dve, dve_gw_hi[j], b + 1)
                    for n in (2 * j, 2 * j + 1):
                        last = V.scalar_tensor_tensor(gw_lo[:, n, :], g[:, n, :], ln_w_cols[:, n:n + 1], gw_hi[:, n, :],
                                                      ALU.mult, ALU.subtract)
                    last.then_inc(dve_gw[j], 1)

                def means():
                    b = s.finish
                    reached(dve, pe_sums, b + 1)
                    reached(dve, pool_g_var, b)
                    reached(dve, dve_centred, b)
                    V.tensor_scalar(g_mean[:, :], sums_ps[:, 0:TILES], 1.0 / WIDE, None, ALU.mult)
                    V.tensor_scalar(g_minus_mean[:, :], sums_ps[:, 0:TILES], -1.0 / WIDE, None, ALU.mult)
                    V.tensor_scalar(g_square_mean[:, :], sums_ps[:, TILES:2 * TILES], 1.0 / (WIDE * SQUARE_SCALE ** 2), LN_EPS,
                                    ALU.mult, ALU.add).then_inc(dve_g_means, 1)

                def finish():
                    b, p = s.finish, 1 - s.parity
                    reached(dve, dve_g_means, b + 1)
                    for t in range(TILES):
                        reached(dve, act_product[t], b + 1)
                    stores = s.pair - 2 if s.parity == 0 else s.pair - 1
                    if s.looped or stores > 0:
                        dve.wait_ge(stored[p], 16 * stores)
                    for t in range(TILES):
                        last = V.scalar_tensor_tensor(result[p][:, t, :], ln_weight_sum[:, :], g_minus_mean[:, t:t + 1],
                                                      product[:, t, :], ALU.mult, ALU.add)
                    last.then_inc(dve_centred, 1)
                    reached(dve, dve_centred, b + 1)
                    reached(dve, pool_g_rstd, b + 1)
                    reached(dve, pool_h2s, b + 1)
                    for t in range(TILES):
                        last = V.scalar_tensor_tensor(result[p][:, t, :], result[p][:, t, :], g_rstd[:, t:t + 1],
                                                      h2s[p][:, t, :], ALU.mult, ALU.add)
                    last.then_inc(dve_result, 1)

                if s.attn is not None:
                    b = s.attn
                    reached(dve, act_k01, b + 1)
                    reached(dve, pe_kv, b)
                    V.tensor_scalar(v[:, 0:2, :, 0:P].rearrange("p t g n -> p (t g) n"),
                                    kv01_ps[:, :, DIM:2 * DIM].rearrange("p t (g n) -> p t g n", g=GROUPS),
                                    1.0 / WEIGHT_SCALE, None, ALU.mult).then_inc(dve_v01, 1)
                    reached(dve, act_k2, b + 1)
                    V.tensor_scalar(v[:, 2, :, 0:P], kv2_ps[:, DIM:2 * DIM].rearrange("p (g n) -> p g n", g=GROUPS),
                                    1.0 / WEIGHT_SCALE, None, ALU.mult).then_inc(dve_v2, 1)
                if s.mlp is not None:
                    low(xT_lo[:, :, :], xT_ps, xT_hi[:, :, :], s.mlp, act_xT, pe_hid23, s.mlp, dve_xT)
                if s.finish is not None:
                    means()
                if s.ffn is not None:
                    low(hT_lo[:, :, :], hT_ps, hT_hi[:, :, :], s.ffn, act_hT, pe_g[PAIRS - 1], s.ffn, dve_hT)
                if s.finish is not None:
                    finish()
                if s.attn is not None:
                    b = s.attn
                    reached(dve, act_q, b + 1)
                    reached(dve, pe_read, b)
                    V.tensor_scalar(q_hi[:, :, :], q[:, :, :], Q_SCALE, None, ALU.mult).then_inc(dve_q_hi, 1)
                    reached(dve, dve_q_hi, b + 1)
                    V.scalar_tensor_tensor(q_lo[:, :, :], q[:, :, :], Q_SCALE, q_hi[:, :, :], ALU.mult,
                                           ALU.subtract).then_inc(dve_q, 1)
                if s.mlp is not None:
                    b = s.mlp
                    for at, ready, hi_done, done in ((0, act_hid01, dve_hid01_hi, dve_hid01),
                                                     (2, act_hid23, dve_hid23_hi, dve_hid23)):
                        reached(dve, ready, b + 1)
                        reached(dve, pe_mlp, b)
                        V.tensor_scalar(hid_hi[:, at:at + 2, :], hid[:, at:at + 2, :], GELU_SCALE, None,
                                        ALU.mult).then_inc(hi_done, 1)
                        reached(dve, hi_done, b + 1)
                        V.scalar_tensor_tensor(hid_lo[:, at:at + 2, :], hid[:, at:at + 2, :], GELU_SCALE,
                                               hid_hi[:, at:at + 2, :], ALU.mult, ALU.subtract).then_inc(done, 1)
                if s.attn is not None:
                    b = s.attn
                    reached(dve, pe_kv, b + 1)
                    reached(dve, dve_kv, b)
                    for n in range(GROUPS):
                        V.scalar_tensor_tensor(kv[:, n, 0:P], kv_ps[:, n, 0:P], KV_SCALE,
                                               block_mask[:, :, :].rearrange("p a b -> p (a b)"),
                                               ALU.mult, ALU.mult)
                        last = V.tensor_scalar(kv[:, n, P:P + GROUP_HEADS], head_mask[:, :],
                                               kv_ps[:, n, P:P + 1], KV_SCALE, ALU.mult, ALU.mult)
                    last.then_inc(dve_kv_masked, 1)
                    reached(dve, dve_kv_masked, b + 1)
                    V.tensor_copy(kv_hi[:, :, :], kv[:, :, :]).then_inc(dve_kv_hi, 1)
                    reached(dve, dve_kv_hi, b + 1)
                    V.tensor_tensor(kv_lo[:, :, :], kv[:, :, :], kv_hi[:, :, :], ALU.subtract).then_inc(dve_kv, 1)
                if s.ffn is not None:
                    split_g(0)
                    split_g(1)
                if s.mlp is not None:
                    b = s.mlp
                    reached(dve, pe_mlp, b + 1)
                    reached(dve, pool_hxb, b + 1)
                    reached(dve, pool_h2s, b)
                    V.scalar_tensor_tensor(h2[:, :, :], mlp_ps, 1.0 / MLP_SCALE, hxb[:, :, :], ALU.mult,
                                           ALU.add).then_inc(dve_h2, 1)
                    reached(dve, dve_h2, b + 1)
                    for t in range(TILES):
                        last = V.bn_stats(stats2[:, t, :], h2[:, t, :])
                    last.then_inc(dve_stats2, 1)
                    reached(dve, dve_stats2, b + 1)
                    V.memset(spacer[:, :], 0.0)
                    for t in range(TILES):
                        last = V.bn_aggr(mv2[:, t, :], stats2[:, t, :])
                    last.then_inc(dve_mv2, 1)
                if s.attn is not None:
                    b = s.attn
                    reached(dve, pe_read, b + 1)
                    V.tensor_scalar(den[:, :, :, :], read_ps[:, :, :, P:ND], DEN_EPS, 1.0 / OUT_SCALE,
                                    ALU.add, ALU.mult).then_inc(dve_den, 1)
                    reached(dve, dve_den, b + 1)
                    V.reciprocal(z[:, :, :, :], den[:, :, :, :]).then_inc(dve_z, 1)
                    reached(dve, dve_z, b + 1)
                    reached(dve, pe_readT, b)
                    for n in range(GROUPS):
                        last = V.tensor_tensor(
                            read[:, :, n * P:(n + 1) * P].rearrange("p t (a c) -> p t a c", c=HEAD),
                            read_ps[:, n, :, 0:P].rearrange("p t (a c) -> p t a c", c=HEAD),
                            z[:, n, :, :][:, :, :, None].to_broadcast([P, TILES, GROUP_HEADS, HEAD]), ALU.mult)
                    last.then_inc(dve_read, 1)
                if s.ffn is not None:
                    split_g(2)
                    split_g(3)
                if s.embed is not None:
                    b, p = s.embed, 1 - s.parity
                    reached(dve, act_h, b + 1)
                    dve.wait_ge(text_loaded[p], 16 * (s.pair + 1 if s.parity == 0 else s.pair + 2))
                    for t in range(TILES):
                        last = V.bn_stats(stats1[:, t, :], h[p][:, t, :])
                    last.then_inc(dve_stats1, 1)
                    reached(dve, dve_stats1, b + 1)
                    reached(dve, pool_ratio_a, b)
                    V.memset(spacer[:, :], 0.0)
                    for t in range(TILES):
                        last = V.bn_aggr(mv1[:, t, :], stats1[:, t, :])
                    last.then_inc(dve_mv1, 1)
                if s.attn is not None:
                    low(readT_lo[:, :, :], readT_ps, readT_hi[:, :, :], s.attn, act_readT, pe_attn, s.attn, dve_readT)
                if s.fetch is not None:
                    split_pixels(s.fetch, s.parity)
                if s.embed is not None:
                    b, p = s.embed, 1 - s.parity
                    reached(dve, pool_rstd1, b + 1)
                    reached(dve, pe_aT[1], b - 1)
                    for t in range(TILES):
                        last = V.tensor_scalar(a[p][:, t, :], h[p][:, t, :], mv1[:, t, 0:1], rstd1[:, t:t + 1],
                                               ALU.subtract, ALU.mult)
                    last.then_inc(dve_a, 1)
                if s.attn is not None:
                    b, p = s.attn, s.parity
                    reached(dve, pe_attn, b + 1)
                    reached(dve, pool_ratio, b + 1)
                    reached(dve, act_squares1, b)
                    for t in range(TILES):
                        last = V.scalar_tensor_tensor(x1[:, t, :], a[p][:, t, :], ratio[p][:, t:t + 1],
                                                      attn_ps[:, t, :], ALU.mult, ALU.add)
                    last.then_inc(dve_x1, 1)
                if s.embed is not None:
                    for c in range(GROUPS):
                        low(aT_lo[:, c, :], aT_ps[:, c, :], aT_hi[:, c, :], s.embed, act_aT[c], pe_q, s.embed, dve_aT[c])
                if s.attn is not None:
                    b, p = s.attn, s.parity
                    reached(dve, dve_x1, b + 1)
                    reached(dve, pool_hxb, b)
                    V.scalar_tensor_tensor(hx[:, :, :], x1[:, :, :], 1.0 / ATTN_SCALE, h[p][:, :, :], ALU.mult,
                                           ALU.add).then_inc(dve_hx, 1)
                if s.mlp is not None:
                    b = s.mlp
                    reached(dve, pool_rstd2, b + 1)
                    reached(dve, pe_hT, b)
                    for t in range(TILES):
                        last = V.tensor_scalar(hn[:, t, :], h2[:, t, :], mv2[:, t, 0:1], rstd2[:, t:t + 1],
                                               ALU.subtract, ALU.mult)
                    last.then_inc(dve_hn, 1)
                if s.attn is not None:
                    b = s.attn
                    reached(dve, pool_rms, b + 1)
                    reached(dve, pe_xT, b)
                    for t in range(TILES):
                        last = V.tensor_scalar(xn[:, t, :], x1[:, t, :], rms[:, t:t + 1], DIM ** 0.5, ALU.mult, ALU.mult)
                    last.then_inc(dve_xn, 1)

            run(dve, body, {-1: embedding_weights, 0: attention_weights, 1: mlp_weights})

        @block.scalar
        def _(act):
            S = nc.scalar
            act.dma_start(cols_all[:, :], columns).then_inc(columns_loaded, 16)
            act.dma_start(qkv_raw[:, :, :], qkv_w.rearrange("(n p) f -> p n f", p=P)).then_inc(qkv_loaded, 16)
            act.dma_start(rows_all[:, :], rows.to_broadcast([P, 3 * DIM])).then_inc(rows_loaded, 16)
            act.dma_start(proj_raw[:, :, :], proj_w.rearrange("(n p) f -> p n f", p=P)).then_inc(proj_loaded, 16)
            act.dma_start(conv1_raw, conv1_w.rearrange("(n p) f -> p n f", p=P)).then_inc(conv1_loaded, 16)
            act.dma_start(conv2_raw, conv2_w.rearrange("(n p) f -> p n f", p=P)).then_inc(conv2_loaded, 16)

            def high_pixels(b, p, loaded):
                act.wait_ge(pixels_loaded[p], 32 * loaded)
                reached(act, pe_tok, b)
                S.activation(pixels_hi[:, :, :], pixels[p][:, :, :], ACT.Copy).then_inc(act_pixels, 1)

            def absolute_sums():
                act.wait_ge(setup_done, 1)
                act.wait_ge(fc_loaded, 16)
                act.wait_ge(ffn_loaded, 16)
                for n, raw in enumerate((fc_raw, ffn_raw)):
                    last = S.activation(unread_abs[n], raw, ACT.Abs, accum_out=absolute_sum[:, n:n + 1])
                last.then_inc(absolute_summed, 1)
                act.wait_ge(columns_loaded, 16)

            def body(s):
                def high(dst, ps, b, ready, war, war_count, done):
                    reached(act, ready, b + 1)
                    reached(act, war, war_count)
                    S.activation(dst, ps, ACT.Copy).then_inc(done, 1)

                def gelu(j):
                    b = s.ffn
                    reached(act, pe_g[j], b + 1)
                    reached(act, dve_gw[j], b)
                    reached(act, act_g_square[j], b)
                    reached(act, pool_g_part[max(j, 1)], b)
                    S.activation(g[:, 2 * j:2 * j + 2, :], g_ps[j], ACT.Gelu).then_inc(act_g[j], 1)

                def high_total(n):
                    b = s.ffn
                    reached(act, (pool_g_total, pool_square_total)[n], b + 1)
                    reached(act, pe_sums, b)
                    S.activation(total_hi[:, n, :], (g_total, square_total)[n][:, :], ACT.Copy
                                 ).then_inc(act_total_hi[n], 1)

                def take_product(t):
                    b = s.ffn
                    reached(act, pe_ffn[t], b + 1)
                    reached(act, dve_centred, b)
                    S.activation(product[:, t, :], ffn_ps[t], ACT.Copy).then_inc(act_product[t], 1)

                def square(j):
                    b = s.ffn
                    reached(act, act_g[j], b + 1)
                    reached(act, pool_square_part[max(j, 1)], b)
                    S.activation(g_square[:, 2 * j:2 * j + 2, :], g[:, 2 * j:2 * j + 2, :],
                                 ACT.Square, scale=SQUARE_SCALE).then_inc(act_g_square[j], 1)

                if s.attn is not None:
                    b = s.attn
                    reached(act, act_k, b)
                    S.activation(unread_exp[:, :], eps[:, 0:1], ACT.Exp)
                    reached(act, pe_kv01, b + 1)
                    S.activation(k_square[:, 0:2, :], kv01_ps[:, :, 0:DIM], ACT.Square,
                                 scale=1.0 / WEIGHT_SCALE).then_inc(act_k01, 1)
                    reached(act, pe_kv2, b + 1)
                    S.activation(k_square[:, 2, :], kv2_ps[:, 0:DIM], ACT.Square,
                                 scale=1.0 / WEIGHT_SCALE).then_inc(act_k2, 1)
                if s.mlp is not None:
                    high(xT_hi[:, :, :], xT_ps, s.mlp, pe_xT, pe_hid23, s.mlp, act_xT)
                if s.ffn is not None:
                    high(hT_hi[:, :, :], hT_ps, s.ffn, pe_hT, pe_g[PAIRS - 1], s.ffn, act_hT)
                if s.attn is not None:
                    b = s.attn
                    reached(act, act_k2, b + 1)
                    reached(act, pe_kv, b)
                    S.activation(k[:, :, :], k_square[:, :, :], ACT.Exp, scale=-0.5).then_inc(act_k, 1)
                    reached(act, pe_q, b + 1)
                    S.activation(q_square[:, :, :], q_ps, ACT.Square, scale=1.0 / WEIGHT_SCALE
                                 ).then_inc(act_q_square, 1)
                    reached(act, act_q_square, b + 1)
                    reached(act, dve_q, b)
                    S.activation(q[:, :, :], q_square[:, :, :], ACT.Exp, scale=-0.5).then_inc(act_q, 1)
                if s.mlp is not None:
                    b = s.mlp
                    for at, ps, ready, split_done, done in ((0, hid01_ps, pe_hid01, dve_hid01, act_hid01),
                                                            (2, hid23_ps, pe_hid23, dve_hid23, act_hid23)):
                        reached(act, ready, b + 1)
                        reached(act, split_done, b)
                        for n in range(2):
                            last = S.activation(hid[:, at + n, :], ps[:, n, :], ACT.Gelu,
                                                bias=conv1_bias[:, at + n:at + n + 1], scale=1.0 / WEIGHT_SCALE)
                        last.then_inc(done, 1)
                if s.ffn is not None:
                    gelu(0)
                    gelu(1)
                    square(0)
                    square(1)
                    gelu(2)
                    square(2)
                    gelu(3)
                    square(3)
                if s.embed is not None:
                    b, p = s.embed, 1 - s.parity
                    reached(act, pe_tok, b + 1)
                    reached(act, dve_hx, b - 1)
                    S.activation(h[p][:, 0:IMAGE_TILES, :], tok_ps, ACT.Copy, scale=1.0 / WEIGHT_SCALE
                                 ).then_inc(act_h, 1)
                if s.attn is not None:
                    high(readT_hi[:, :, :], readT_ps, s.attn, pe_readT, pe_attn, s.attn, act_readT)
                if s.fetch is not None:
                    high_pixels(s.fetch, s.parity, s.pair + 2)
                if s.ffn is not None:
                    take_product(0)
                    take_product(1)
                if s.embed is not None:
                    for c in range(GROUPS):
                        high(aT_hi[:, c, :], aT_ps[:, c, :], s.embed, pe_aT[c], pe_q, s.embed, act_aT[c])
                if s.attn is not None:
                    b = s.attn
                    reached(act, dve_x1, b + 1)
                    reached(act, pool_rms, b)
                    for t in range(TILES):
                        last = S.activation(unread1[:, t, :], x1[:, t, :], ACT.Square, accum_out=squares1[:, t:t + 1])
                    last.then_inc(act_squares1, 1)
                if s.ffn is not None:
                    take_product(2)
                    high_total(0)
                    high_total(1)

            run(act, body, {-1: lambda: high_pixels(0, 0, 1), 0: absolute_sums})

        @block.tensor
        def _(pe):
            T = nc.tensor
            def ahead_of_embedding():
                pe.wait_ge(tok_ready, 1)

            def ahead_of_attention():
                pe.wait_ge(setup_done, 1)
                pe.wait_ge(absolute_summed, 1)
                T.matmul(D[:, 0:2], ones_f[:, :], absolute_sum[:, :], start=True, stop=True).then_inc(pe_absolute, 1)
                pe.wait_ge(qkv_ready, 1)

            def ahead_of_mlp():
                pe.wait_ge(ternary_ready, 1)
                pe.wait_ge(dve_readT, 1)
                for n in range(WIDE_TILES):
                    last = T.matmul(D[:, 0:DIM], ln_b_wide[:, n, :], ffn_q32[:, n, :], start=n == 0,
                                    stop=n == WIDE_TILES - 1)
                for n in range(WIDE_TILES):
                    last = T.matmul(D[:, DIM:2 * DIM], ln_w_wide[:, n, :], ffn_q32[:, n, :], start=n == 0,
                                    stop=n == WIDE_TILES - 1)
                last.then_inc(pe_shift, 1)

            def three(dst, pairs, bias=None):
                products = []
                for (s_hi, s_lo), (m_hi, m_lo) in pairs:
                    products += [(s_hi, m_hi), (s_hi, m_lo), (s_lo, m_hi)]
                if bias is not None:
                    products.append((ones_bf[:, :], bias))
                for n, (stationary, mov) in enumerate(products):
                    last = T.matmul(dst, stationary, mov, start=n == 0, stop=n == len(products) - 1)
                return last

            def tile(x, c, t):
                return x[:, c, t * P:(t + 1) * P]

            def turn(ps, src, groups_done=None):
                for c in range(GROUPS):
                    for t in range(TILES):
                        last = T.transpose(ps[:, c, t * P:(t + 1) * P], src[:, t, c * P:(c + 1) * P], identity[:, :])
                    if groups_done:
                        last.then_inc(groups_done[c], 1)
                return last

            def body(s):
                def keys_values(t, ps):
                    return three(ps, [((tile(aT_hi, c, t), tile(aT_lo, c, t)),
                                             (qkv_hi[:, c, DIM:], qkv_lo[:, c, DIM:])) for c in range(GROUPS)])

                def wide(j):
                    for half in range(2):
                        w = slice((2 * j + half) * P, (2 * j + half + 1) * P)
                        n = 0
                        for c in range(GROUPS):
                            for part in (hT_hi, hT_lo):
                                last = T.matmul(g_ps[j][:, half, :], fc_q[:, c, w], part[:, c, :], start=n == 0, stop=n == 3)
                                n += 1
                    last.then_inc(pe_g[j], 1)

                def narrow(t):
                    n = 0
                    for w in range(WIDE_TILES):
                        if t == 0 and w % 2 == 0:
                            reached(pe, dve_gw[w // 2], s.ffn + 1)
                        for part in (gw_hi, gw_lo):
                            last = T.matmul(ffn_ps[t], tile(part, w, t), ffn_q[:, w, :], start=n == 0,
                                            stop=n == 2 * WIDE_TILES - 1)
                            n += 1
                    last.then_inc(pe_ffn[t], 1)

                def sums():
                    for n in range(2):
                        reached(pe, pool_total[n], s.finish + 1)
                        for t in range(TILES):
                            at = n * TILES + t
                            for part in (total_hi, total_lo):
                                last = T.matmul(sums_ps[:, at:at + 1], tile(part, n, t), ones_16[:, 0:1],
                                                start=part is total_hi, stop=part is total_lo)
                    last.then_inc(pe_sums, 1)

                if s.attn is not None:
                    b = s.attn
                    for c in range(GROUPS):
                        reached(pe, dve_aT[c], b + 1)
                    reached(pe, dve_x1, b)
                    for t in range(2):
                        last = keys_values(t, kv01_ps[:, t, :])
                    last.then_inc(pe_kv01, 1)
                    reached(pe, dve_readT, b)
                    keys_values(2, kv2_ps).then_inc(pe_kv2, 1)
                if s.finish is not None:
                    if s.attn is not None:
                        reached(pe, dve_aT[1], s.attn + 1)
                    else:
                        reached(pe, act_g[3], s.finish + 1)
                    sums()
                if s.mlp is not None:
                    b = s.mlp
                    reached(pe, dve_xn, b + 1)
                    if s.attn is not None:
                        reached(pe, dve_aT[1], s.attn + 1)
                    turn(xT_ps, xn).then_inc(pe_xT, 1)
                if s.ffn is not None:
                    b = s.ffn
                    reached(pe, dve_hn, b + 1)
                    if s.attn is not None:
                        reached(pe, act_k01, s.attn + 1)
                        reached(pe, dve_v01, s.attn + 1)
                    else:
                        reached(pe, dve_x1, BATCHES)
                    turn(hT_ps, hn).then_inc(pe_hT, 1)
                if s.attn is not None:
                    b = s.attn
                    reached(pe, act_h, b + 1)
                    if s.ffn is not None:
                        for t in range(2):
                            reached(pe, act_product[t], s.ffn)
                    for c in range(GROUPS):
                        w = slice(c * P, (c + 1) * P)
                        last = three(q_ps[:, c, :], [((qkv_hi[:, d, w], qkv_lo[:, d, w]),
                                                            (aT_hi[:, d, :], aT_lo[:, d, :])) for d in range(GROUPS)])
                    last.then_inc(pe_q, 1)
                if s.mlp is not None:
                    b = s.mlp
                    reached(pe, dve_xT, b + 1)
                    if s.finish is not None:
                        reached(pe, dve_g_means, s.finish + 1)
                    for n, (ps, done) in enumerate(((hid01_ps, pe_hid01), (hid23_ps, pe_hid23))):
                        if n and s.attn is not None:
                            reached(pe, act_q_square, s.attn + 1)
                        elif n and s.ffn is not None:
                            for t in range(2):
                                reached(pe, act_product[t], s.ffn)
                        for m in range(2):
                            w = slice((2 * n + m) * P, (2 * n + m + 1) * P)
                            last = three(ps[:, m, :], [((conv1_hi[:, c, w], conv1_lo[:, c, w]),
                                                              (xT_hi[:, c, :], xT_lo[:, c, :])) for c in range(GROUPS)])
                        last.then_inc(done, 1)
                if s.ffn is not None:
                    b = s.ffn
                    reached(pe, dve_hT, b + 1)
                    if s.attn is not None:
                        reached(pe, act_k2, s.attn + 1)
                        reached(pe, dve_v2, s.attn + 1)
                    reached(pe, act_product[2], b)
                    wide(0)
                if s.attn is not None:
                    b = s.attn
                    reached(pe, act_k, b + 1)
                    reached(pe, dve_v2, b + 1)
                    reached(pe, dve_v01, b + 1)
                    if s.ffn is not None:
                        reached(pe, dve_hT, s.ffn + 1)
                    for n in range(GROUPS):
                        for t in range(TILES):
                            last = T.matmul(kv_ps[:, n, :], k[:, t, n * P:(n + 1) * P], v[:, t, n, :],
                                            start=t == 0, stop=t == TILES - 1)
                    last.then_inc(pe_kv, 1)
                if s.ffn is not None:
                    if s.mlp is not None:
                        reached(pe, act_hid01, s.mlp + 1)
                    else:
                        reached(pe, dve_g_means, s.finish + 1)
                    wide(1)
                if s.mlp is not None:
                    b = s.mlp
                    reached(pe, dve_hid01, b + 1)
                    reached(pe, dve_hid23, b + 1)
                    for t in range(TILES):
                        last = three(mlp_ps[:, t, :],
                                     [((tile(hid_hi, n, t), tile(hid_lo, n, t)), (conv2_hi[:, n, :], conv2_lo[:, n, :]))
                                      for n in range(HIDDEN_TILES)])
                    last.then_inc(pe_mlp, 1)
                if s.ffn is not None:
                    if s.attn is not None:
                        reached(pe, dve_kv, s.attn + 1)
                    wide(2)
                if s.attn is not None:
                    b = s.attn
                    reached(pe, dve_kv, b + 1)
                    reached(pe, dve_q, b + 1)
                    if s.ffn is not None:
                        reached(pe, act_g[0], s.ffn + 1)
                    for t in range(TILES):
                        for n in range(GROUPS):
                            last = three(read_ps[:, n, t, :],
                                         [((tile(q_hi, n, t), tile(q_lo, n, t)), (kv_hi[:, n, :], kv_lo[:, n, :]))])
                    last.then_inc(pe_read, 1)
                if s.ffn is not None:
                    reached(pe, act_g[1], s.ffn + 1)
                    wide(3)
                if s.embed is not None:
                    b, p = s.embed, 1 - s.parity
                    reached(pe, dve_pixels, b + 1)
                    if s.mlp is not None:
                        reached(pe, dve_h2, s.mlp + 1)
                    elif s.attn is not None:
                        reached(pe, act_q_square, s.attn + 1)
                    for t in range(IMAGE_TILES):
                        last = three(tok_ps[:, t, :],
                                     [tuple(tuple(x[0:P if n < FULL else REST + 1, n, cut] for x in pair)
                                            for pair, cut in (((pixels_hi, pixels_lo), slice(t * P, (t + 1) * P)),
                                                              ((tok_hi, tok_lo), slice(0, DIM))))
                                      for n in range(FULL + 1)])
                    last.then_inc(pe_tok, 1)
                if s.attn is not None:
                    b = s.attn
                    reached(pe, dve_read, b + 1)
                    turn(readT_ps, read).then_inc(pe_readT, 1)
                if s.ffn is not None:
                    if s.mlp is not None:
                        reached(pe, dve_h2, s.mlp + 1)
                    narrow(0)
                    if s.embed is not None:
                        reached(pe, act_h, s.embed + 1)
                    narrow(1)
                if s.attn is not None:
                    b = s.attn
                    reached(pe, dve_readT, b + 1)
                    if s.ffn is not None:
                        reached(pe, act_g[2], s.ffn + 1)
                    for t in range(TILES):
                        last = three(attn_ps[:, t, :],
                                     [((tile(readT_hi, c, t), tile(readT_lo, c, t)), (proj_hi[:, c, :], proj_lo[:, c, :]))
                                      for c in range(GROUPS)], bias=attn_bias[:, :])
                    last.then_inc(pe_attn, 1)
                if s.embed is not None:
                    b, p = s.embed, 1 - s.parity
                    reached(pe, dve_a, b + 1)
                    if s.ffn is not None:
                        reached(pe, act_g[3], s.ffn + 1)
                    elif s.mlp is not None:
                        reached(pe, act_hid01, s.mlp + 1)
                    turn(aT_ps, a[p], pe_aT)
                if s.ffn is not None:
                    if s.attn is not None:
                        reached(pe, dve_readT, s.attn + 1)
                    narrow(2)

            run(pe, body, {-1: ahead_of_embedding, 0: ahead_of_attention, 1: ahead_of_mlp})


_INS = ["image", "text", "tok_w", "tok_b", "columns", "rows", "qkv_w", "proj_w", "conv1_w", "conv2_w",
        "fc_w", "ffn_w"]


def kernel(x, txt, L0_tok_W, L0_tok_b, L0_attn_scale1, L0_attn_scale2, L0_attn_gamma, L0_attn_qkv_w,
           L0_attn_proj_w, L0_attn_proj_b, L0_attn_conv1_w, L0_attn_conv1_b, L0_attn_conv2_w,
           L0_attn_conv2_b, L0_ffn_W_fc, L0_ffn_ln_w, L0_ffn_ln_b, L0_ffn_W_proj):
    import concourse.bacc as _bacc
    from concourse.bass_utils import run_bass_kernel_spmd as _run

    image = np.asarray(x).reshape(BATCHES, CHANNELS, GRID, PATCH, GRID, PATCH).transpose(0, 1, 3, 5, 2, 4)
    image = image.reshape(BATCHES, PIXELS, PATCHES)
    columns = np.concatenate([np.asarray(c).reshape(-1, P).T for c in (
        L0_attn_scale1, L0_attn_scale2, L0_attn_conv1_b, L0_ffn_ln_b, L0_ffn_ln_w)], axis=1)
    rows = np.concatenate([np.asarray(r)[None] for r in (
        L0_attn_gamma, L0_attn_proj_b, L0_attn_conv2_b)], axis=1)
    given = [image, txt, np.asarray(L0_tok_W).T, L0_tok_b, columns, rows,
             np.asarray(L0_attn_qkv_w).T, np.asarray(L0_attn_proj_w).T, np.asarray(L0_attn_conv1_w).T,
             np.asarray(L0_attn_conv2_w).T, np.asarray(L0_ffn_W_fc).T, np.asarray(L0_ffn_W_proj).T]
    nc = _bacc.Bacc("TRN2", target_bir_lowering=False, num_devices=1)
    arrays, args = {}, []
    for name, array in zip(_INS, given):
        array = np.ascontiguousarray(array)
        arrays[f"in_{name}"] = array
        args.append(nc.dram_tensor(f"in_{name}", array.shape, mybir.dt.from_np(array.dtype),
                                   kind="ExternalInput").ap())
    out = nc.dram_tensor("out", (BATCHES, TOKENS, DIM), mybir.dt.float32, kind="ExternalOutput").ap()
    build(nc, *args, out)
    r = _run(nc, [arrays], core_ids=[0])
    return r.results[0]["out"]
```

```python
import numpy as np
from contextlib import ExitStack

import concourse.bass as bass
from concourse import mybir

P = 128
BATCHES = 32
GRID, PATCH, CHANNELS = 16, 14, 3
PATCHES = GRID * GRID
PIXELS = CHANNELS * PATCH * PATCH
TEXT = 128
TOKENS = PATCHES + TEXT
TILES = TOKENS // P
IMAGE_TILES = PATCHES // P
DIM = 256
GROUPS = DIM // P
HEADS, HEAD = 16, 16
GROUP_HEADS = P // HEAD
HIDDEN = 512
HIDDEN_TILES = HIDDEN // P
WIDE = 1024
WIDE_TILES = WIDE // P
PAIRS = WIDE_TILES // 2
FULL = PIXELS // P
REST = PIXELS - FULL * P
LN_EPS = 1e-5
RMS_EPS = 1e-6

WEIGHT_SCALE = 64.0
KV_SCALE = 1.0 / 64
Q_SCALE = 16384.0
OUT_SCALE = 8.0
GELU_SCALE = 16.0
ATTN_SCALE = OUT_SCALE * WEIGHT_SCALE
MLP_SCALE = GELU_SCALE * WEIGHT_SCALE
SQUARE_SCALE = 1.0 / 16
RMS_FACTOR = (DIM ** 0.5 + RMS_EPS) / DIM ** 0.5
DEN_EPS = 1e-6 * Q_SCALE * KV_SCALE

FIRST_LOOPED, LAST_LOOPED = 6, 29


def build(nc, image, text, tok_w, tok_b, columns, rows, qkv_w, proj_w, conv1_w, conv2_w, fc_w,
          ffn_w, out):
    fp32, fp16, bf16 = mybir.dt.float32, mybir.dt.float16, mybir.dt.bfloat16
    ALU, ACT, AX = mybir.AluOpType, mybir.ActivationFunctionType, mybir.AxisListType

    out_v = out.rearrange("b (t p) e -> b p t e", p=P)

    ctx = ExitStack()
    with ctx:
        def sb(name, shape, dt=fp32):
            return ctx.enter_context(nc.sbuf_tensor(name, shape, dt))

        def sem(name):
            return ctx.enter_context(nc.semaphore(name))

        tok_hi, tok_lo = (sb(f"tok_{s}", [P, FULL + 1, DIM], fp16) for s in ("hi", "lo"))
        qkv_hi, qkv_lo = (sb(f"qkv_{s}", [P, GROUPS, 3 * DIM], fp16) for s in ("hi", "lo"))
        proj_hi, proj_lo = (sb(f"proj_{s}", [P, GROUPS, DIM], fp16) for s in ("hi", "lo"))
        conv1_hi, conv1_lo = (sb(f"conv1_{s}", [P, GROUPS, HIDDEN], fp16) for s in ("hi", "lo"))
        conv2_hi, conv2_lo = (sb(f"conv2_{s}", [P, HIDDEN_TILES, DIM], fp16) for s in ("hi", "lo"))
        fc_q = sb("fc_q", [P, GROUPS, WIDE], fp16)
        ffn_q = sb("ffn_q", [P, WIDE_TILES, DIM], fp16)
        attn_bias = sb("attn_bias", [P, DIM], bf16)
        ones_bf = sb("ones_bf", [P, P], bf16)
        mlp_bias = sb("mlp_bias", [P, DIM])
        ln_shift = sb("ln_shift", [P, DIM])
        identity = sb("identity", [P, P])
        head_mask = sb("head_mask", [P, GROUP_HEADS])
        block_mask = sb("block_mask", [P, GROUP_HEADS, HEAD])
        ln_weight_sum = sb("ln_weight_sum", [P, DIM])
        minus_half, eps, attn_scale = (sb(s, [P, 8]) for s in ("minus_half", "eps", "attn_scale"))
        spacer = sb("spacer", [P, 1])
        cols_all = sb("cols_all", [P, columns.shape[1]])
        scale1_cols, scale2_cols = cols_all[:, 0:GROUPS], cols_all[:, GROUPS:2 * GROUPS]
        conv1_bias = cols_all[:, 2 * GROUPS:2 * GROUPS + HIDDEN_TILES]
        ln_b_cols, ln_w_cols = (cols_all[:, 2 * GROUPS + HIDDEN_TILES + n * WIDE_TILES:][:, 0:WIDE_TILES]
                                for n in range(2))
        rows_all = sb("rows_all", [P, 3 * DIM])
        gamma_all, proj_b_all, conv2_b_all = (rows_all[:, n * DIM:(n + 1) * DIM] for n in range(3))

        tok_raw = sb("tok_raw", [P, FULL + 1, DIM])
        proj_raw = sb("proj_raw", [P, GROUPS, DIM])
        bias_rest = sb("bias_rest", [P, DIM])
        bias_part = sb("bias_part", [P, DIM], bf16)
        absolute_sum = sb("absolute_sum", [P, 2])
        ones_f = sb("ones_f", [P, P])
        ones_16 = sb("ones_16", [P, 2], fp16)
        threshold = sb("threshold", [P, 2, 3])

        pixels = [sb(f"pixels{p}", [P, FULL + 1, PATCHES]) for p in range(2)]
        pixels_hi, pixels_lo = (sb(f"pixels_{s}", [P, FULL + 1, PATCHES], fp16) for s in ("hi", "lo"))
        h = [sb(f"h{p}", [P, TILES, DIM]) for p in range(2)]
        a = [sb(f"a{p}", [P, TILES, DIM]) for p in range(2)]
        ratio = [sb(f"ratio{p}", [P, TILES]) for p in range(2)]
        stats1 = sb("stats1", [P, TILES, 6])
        mv1 = sb("mv1", [P, TILES, 2])
        var1 = sb("var1", [P, TILES])
        rstd1 = sb("rstd1", [P, 2 * TILES])
        ratio_part = sb("ratio_part", [P, 2 * TILES])
        aT_hi, aT_lo = (sb(f"aT_{s}", [P, GROUPS, TOKENS], fp16) for s in ("hi", "lo"))
        k_square = sb("k_square", [P, TILES, DIM])
        k = sb("k", [P, TILES, DIM])
        v = sb("v", [P, TILES, GROUPS, P + 1])
        q_square = sb("q_square", [P, GROUPS, TOKENS])
        q = sb("q", [P, GROUPS, TOKENS])
        q_hi, q_lo = (sb(f"q_{s}", [P, GROUPS, TOKENS], fp16) for s in ("hi", "lo"))
        kv = sb("kv", [P, GROUPS, P + GROUP_HEADS])
        kv_hi, kv_lo = (sb(f"kv_{s}", [P, GROUPS, P + GROUP_HEADS], fp16) for s in ("hi", "lo"))
        den = sb("den", [P, GROUPS, TILES, GROUP_HEADS])
        z = sb("z", [P, GROUPS, TILES, GROUP_HEADS])
        read = sb("read", [P, TILES, DIM])
        readT_hi, readT_lo = (sb(f"readT_{s}", [P, GROUPS, TOKENS], fp16) for s in ("hi", "lo"))
        x1 = sb("x1", [P, TILES, DIM])
        unread_exp = sb("unread_exp", [P, 1])
        unread1 = sb("unread1", [P, TILES, DIM], bf16)
        squares1 = sb("squares1", [P, TILES])
        rms = sb("rms", [P, TILES])
        xn = sb("xn", [P, TILES, DIM])
        hx = sb("hx", [P, TILES, DIM])
        hxb = sb("hxb", [P, TILES, DIM])
        xT_hi, xT_lo = (sb(f"xT_{s}", [P, GROUPS, TOKENS], fp16) for s in ("hi", "lo"))
        hid = sb("hid", [P, HIDDEN_TILES, TOKENS])
        hid_hi, hid_lo = (sb(f"hid_{s}", [P, HIDDEN_TILES, TOKENS], fp16) for s in ("hi", "lo"))
        h2 = sb("h2", [P, TILES, DIM])
        h2s = [sb(f"h2s{p}", [P, TILES, DIM]) for p in range(2)]
        stats2 = sb("stats2", [P, TILES, 6])
        mv2 = sb("mv2", [P, TILES, 2])
        var2 = sb("var2", [P, TILES])
        rstd2 = sb("rstd2", [P, TILES])
        hn = sb("hn", [P, TILES, DIM])
        hT_hi, hT_lo = (sb(f"hT_{s}", [P, GROUPS, TOKENS], fp16) for s in ("hi", "lo"))
        g = sb("g", [P, WIDE_TILES, TOKENS])
        g_square = sb("g_square", [P, WIDE_TILES, TOKENS])
        g_part, square_part = (sb(f"{s}_part", [P, 2, TOKENS]) for s in ("g", "square"))
        g_total, square_total = (sb(f"{s}_total", [P, TOKENS]) for s in ("g", "square"))
        total_hi, total_lo = (sb(f"total_{s}", [P, 2, TOKENS], fp16) for s in ("hi", "lo"))
        g_mean = sb("g_mean", [P, TILES])
        g_minus_mean = sb("g_minus_mean", [P, TILES])
        g_square_mean = sb("g_square_mean", [P, TILES])
        g_mean_square = sb("g_mean_square", [P, TILES])
        g_spread = sb("g_spread", [P, TILES])
        g_var = sb("g_var", [P, TILES])
        g_rstd = sb("g_rstd", [P, TILES])
        gw_hi, gw_lo = (sb(f"gw_{s}", [P, WIDE_TILES, TOKENS], fp16) for s in ("hi", "lo"))
        product = sb("product", [P, TILES, DIM])
        result = [sb(f"result{p}", [P, TILES, DIM]) for p in range(2)]

        g_flat, g_square_flat, gw_hi_flat, gw_lo_flat = (
            x[:, :, :].rearrange("p n f -> p (n f)") for x in (g, g_square, gw_hi, gw_lo))
        RAW = GROUPS * WIDE
        fc_raw, ffn_raw = g_flat[:, 0:RAW], g_square_flat[:, 0:RAW]
        conv1_raw = g_flat[:, RAW:RAW + GROUPS * HIDDEN].rearrange("p (n f) -> p n f", n=GROUPS)
        conv2_raw = g_square_flat[:, RAW:RAW + HIDDEN_TILES * DIM].rearrange("p (n f) -> p n f", n=HIDDEN_TILES)
        ffn_q32 = ffn_raw.rearrange("p (n f) -> p n f", n=WIDE_TILES)
        unread_abs = below = [x[:, 0:RAW] for x in (gw_hi_flat, gw_lo_flat)]
        hid_flat = hid[:, :, :].rearrange("p n f -> p (n f)")
        qkv_raw = hid_flat.rearrange("p (n f) -> p n f", n=GROUPS)
        ln_b_wide, ln_w_wide = (fc_raw[:, n * WIDE:(n + 1) * WIDE].rearrange("p (n f) -> p n f", n=WIDE_TILES)
                                for n in range(2))

        BANK = 512
        A, B, C, D = (ctx.enter_context(nc.psum_tensor(f"pair_{s}", [P, 2 * BANK], fp32)) for s in "ABCD")

        def by_token(pair):
            return pair[:, 0:TILES * DIM].rearrange("p (t e) -> p t e", t=TILES)

        def by_channel(pair):
            return pair[:, :].rearrange("p (g n) -> p g n", g=2)[:, :, 0:TOKENS]

        kv01_ps = A[:, :].rearrange("p (t n) -> p t n", t=2)
        kv2_ps = D[:, BANK:2 * BANK]
        xT_ps, q_ps, hT_ps = by_channel(B), by_channel(C), by_channel(A)
        hid01_ps, hid23_ps = by_channel(B), by_channel(C)
        g_ps = [by_channel(pair) for pair in (D, B, A, B)]
        kv_ps = A[:, 0:GROUPS * (P + 1)].rearrange("p (g n) -> p g n", g=GROUPS)
        mlp_ps = by_token(C)
        ND = P + GROUP_HEADS
        read_ps = D[:, :].rearrange("p (g n) -> p g n", g=2)[:, :, 0:TILES * ND].rearrange(
            "p g (t n) -> p g t n", t=TILES)
        tok_ps = C[:, 0:BANK].rearrange("p (t e) -> p t e", t=IMAGE_TILES)
        readT_ps, aT_ps = by_channel(D), by_channel(B)
        attn_ps = by_token(A)
        ffn_ps = [C[:, BANK:BANK + DIM], C[:, 0:DIM], D[:, 0:DIM]]
        sums_ps = A[:, TOKENS:TOKENS + 2 * TILES]

        (tok_loaded, columns_loaded, qkv_loaded, rows_loaded, proj_loaded, conv1_loaded, conv2_loaded,
         fc_loaded, ffn_loaded) = (sem(f"{s}_loaded") for s in (
             "tok", "columns", "qkv", "rows", "proj", "conv1", "conv2", "fc", "ffn"))
        setup_done = sem("setup_done")
        ones_row_set = sem("ones_row_set")
        setup_chain = sem("setup_chain")
        pool_chain = sem("pool_chain")
        tok_ready, qkv_ready, ternary_ready, shift_ready = (
            sem(f"{s}_ready") for s in ("tok", "qkv", "ternary", "shift"))
        absolute_summed = sem("absolute_summed")
        wide_ready = sem("wide_ready")
        bias_ready = sem("bias_ready")
        absolute_taken = sem("absolute_taken")
        compared = sem("compared")
        pe_absolute, pe_shift = sem("pe_absolute"), sem("pe_shift")
        pixels_loaded = [sem(f"pixels_loaded{p}") for p in range(2)]
        text_loaded = [sem(f"text_loaded{p}") for p in range(2)]
        stored = [sem(f"stored{p}") for p in range(2)]
        (pe_kv01, pe_kv2, pe_xT, pe_q, pe_hT, pe_hid01, pe_hid23, pe_kv, pe_mlp, pe_read, pe_tok,
         pe_readT, pe_attn) = (sem(f"pe_{s}") for s in (
             "kv01", "kv2", "xT", "q", "hT", "hid01", "hid23", "kv", "mlp", "read", "tok",
             "readT", "attn"))
        pe_aT, act_aT, dve_aT = ([sem(f"{s}_aT{c}") for c in range(GROUPS)] for s in ("pe", "act", "dve"))
        pe_g = [sem(f"pe_g{j}") for j in range(PAIRS)]
        pe_ffn = [sem(f"pe_ffn{t}") for t in range(TILES)]
        pe_sums = sem("pe_sums")
        (act_k01, act_k2, act_k, act_xT, act_q_square, act_q, act_hT, act_hid01, act_hid23, act_h,
         act_readT, act_squares1, act_pixels) = (sem(f"act_{s}") for s in (
             "k01", "k2", "k", "xT", "q_square", "q", "hT", "hid01", "hid23", "h", "readT",
             "squares1", "pixels"))
        act_product = [sem(f"act_product{t}") for t in range(TILES)]
        act_exp_table = sem("act_exp_table")
        act_g, act_g_square = ([sem(f"act_{s}{j}") for j in range(PAIRS)] for s in ("g", "g_square"))
        (dve_v01, dve_v2, dve_xT, dve_q_hi, dve_q, dve_hT, dve_hid01_hi, dve_hid01, dve_hid23_hi,
         dve_hid23, dve_kv_masked, dve_kv_hi, dve_kv, dve_h2, dve_stats2, dve_mv2, dve_den, dve_z,
         dve_read, dve_hn, dve_stats1, dve_mv1, dve_readT, dve_a, dve_x1, dve_hx,
         dve_xn, dve_pixels) = (sem(f"dve_{s}") for s in (
             "v01", "v2", "xT", "q_hi", "q", "hT", "hid01_hi", "hid01", "hid23_hi", "hid23",
             "kv_masked", "kv_hi", "kv", "h2", "stats2", "mv2", "den", "z", "read", "hn",
             "stats1", "mv1", "readT", "a", "x1", "hx", "xn", "pixels"))
        dve_gw_hi, dve_gw = ([sem(f"dve_{s}{j}") for j in range(PAIRS)] for s in ("gw_hi", "gw"))
        dve_g_means, dve_g_mean_square, dve_g_spread, dve_g_var, dve_centred, dve_result = (
            sem(f"dve_{s}") for s in ("g_means", "g_mean_square", "g_spread", "g_var", "centred", "result"))
        (pool_var2, pool_rstd2, pool_h2s, pool_var1, pool_rstd1, pool_ratio_a, pool_ratio_b,
         pool_ratio, pool_g_rstd, pool_rms, pool_rstd1_eps,
         pool_hxb) = (sem(f"pool_{s}") for s in (
             "var2", "rstd2", "h2s", "var1", "rstd1", "ratio_a", "ratio_b", "ratio",
             "g_rstd", "rms", "rstd1_eps", "hxb"))
        pool_g_part, square_part_done = ([None] + [sem(f"{s}{j}") for j in range(1, PAIRS)]
                                         for s in ("pool_g_part", "square_part_done"))
        pool_g_total, square_total_done = sem("pool_g_total"), sem("square_total_done")
        act_total_hi, total_split = ([sem(f"{s}{n}") for n in range(2)] for s in ("act_total_hi", "total_split"))

        def reached(engine, semaphore, count):
            if not isinstance(count, int) or count > 0:
                engine.wait_ge(semaphore, count)

        class Step:

            def __init__(self, pair, parity):
                self.looped = not isinstance(pair, int)
                step = 2 * pair + parity
                self.parity = parity
                self.embed, self.attn, self.mlp, self.ffn, self.finish, self.fetch = (
                    step + d if self.looped or 0 <= step + d < BATCHES else None
                    for d in (1, 0, -1, -2, -3, 2))
                if self.looped:
                    self.pair = pair
                else:
                    self.pair = step // 2

        def last_but_one(b):
            return isinstance(b, int) and b == BATCHES - 2

        def squares_by_vector(b):
            return isinstance(b, int) and b == BATCHES - 1

        def run(engine, body, ahead=None):
            for step in range(-1, FIRST_LOOPED):
                if ahead and step in ahead:
                    ahead[step]()
                body(Step(step // 2, step % 2))
            with engine.Fori(FIRST_LOOPED // 2, (LAST_LOOPED + 1) // 2) as pair:
                for parity in range(2):
                    body(Step(pair, parity))
            for step in range(LAST_LOOPED + 1, BATCHES + 3):
                body(Step(step // 2, step % 2))

        block = ctx.enter_context(nc.Block())

        @block.sync
        def _(sp):
            def by_row(w):
                return w.rearrange("(n p) f -> p n f", p=P)

            def fetch_pixels(parity, b):
                sp.dma_start(pixels[parity][:, 0:FULL, :],
                             image[b, 0:FULL * P, :].rearrange("(n p) f -> p n f", p=P)
                             ).then_inc(pixels_loaded[parity], 16)
                sp.dma_start(pixels[parity][0:REST, FULL, :],
                             image[b, FULL * P:PIXELS, :]).then_inc(pixels_loaded[parity], 16)

            sp.dma_start(pixels[0][:, 0:FULL, :], image[0, 0:FULL * P, :].rearrange("(n p) f -> p n f", p=P)
                         ).then_inc(pixels_loaded[0], 16)
            sp.wait_ge(ones_row_set, 1)
            sp.dma_start(pixels[0][0:REST, FULL, :], image[0, FULL * P:PIXELS, :]).then_inc(pixels_loaded[0], 16)
            sp.dma_start(tok_raw[:, 0:FULL, :], tok_w[0:FULL * P, :].rearrange("(n p) f -> p n f", p=P)
                         ).then_inc(tok_loaded, 16)
            sp.dma_start(tok_raw[0:REST, FULL, :], tok_w[FULL * P:PIXELS, :]).then_inc(tok_loaded, 16)
            sp.dma_start(tok_raw[REST:REST + 1, FULL, :], tok_b[None, :]).then_inc(tok_loaded, 16)
            for dst, src, loaded in ((cols_all[:, :], columns, columns_loaded), (qkv_raw, by_row(qkv_w), qkv_loaded),
                                     (h[0][:, IMAGE_TILES, :], text[0, :, :], text_loaded[0]),
                                     (conv1_raw, by_row(conv1_w), conv1_loaded),
                                     (rows_all[:, :], rows.to_broadcast([P, 3 * DIM]), rows_loaded),
                                     (proj_raw[:, :, :], by_row(proj_w), proj_loaded)):
                sp.dma_start(dst, src).then_inc(loaded, 16)
            fetch_pixels(1, 1)
            for dst, src, loaded in ((conv2_raw, by_row(conv2_w), conv2_loaded),
                                     (fc_raw.rearrange("p (n f) -> p n f", n=GROUPS), by_row(fc_w), fc_loaded),
                                     (ffn_q32, by_row(ffn_w), ffn_loaded)):
                sp.dma_start(dst, src).then_inc(loaded, 16)

            def body(s):
                if s.embed is not None and (s.looped or s.embed > 0):
                    p = 1 - s.parity
                    reached(sp, dve_hx, s.embed - 1)
                    sp.dma_start(h[p][:, IMAGE_TILES, :], text[s.embed, :, :]).then_inc(text_loaded[p], 16)
                if s.fetch is not None and not (isinstance(s.fetch, int) and s.fetch < 2):
                    reached(sp, act_pixels, s.fetch - 1)
                    reached(sp, dve_pixels, s.fetch - 1)
                    fetch_pixels(s.parity, s.fetch)
                if s.finish is not None:
                    p = 1 - s.parity
                    reached(sp, dve_result, s.finish + 1)
                    sp.dma_start(out_v[s.finish, :, :, :], result[p][:, :, :]).then_inc(stored[p], 16)

            run(sp, body)
            for p in range(2):
                sp.wait_ge(stored[p], 16 * (BATCHES // 2))

        @block.gpsimd
        def _(pool):
            G = nc.gpsimd
            G.memset(identity[:, :], 0.0)
            G.memset(head_mask[:, :], 1.0)
            G.memset(minus_half[:, :], -0.5)
            G.memset(eps[:, :], LN_EPS)
            G.memset(attn_scale[:, :], ATTN_SCALE)
            G.memset(ones_f[:, :], 1.0)
            G.memset(ones_bf[:, :], 1.0)
            G.memset(ones_16[:, :], 1.0)
            G.memset(attn_bias[:, :], 0.0)
            G.memset(v[:, :, :, P:P + 1], 1.0).then_inc(pool_chain, 1)
            pool.wait_ge(pool_chain, 1)
            G.affine_select(out=identity[:, :], in_=identity[:, :], compare_op=ALU.not_equal, fill=1.0,
                            base=0, pattern=[[-1, P]], channel_multiplier=1)
            G.affine_select(out=head_mask[:, :], in_=head_mask[:, :], compare_op=ALU.is_ge, fill=0.0,
                            base=0, pattern=[[-HEAD, GROUP_HEADS]], channel_multiplier=1).then_inc(pool_chain, 1)
            pool.wait_ge(pool_chain, 2)
            G.affine_select(out=head_mask[:, :], in_=head_mask[:, :], compare_op=ALU.is_ge, fill=0.0,
                            base=HEAD - 1, pattern=[[HEAD, GROUP_HEADS]], channel_multiplier=-1).then_inc(pool_chain, 1)
            pool.wait_ge(pool_chain, 3)
            G.tensor_copy(block_mask[:, :, :], head_mask[:, :, None].to_broadcast([P, GROUP_HEADS, HEAD])
                          ).then_inc(setup_done, 1)

            def power(dst, src, n, done):
                return G.tensor_tensor(dst, src, minus_half[:, 0:n], ALU.pow).then_inc(done, 1)

            def body(s):
                def g_deviation():
                    b = s.finish
                    reached(pool, dve_g_var, b + 1)
                    reached(pool, dve_result, b)
                    power(g_rstd[:, :], g_var[:, :], TILES, pool_g_rstd)

                def add_pair(src, part, done, ready, j):
                    b = s.ffn
                    reached(pool, ready[j], b + 1)
                    if j == 1:
                        reached(pool, ready[0], b + 1)
                        first = src[:, 0:2, :]
                    else:
                        reached(pool, done[j - 1], b + 1)
                        first = part[:, :, :]
                    G.tensor_tensor(part[:, :, :], first, src[:, 2 * j:2 * j + 2, :], ALU.add).then_inc(done[j], 1)

                def add_halves(part, total, parts_done, done):
                    b = s.ffn
                    reached(pool, parts_done[PAIRS - 1], b + 1)
                    G.tensor_tensor(total[:, :], part[:, 0, :], part[:, 1, :], ALU.add).then_inc(done, 1)

                def low_total(n, b):
                    reached(pool, act_total_hi[n], b + 1)
                    G.tensor_tensor(total_lo[:, n, :], (g_total, square_total)[n][:, :], total_hi[:, n, :],
                                    ALU.subtract).then_inc(total_split[n], 1)

                def add_g(j):
                    if j == 1:
                        reached(pool, pool_g_total, s.ffn)
                    add_pair(g, g_part, pool_g_part, act_g, j)

                def add_square(j):
                    if j == 1:
                        reached(pool, square_total_done, s.ffn)
                    add_pair(g_square, square_part, square_part_done, act_g_square, j)

                if s.finish is not None and s.attn is not None:
                    g_deviation()
                if s.ffn is not None:
                    add_g(1)
                    if not squares_by_vector(s.ffn):
                        add_square(1)
                if last_but_one(s.finish):
                    low_total(0, s.finish)
                    low_total(1, s.finish)
                if s.finish is not None and s.ffn is None:
                    g_deviation()
                if s.mlp is not None:
                    b = s.mlp
                    reached(pool, dve_mv2, b + 1)
                    G.tensor_tensor(var2[:, :], mv2[:, :, 1], eps[:, 0:TILES], ALU.add).then_inc(pool_var2, 1)
                    reached(pool, pool_var2, b + 1)
                    reached(pool, dve_hn, b)
                    power(rstd2[:, :], var2[:, :], TILES, pool_rstd2)
                if s.ffn is not None:
                    add_g(2)
                    if not squares_by_vector(s.ffn):
                        add_square(2)
                    if last_but_one(s.ffn):
                        g_deviation()
                    add_g(3)
                    add_halves(g_part, g_total, pool_g_part, pool_g_total)
                if s.embed is not None:
                    b, p = s.embed, 1 - s.parity
                    reached(pool, dve_mv1, b + 1)
                    reached(pool, dve_a, b)
                    power(rstd1[:, 0:TILES], mv1[:, :, 1], TILES, pool_rstd1)
                    G.tensor_tensor(var1[:, :], mv1[:, :, 1], eps[:, 0:TILES], ALU.add).then_inc(pool_var1, 1)
                    reached(pool, pool_var1, b + 1)
                    power(rstd1[:, TILES:2 * TILES], var1[:, :], TILES, pool_rstd1_eps)
                    reached(pool, pool_rstd1, b + 1)
                    G.tensor_tensor(ratio_part[:, 0:TILES], mv1[:, :, 1], rstd1[:, 0:TILES],
                                    ALU.mult).then_inc(pool_ratio_a, 1)
                    reached(pool, pool_rstd1_eps, b + 1)
                    reached(pool, pool_ratio_a, b + 1)
                    G.tensor_tensor(ratio_part[:, TILES:2 * TILES], ratio_part[:, 0:TILES],
                                    rstd1[:, TILES:2 * TILES], ALU.mult).then_inc(pool_ratio_b, 1)
                    reached(pool, pool_ratio_b, b + 1)
                    reached(pool, dve_x1, b - 1)
                    G.tensor_tensor(ratio[p][:, :], ratio_part[:, TILES:2 * TILES], attn_scale[:, 0:TILES],
                                    ALU.mult).then_inc(pool_ratio, 1)
                    if not s.looped and b == 1:
                        ternary(0)
                if s.ffn is not None and not squares_by_vector(s.ffn):
                    add_square(3)
                if s.attn is not None:
                    b = s.attn
                    reached(pool, act_squares1, b + 1)
                    reached(pool, dve_xn, b)
                    power(rms[:, :], squares1[:, :], TILES, pool_rms)
                if s.ffn is not None and not squares_by_vector(s.ffn):
                    add_halves(square_part, square_total, square_part_done, square_total_done)
                if s.ffn is not None and s.attn is not None:
                    low_total(0, s.ffn)
                    low_total(1, s.ffn)
                elif squares_by_vector(s.ffn):
                    g_deviation()
                    low_total(0, s.ffn)
                if s.mlp is not None:
                    b = s.mlp
                    reached(pool, dve_h2, b + 1)
                    reached(pool, dve_result, b - 1)
                    if not s.looped:
                        pool.wait_ge(shift_ready, 1)
                    G.tensor_tensor(h2s[1 - s.parity][:, :, :], h2[:, :, :],
                                    ln_shift[:, None, :].to_broadcast([P, TILES, DIM]), ALU.add).then_inc(pool_h2s, 1)
                if s.attn is not None:
                    b = s.attn
                    reached(pool, dve_hx, b + 1)
                    reached(pool, dve_h2, b)
                    G.tensor_tensor(hxb[:, :, :], hx[:, :, :], mlp_bias[:, None, :].to_broadcast([P, TILES, DIM]),
                                    ALU.add).then_inc(pool_hxb, 1)
                    if not s.looped and b == 0:
                        ternary(1)

            links = [3]

            def link(ins):
                links[0] += 1
                ins.then_inc(pool_chain, 1)
                pool.wait_ge(pool_chain, links[0])

            def biases():
                pool.wait_ge(rows_loaded, 16)
                G.tensor_tensor(mlp_bias[:, :], conv2_b_all, gamma_all, ALU.mult)
                link(G.tensor_tensor(bias_rest[:, :], proj_b_all, gamma_all, ALU.mult))
                link(G.tensor_tensor(bias_rest[:, :], bias_rest[:, :], attn_scale[:, 0:1].to_broadcast([P, DIM]),
                                     ALU.mult))
                for part in range(3):
                    at = slice(32 * part, 32 * part + 1)
                    G.tensor_copy(attn_bias[at, :], bias_rest[at, :]).then_inc(bias_ready, 1)
                    pool.wait_ge(bias_ready, part + 1)
                    if part < 2:
                        link(G.tensor_copy(bias_part[:, :], bias_rest[:, :]))
                        link(G.tensor_tensor(bias_rest[:, :], bias_rest[:, :], bias_part[:, :], ALU.subtract))

            def ternary(which):
                flat = (fc_q, ffn_q)[which][:, :, :].rearrange("p n f -> p (n f)")
                pool.wait_ge(compared, which + 1)
                G.tensor_tensor(flat, flat, below[which], ALU.subtract).then_inc(ternary_ready, 1)

            run(pool, body, {0: biases})

        @block.vector
        def _(dve):
            V = nc.vector
            links = [0]

            def link(ins):
                links[0] += 1
                ins.then_inc(setup_chain, 1)
                dve.wait_ge(setup_chain, links[0])

            def split(hi, lo, src):
                link(V.tensor_copy(hi, src))
                link(V.tensor_tensor(lo, src, hi, ALU.subtract))

            def split_scaled(hi, lo, raw, scale_cols):
                for i in range(GROUPS):
                    last = V.tensor_scalar(hi[:, i, :], raw[:, i, :], scale_cols[:, i:i + 1], None, ALU.mult)
                link(last)
                for i in range(GROUPS):
                    last = V.scalar_tensor_tensor(lo[:, i, :], raw[:, i, :], scale_cols[:, i:i + 1], hi[:, i, :],
                                                  ALU.mult, ALU.subtract)
                link(last)

            V.memset(pixels[0][64:P, FULL, :], 1.0)
            V.memset(pixels[1][64:P, FULL, :], 1.0)
            V.memset(tok_raw[64:P, FULL, :], 1.0).then_inc(ones_row_set, 1)

            def ternary_for_bias():
                dve.wait_ge(ternary_ready, 2)
                V.tensor_copy(ffn_q32, ffn_q[:, :, :])
                V.tensor_copy(ln_w_wide, ln_w_cols[:, :, None].to_broadcast([P, WIDE_TILES, P]))
                V.tensor_copy(ln_b_wide, ln_b_cols[:, :, None].to_broadcast([P, WIDE_TILES, P])
                              ).then_inc(wide_ready, 1)

            def embedding_weights():
                split_pixels(0, 0)
                dve.wait_ge(tok_loaded, 16 * 3)
                link(V.tensor_scalar(tok_hi[:, :, :], tok_raw[:, :, :], WEIGHT_SCALE, None, ALU.mult))
                link(V.scalar_tensor_tensor(tok_lo[:, :, :], tok_raw[:, :, :], WEIGHT_SCALE, tok_hi[:, :, :],
                                            ALU.mult, ALU.subtract))
                V.memset(spacer[:, :], 0.0).then_inc(tok_ready, 1)
                dve.wait_ge(columns_loaded, 16)
                link(V.tensor_scalar(cols_all[:, 0:2 * GROUPS], cols_all[:, 0:2 * GROUPS], RMS_FACTOR * WEIGHT_SCALE,
                                     None, ALU.mult))
                dve.wait_ge(qkv_loaded, 16)
                split_scaled(qkv_hi, qkv_lo, qkv_raw, scale1_cols)
                V.tensor_copy(spacer[:, :], qkv_lo[:, 0, 0:1]).then_inc(qkv_ready, 1)
                conv1_weights()

            def attention_weights():
                dve.wait_ge(setup_done, 1)
                dve.wait_ge(rows_loaded, 16)
                dve.wait_ge(proj_loaded, 16)
                for i in range(GROUPS):
                    last = V.scalar_tensor_tensor(proj_raw[:, i, :], proj_raw[:, i, :], WEIGHT_SCALE,
                                                  gamma_all, ALU.mult, ALU.mult)
                link(last)
                split(proj_hi[:, :, :], proj_lo[:, :, :], proj_raw[:, :, :])
                dve.wait_ge(conv2_loaded, 16)
                for i in range(HIDDEN_TILES):
                    last = V.scalar_tensor_tensor(conv2_raw[:, i, :], conv2_raw[:, i, :], WEIGHT_SCALE, gamma_all,
                                                  ALU.mult, ALU.mult)
                link(last)
                split(conv2_hi[:, :, :], conv2_lo[:, :, :], conv2_raw)

            def mean_absolute():
                dve.wait_ge(pe_absolute, 1)
                V.tensor_scalar(threshold[:, :, 0], D[:, 0:2], 1.0 / (WIDE * DIM), 1e-6, ALU.mult, ALU.add
                                ).then_inc(absolute_taken, 1)

            def compare(which):
                raw, above = ((fc_raw, fc_q), (ffn_raw, ffn_q))[which]
                if which == 0:
                    dve.wait_ge(fc_loaded, 16)
                    dve.wait_ge(ffn_loaded, 16)
                    dve.wait_ge(absolute_taken, 1)
                    V.tensor_scalar(threshold[:, :, 1], threshold[:, :, 0], 0.5, None, ALU.mult)
                    link(V.tensor_scalar(threshold[:, :, 2], threshold[:, :, 0], -0.5, None, ALU.mult))
                V.tensor_scalar(below[which], raw, threshold[:, which, 2:3], None, ALU.is_lt)
                V.tensor_scalar(above[:, :, :].rearrange("p n f -> p (n f)"), raw, threshold[:, which, 1:2], None,
                                ALU.is_gt).then_inc(compared, 1)

            def conv1_weights():
                dve.wait_ge(conv1_loaded, 16)
                split_scaled(conv1_hi, conv1_lo, conv1_raw, scale2_cols)

            def shift():
                dve.wait_ge(pe_shift, 1)
                V.tensor_copy(ln_weight_sum[:, :], D[:, DIM:2 * DIM])
                V.tensor_copy(ln_shift[:, :], D[:, 0:DIM]).then_inc(shift_ready, 1)

            def split_pixels(b, p):
                reached(dve, act_pixels, b + 1)
                reached(dve, pe_tok, b)
                V.tensor_tensor(pixels_lo[:, :, :], pixels[p][:, :, :], pixels_hi[:, :, :],
                                ALU.subtract).then_inc(dve_pixels, 1)

            def body(s):
                def low(dst, ps, hi, b, ready, war, war_count, done):
                    reached(dve, ready, b + 1)
                    reached(dve, war, war_count)
                    V.tensor_tensor(dst, ps, hi, ALU.subtract).then_inc(done, 1)

                def split_g(j):
                    b = s.ffn
                    reached(dve, act_g[j], b + 1)
                    reached(dve, pe_ffn[TILES - 1], b)
                    for n in (2 * j, 2 * j + 1):
                        last = V.tensor_scalar(gw_hi[:, n, :], g[:, n, :], ln_w_cols[:, n:n + 1], None, ALU.mult)
                    last.then_inc(dve_gw_hi[j], 1)
                    reached(dve, dve_gw_hi[j], b + 1)
                    for n in (2 * j, 2 * j + 1):
                        last = V.scalar_tensor_tensor(gw_lo[:, n, :], g[:, n, :], ln_w_cols[:, n:n + 1], gw_hi[:, n, :],
                                                      ALU.mult, ALU.subtract)
                    last.then_inc(dve_gw[j], 1)

                def add_squares():
                    b = s.ffn
                    for j in range(1, PAIRS):
                        reached(dve, act_g_square[j], b + 1)
                        if j == 1:
                            reached(dve, act_g_square[0], b + 1)
                            reached(dve, square_total_done, b)
                            first = g_square[:, 0:2, :]
                        else:
                            reached(dve, square_part_done[j - 1], b + 1)
                            first = square_part[:, :, :]
                        V.tensor_tensor(square_part[:, :, :], first, g_square[:, 2 * j:2 * j + 2, :],
                                        ALU.add).then_inc(square_part_done[j], 1)
                    reached(dve, square_part_done[PAIRS - 1], b + 1)
                    reached(dve, total_split[1], b)
                    V.tensor_tensor(square_total[:, :], square_part[:, 0, :], square_part[:, 1, :],
                                    ALU.add).then_inc(square_total_done, 1)

                def low_squares():
                    b = s.ffn
                    reached(dve, act_total_hi[1], b + 1)
                    V.tensor_tensor(total_lo[:, 1, :], square_total[:, :], total_hi[:, 1, :],
                                    ALU.subtract).then_inc(total_split[1], 1)

                def means():
                    b = s.finish
                    reached(dve, pe_sums, b + 1)
                    reached(dve, dve_centred, b)
                    V.tensor_scalar(g_mean[:, :], sums_ps[:, 0:TILES], 1.0 / WIDE, None, ALU.mult)
                    V.tensor_scalar(g_minus_mean[:, :], sums_ps[:, 0:TILES], -1.0 / WIDE, None, ALU.mult)
                    V.tensor_scalar(g_square_mean[:, :], sums_ps[:, TILES:2 * TILES], 1.0 / (WIDE * SQUARE_SCALE ** 2),
                                    None, ALU.mult).then_inc(dve_g_means, 1)

                def centre():
                    b, p = s.finish, 1 - s.parity
                    reached(dve, dve_g_means, b + 1)
                    V.tensor_tensor(g_mean_square[:, :], g_mean[:, :], g_mean[:, :], ALU.mult).then_inc(dve_g_mean_square, 1)
                    for t in range(TILES):
                        reached(dve, act_product[t], b + 1)
                    stores = s.pair - 2 if s.parity == 0 else s.pair - 1
                    if s.looped or stores > 0:
                        dve.wait_ge(stored[p], 16 * stores)

                    def take_off(t):
                        return V.scalar_tensor_tensor(result[p][:, t, :], ln_weight_sum[:, :], g_minus_mean[:, t:t + 1],
                                                      product[:, t, :], ALU.mult, ALU.add)
                    take_off(0)
                    reached(dve, dve_g_mean_square, b + 1)
                    V.tensor_tensor(g_spread[:, :], g_square_mean[:, :], g_mean_square[:, :],
                                    ALU.subtract).then_inc(dve_g_spread, 1)
                    take_off(1)
                    reached(dve, dve_g_spread, b + 1)
                    reached(dve, pool_g_rstd, b)
                    V.tensor_scalar(g_var[:, :], g_spread[:, :], 0.0, LN_EPS, ALU.max, ALU.add).then_inc(dve_g_var, 1)
                    take_off(2).then_inc(dve_centred, 1)

                def finish():
                    b, p = s.finish, 1 - s.parity
                    reached(dve, dve_centred, b + 1)
                    reached(dve, pool_g_rstd, b + 1)
                    reached(dve, pool_h2s, b + 1)
                    for t in range(TILES):
                        last = V.scalar_tensor_tensor(result[p][:, t, :], result[p][:, t, :], g_rstd[:, t:t + 1],
                                                      h2s[p][:, t, :], ALU.mult, ALU.add)
                    last.then_inc(dve_result, 1)

                if s.attn is not None:
                    b = s.attn
                    reached(dve, act_k01, b + 1)
                    reached(dve, pe_kv, b)
                    V.tensor_scalar(v[:, 0:2, :, 0:P].rearrange("p t g n -> p (t g) n"),
                                    kv01_ps[:, :, DIM:2 * DIM].rearrange("p t (g n) -> p t g n", g=GROUPS),
                                    1.0 / WEIGHT_SCALE, None, ALU.mult).then_inc(dve_v01, 1)
                    reached(dve, act_k2, b + 1)
                    V.tensor_scalar(v[:, 2, :, 0:P], kv2_ps[:, DIM:2 * DIM].rearrange("p (g n) -> p g n", g=GROUPS),
                                    1.0 / WEIGHT_SCALE, None, ALU.mult).then_inc(dve_v2, 1)
                    if not s.looped and b == 0:
                        mean_absolute()
                if s.mlp is not None:
                    low(xT_lo[:, :, :], xT_ps, xT_hi[:, :, :], s.mlp, act_xT, pe_hid23, s.mlp, dve_xT)
                if s.ffn is not None:
                    low(hT_lo[:, :, :], hT_ps, hT_hi[:, :, :], s.ffn, act_hT, pe_g[PAIRS - 1], s.ffn, dve_hT)
                if s.finish is not None and s.attn is not None:
                    means()
                    centre()
                if s.attn is not None:
                    b = s.attn
                    reached(dve, act_q, b + 1)
                    reached(dve, pe_read, b)
                    V.tensor_scalar(q_hi[:, :, :], q[:, :, :], Q_SCALE, None, ALU.mult).then_inc(dve_q_hi, 1)
                    reached(dve, dve_q_hi, b + 1)
                    V.scalar_tensor_tensor(q_lo[:, :, :], q[:, :, :], Q_SCALE, q_hi[:, :, :], ALU.mult,
                                           ALU.subtract).then_inc(dve_q, 1)
                if s.finish is not None and s.attn is not None:
                    finish()
                if s.mlp is not None:
                    b = s.mlp
                    for at, ready, hi_done, done in ((0, act_hid01, dve_hid01_hi, dve_hid01),
                                                     (2, act_hid23, dve_hid23_hi, dve_hid23)):
                        reached(dve, ready, b + 1)
                        reached(dve, pe_mlp, b)
                        V.tensor_scalar(hid_hi[:, at:at + 2, :], hid[:, at:at + 2, :], GELU_SCALE, None,
                                        ALU.mult).then_inc(hi_done, 1)
                        reached(dve, hi_done, b + 1)
                        V.scalar_tensor_tensor(hid_lo[:, at:at + 2, :], hid[:, at:at + 2, :], GELU_SCALE,
                                               hid_hi[:, at:at + 2, :], ALU.mult, ALU.subtract).then_inc(done, 1)
                if s.attn is not None:
                    b = s.attn
                    reached(dve, pe_kv, b + 1)
                    reached(dve, dve_kv, b)
                    for n in range(GROUPS):
                        V.scalar_tensor_tensor(kv[:, n, 0:P], kv_ps[:, n, 0:P], KV_SCALE,
                                               block_mask[:, :, :].rearrange("p a b -> p (a b)"),
                                               ALU.mult, ALU.mult)
                        last = V.tensor_scalar(kv[:, n, P:P + GROUP_HEADS], head_mask[:, :],
                                               kv_ps[:, n, P:P + 1], KV_SCALE, ALU.mult, ALU.mult)
                    last.then_inc(dve_kv_masked, 1)
                    reached(dve, dve_kv_masked, b + 1)
                    V.tensor_copy(kv_hi[:, :, :], kv[:, :, :]).then_inc(dve_kv_hi, 1)
                    reached(dve, dve_kv_hi, b + 1)
                    V.tensor_tensor(kv_lo[:, :, :], kv[:, :, :], kv_hi[:, :, :], ALU.subtract).then_inc(dve_kv, 1)
                if s.finish is not None and s.ffn is None:
                    means()
                    centre()
                    finish()
                if s.ffn is not None:
                    split_g(0)
                    split_g(1)
                if s.mlp is not None:
                    b = s.mlp
                    reached(dve, pe_mlp, b + 1)
                    reached(dve, pool_hxb, b + 1)
                    reached(dve, pool_h2s, b)
                    V.scalar_tensor_tensor(h2[:, :, :], mlp_ps, 1.0 / MLP_SCALE, hxb[:, :, :], ALU.mult,
                                           ALU.add).then_inc(dve_h2, 1)
                    reached(dve, dve_h2, b + 1)
                    for t in range(TILES):
                        last = V.bn_stats(stats2[:, t, :], h2[:, t, :])
                    last.then_inc(dve_stats2, 1)
                    reached(dve, dve_stats2, b + 1)
                    V.memset(spacer[:, :], 0.0)
                    for t in range(TILES):
                        last = V.bn_aggr(mv2[:, t, :], stats2[:, t, :])
                    last.then_inc(dve_mv2, 1)
                if s.attn is not None:
                    b = s.attn
                    reached(dve, pe_read, b + 1)
                    V.tensor_scalar(den[:, :, :, :], read_ps[:, :, :, P:ND], DEN_EPS, 1.0 / OUT_SCALE,
                                    ALU.add, ALU.mult).then_inc(dve_den, 1)
                    reached(dve, dve_den, b + 1)
                    V.reciprocal(z[:, :, :, :], den[:, :, :, :]).then_inc(dve_z, 1)
                    reached(dve, dve_z, b + 1)
                    reached(dve, pe_readT, b)
                    for n in range(GROUPS):
                        last = V.tensor_tensor(
                            read[:, :, n * P:(n + 1) * P].rearrange("p t (a c) -> p t a c", c=HEAD),
                            read_ps[:, n, :, 0:P].rearrange("p t (a c) -> p t a c", c=HEAD),
                            z[:, n, :, :][:, :, :, None].to_broadcast([P, TILES, GROUP_HEADS, HEAD]), ALU.mult)
                    last.then_inc(dve_read, 1)
                    if not s.looped and b == 0:
                        compare(0)
                    elif not s.looped and b == 1:
                        ternary_for_bias()
                if s.ffn is not None:
                    split_g(2)
                    split_g(3)
                if s.embed is not None:
                    b, p = s.embed, 1 - s.parity
                    reached(dve, act_h, b + 1)
                    dve.wait_ge(text_loaded[p], 16 * (s.pair + 1 if s.parity == 0 else s.pair + 2))
                    for t in range(TILES):
                        last = V.bn_stats(stats1[:, t, :], h[p][:, t, :])
                    last.then_inc(dve_stats1, 1)
                    reached(dve, dve_stats1, b + 1)
                    reached(dve, pool_ratio_a, b)
                    V.memset(spacer[:, :], 0.0)
                    for t in range(TILES):
                        last = V.bn_aggr(mv1[:, t, :], stats1[:, t, :])
                    last.then_inc(dve_mv1, 1)
                if s.attn is not None:
                    low(readT_lo[:, :, :], readT_ps, readT_hi[:, :, :], s.attn, act_readT, pe_attn, s.attn, dve_readT)
                if s.embed is not None:
                    b, p = s.embed, 1 - s.parity
                    reached(dve, pool_rstd1, b + 1)
                    reached(dve, pe_aT[1], b - 1)
                    for t in range(TILES):
                        last = V.tensor_scalar(a[p][:, t, :], h[p][:, t, :], mv1[:, t, 0:1], rstd1[:, t:t + 1],
                                               ALU.subtract, ALU.mult)
                    last.then_inc(dve_a, 1)
                if s.fetch is not None:
                    split_pixels(s.fetch, s.parity)
                if s.attn is not None:
                    b, p = s.attn, s.parity
                    reached(dve, pe_attn, b + 1)
                    reached(dve, pool_ratio, b + 1)
                    reached(dve, act_squares1, b)
                    for t in range(TILES):
                        last = V.scalar_tensor_tensor(x1[:, t, :], a[p][:, t, :], ratio[p][:, t:t + 1],
                                                      attn_ps[:, t, :], ALU.mult, ALU.add)
                    last.then_inc(dve_x1, 1)
                if s.embed is not None:
                    for c in range(GROUPS):
                        low(aT_lo[:, c, :], aT_ps[:, c, :], aT_hi[:, c, :], s.embed, act_aT[c], pe_q, s.embed, dve_aT[c])
                if s.attn is not None:
                    b, p = s.attn, s.parity
                    reached(dve, dve_x1, b + 1)
                    reached(dve, pool_hxb, b)
                    V.scalar_tensor_tensor(hx[:, :, :], x1[:, :, :], 1.0 / ATTN_SCALE, h[p][:, :, :], ALU.mult,
                                           ALU.add).then_inc(dve_hx, 1)
                if s.mlp is not None:
                    b = s.mlp
                    reached(dve, pool_rstd2, b + 1)
                    reached(dve, pe_hT, b)
                    for t in range(TILES):
                        last = V.tensor_scalar(hn[:, t, :], h2[:, t, :], mv2[:, t, 0:1], rstd2[:, t:t + 1],
                                               ALU.subtract, ALU.mult)
                    last.then_inc(dve_hn, 1)
                if s.attn is not None:
                    b = s.attn
                    reached(dve, pool_rms, b + 1)
                    reached(dve, pe_xT, b)
                    for t in range(TILES):
                        last = V.tensor_scalar(xn[:, t, :], x1[:, t, :], rms[:, t:t + 1], DIM ** 0.5, ALU.mult, ALU.mult)
                    last.then_inc(dve_xn, 1)
                if s.ffn is not None and s.attn is None:
                    means()
                    if squares_by_vector(s.ffn):
                        add_squares()
                        low_squares()
                    centre()
                    finish()

            run(dve, body, {-1: embedding_weights, 0: attention_weights, 1: lambda: compare(1), 2: shift})

        @block.scalar
        def _(act):
            S = nc.scalar
            act.wait_ge(setup_done, 1)
            S.activation(unread_exp[:, :], eps[:, 0:1], ACT.Exp).then_inc(act_exp_table, 1)
            def high_pixels(b, p, loaded):
                act.wait_ge(pixels_loaded[p], 32 * loaded)
                reached(act, pe_tok, b)
                S.activation(pixels_hi[:, :, :], pixels[p][:, :, :], ACT.Copy).then_inc(act_pixels, 1)

            def absolute_sums():
                act.wait_ge(fc_loaded, 16)
                act.wait_ge(ffn_loaded, 16)
                for n, raw in enumerate((fc_raw, ffn_raw)):
                    last = S.activation(unread_abs[n], raw, ACT.Abs, accum_out=absolute_sum[:, n:n + 1])
                last.then_inc(absolute_summed, 1)

            def body(s):
                def high(dst, ps, b, ready, war, war_count, done):
                    reached(act, ready, b + 1)
                    reached(act, war, war_count)
                    S.activation(dst, ps, ACT.Copy).then_inc(done, 1)

                def gelu(j):
                    b = s.ffn
                    reached(act, pe_g[j], b + 1)
                    reached(act, dve_gw[j], b)
                    reached(act, act_g_square[j], b)
                    reached(act, pool_g_part[max(j, 1)], b)
                    S.activation(g[:, 2 * j:2 * j + 2, :], g_ps[j], ACT.Gelu).then_inc(act_g[j], 1)

                def high_total(n, b):
                    reached(act, (pool_g_total, square_total_done)[n], b + 1)
                    reached(act, pe_sums, b)
                    S.activation(total_hi[:, n, :], (g_total, square_total)[n][:, :], ACT.Copy
                                 ).then_inc(act_total_hi[n], 1)

                def take_product(t):
                    b = s.ffn
                    reached(act, pe_ffn[t], b + 1)
                    reached(act, dve_centred, b)
                    S.activation(product[:, t, :], ffn_ps[t], ACT.Copy).then_inc(act_product[t], 1)

                def square(j):
                    b = s.ffn
                    reached(act, act_g[j], b + 1)
                    reached(act, square_part_done[max(j, 1)], b)
                    S.activation(g_square[:, 2 * j:2 * j + 2, :], g[:, 2 * j:2 * j + 2, :],
                                 ACT.Square, scale=SQUARE_SCALE).then_inc(act_g_square[j], 1)

                if s.attn is not None:
                    b = s.attn
                    reached(act, act_k, b)
                    reached(act, pe_kv01, b + 1)
                    S.activation(k_square[:, 0:2, :], kv01_ps[:, :, 0:DIM], ACT.Square,
                                 scale=1.0 / WEIGHT_SCALE).then_inc(act_k01, 1)
                    reached(act, pe_kv2, b + 1)
                    S.activation(k_square[:, 2, :], kv2_ps[:, 0:DIM], ACT.Square,
                                 scale=1.0 / WEIGHT_SCALE).then_inc(act_k2, 1)
                if s.mlp is not None:
                    high(xT_hi[:, :, :], xT_ps, s.mlp, pe_xT, pe_hid23, s.mlp, act_xT)
                if s.ffn is not None:
                    high(hT_hi[:, :, :], hT_ps, s.ffn, pe_hT, pe_g[PAIRS - 1], s.ffn, act_hT)
                if s.attn is not None:
                    b = s.attn
                    reached(act, act_k2, b + 1)
                    reached(act, pe_kv, b)
                    S.activation(k[:, :, :], k_square[:, :, :], ACT.Exp, scale=-0.5).then_inc(act_k, 1)
                    reached(act, pe_q, b + 1)
                    S.activation(q_square[:, :, :], q_ps, ACT.Square, scale=1.0 / WEIGHT_SCALE
                                 ).then_inc(act_q_square, 1)
                    reached(act, act_q_square, b + 1)
                    reached(act, dve_q, b)
                    S.activation(q[:, :, :], q_square[:, :, :], ACT.Exp, scale=-0.5).then_inc(act_q, 1)
                if s.mlp is not None:
                    b = s.mlp
                    for at, ps, ready, split_done, done in ((0, hid01_ps, pe_hid01, dve_hid01, act_hid01),
                                                            (2, hid23_ps, pe_hid23, dve_hid23, act_hid23)):
                        reached(act, ready, b + 1)
                        reached(act, split_done, b)
                        for n in range(2):
                            last = S.activation(hid[:, at + n, :], ps[:, n, :], ACT.Gelu,
                                                bias=conv1_bias[:, at + n:at + n + 1], scale=1.0 / WEIGHT_SCALE)
                        last.then_inc(done, 1)
                if s.ffn is not None:
                    gelu(0)
                    gelu(1)
                    square(0)
                    square(1)
                if s.ffn is not None and last_but_one(s.finish):
                    high_total(0, s.finish)
                    high_total(1, s.finish)
                if s.ffn is not None:
                    gelu(2)
                    square(2)
                    gelu(3)
                    square(3)
                if s.embed is not None:
                    b, p = s.embed, 1 - s.parity
                    reached(act, pe_tok, b + 1)
                    reached(act, dve_hx, b - 1)
                    S.activation(h[p][:, 0:IMAGE_TILES, :], tok_ps, ACT.Copy, scale=1.0 / WEIGHT_SCALE
                                 ).then_inc(act_h, 1)
                if s.attn is not None:
                    high(readT_hi[:, :, :], readT_ps, s.attn, pe_readT, pe_attn, s.attn, act_readT)
                if s.fetch is not None:
                    high_pixels(s.fetch, s.parity, s.pair + 2)
                if s.ffn is not None:
                    if squares_by_vector(s.ffn):
                        high_total(0, s.ffn)
                        high_total(1, s.ffn)
                    take_product(0)
                    take_product(1)
                if s.ffn is not None and s.attn is not None:
                    high_total(0, s.ffn)
                if s.embed is not None:
                    for c in range(GROUPS):
                        high(aT_hi[:, c, :], aT_ps[:, c, :], s.embed, pe_aT[c], pe_q, s.embed, act_aT[c])
                if s.attn is not None:
                    b = s.attn
                    reached(act, dve_x1, b + 1)
                    reached(act, pool_rms, b)
                    for t in range(TILES):
                        last = S.activation(unread1[:, t, :], x1[:, t, :], ACT.Square, accum_out=squares1[:, t:t + 1])
                    last.then_inc(act_squares1, 1)
                if s.ffn is not None:
                    take_product(2)
                if s.embed is not None:
                    reached(act, act_exp_table, s.embed + 1)
                    S.activation(unread_exp[:, :], eps[:, 0:1], ACT.Exp).then_inc(act_exp_table, 1)
                if s.ffn is not None and s.attn is not None:
                    high_total(1, s.ffn)

            def ahead_of_embedding():
                high_pixels(0, 0, 1)
                act.wait_ge(columns_loaded, 16)

            run(act, body, {-1: ahead_of_embedding, 0: absolute_sums})

        @block.tensor
        def _(pe):
            T = nc.tensor
            def ahead_of_embedding():
                pe.wait_ge(tok_ready, 1)

            def ahead_of_attention():
                pe.wait_ge(qkv_ready, 1)

            def mean_absolute():
                pe.wait_ge(setup_done, 1)
                pe.wait_ge(absolute_summed, 1)
                T.matmul(D[:, 0:2], ones_f[:, :], absolute_sum[:, :], start=True, stop=True).then_inc(pe_absolute, 1)

            def ahead_of_ffn():
                pe.wait_ge(wide_ready, 1)
                pe.wait_ge(dve_readT, 2)
                for n in range(WIDE_TILES):
                    last = T.matmul(D[:, 0:DIM], ln_b_wide[:, n, :], ffn_q32[:, n, :], start=n == 0,
                                    stop=n == WIDE_TILES - 1)
                for n in range(WIDE_TILES):
                    last = T.matmul(D[:, DIM:2 * DIM], ln_w_wide[:, n, :], ffn_q32[:, n, :], start=n == 0,
                                    stop=n == WIDE_TILES - 1)
                last.then_inc(pe_shift, 1)

            def three(dst, pairs, bias=None):
                products = []
                for (s_hi, s_lo), (m_hi, m_lo) in pairs:
                    products += [(s_hi, m_hi), (s_hi, m_lo), (s_lo, m_hi)]
                if bias is not None:
                    products.append((ones_bf[:, :], bias))
                for n, (stationary, mov) in enumerate(products):
                    last = T.matmul(dst, stationary, mov, start=n == 0, stop=n == len(products) - 1)
                return last

            def tile(x, c, t):
                return x[:, c, t * P:(t + 1) * P]

            def turn(ps, src, groups_done=None):
                for c in range(GROUPS):
                    for t in range(TILES):
                        last = T.transpose(ps[:, c, t * P:(t + 1) * P], src[:, t, c * P:(c + 1) * P], identity[:, :])
                    if groups_done:
                        last.then_inc(groups_done[c], 1)
                return last

            def body(s):
                def first_keys_values(b):
                    hi = [(tile(aT_hi, c, 0), part[:, c, DIM:]) for c in range(GROUPS) for part in (qkv_hi, qkv_lo)]
                    for c in range(GROUPS):
                        reached(pe, act_aT[c], b + 1)
                    for n, (stationary, mov) in enumerate(hi):
                        T.matmul(kv01_ps[:, 0, :], stationary, mov, start=n == 0, stop=False)
                    for c in range(GROUPS):
                        reached(pe, dve_aT[c], b + 1)
                        T.matmul(kv01_ps[:, 0, :], tile(aT_lo, c, 0), qkv_hi[:, c, DIM:], start=False,
                                 stop=c == GROUPS - 1)

                def keys_values(t, ps):
                    return three(ps, [((tile(aT_hi, c, t), tile(aT_lo, c, t)),
                                             (qkv_hi[:, c, DIM:], qkv_lo[:, c, DIM:])) for c in range(GROUPS)])

                def wide(j):
                    for half in range(2):
                        w = slice((2 * j + half) * P, (2 * j + half + 1) * P)
                        n = 0
                        for c in range(GROUPS):
                            for part in (hT_hi, hT_lo):
                                last = T.matmul(g_ps[j][:, half, :], fc_q[:, c, w], part[:, c, :], start=n == 0,
                                                stop=n == 2 * GROUPS - 1)
                                n += 1
                    last.then_inc(pe_g[j], 1)

                def narrow(t):
                    n = 0
                    for w in range(WIDE_TILES):
                        if t == 0 and w % 2 == 0:
                            reached(pe, dve_gw[w // 2], s.ffn + 1)
                        for part in (gw_hi, gw_lo):
                            last = T.matmul(ffn_ps[t], tile(part, w, t), ffn_q[:, w, :], start=n == 0,
                                            stop=n == 2 * WIDE_TILES - 1)
                            n += 1
                    last.then_inc(pe_ffn[t], 1)

                def narrow_together():
                    for w in range(WIDE_TILES):
                        if w % 2 == 0:
                            reached(pe, dve_gw[w // 2], s.ffn + 1)
                        for t in range(TILES):
                            for part in (gw_hi, gw_lo):
                                last = T.matmul(ffn_ps[t], tile(part, w, t), ffn_q[:, w, :],
                                                start=w == 0 and part is gw_hi,
                                                stop=w == WIDE_TILES - 1 and part is gw_lo)
                            if w == WIDE_TILES - 1:
                                last.then_inc(pe_ffn[t], 1)

                def sums():
                    for n in range(2):
                        reached(pe, total_split[n], s.finish + 1)
                        for t in range(TILES):
                            at = n * TILES + t
                            for part in (total_hi, total_lo):
                                last = T.matmul(sums_ps[:, at:at + 1], tile(part, n, t), ones_16[:, 0:1],
                                                start=part is total_hi, stop=part is total_lo)
                    last.then_inc(pe_sums, 1)

                if s.attn is not None:
                    b = s.attn
                    reached(pe, dve_x1, b)
                    first_keys_values(b)
                    keys_values(1, kv01_ps[:, 1, :]).then_inc(pe_kv01, 1)
                    reached(pe, dve_readT, b)
                    keys_values(2, kv2_ps).then_inc(pe_kv2, 1)
                if s.mlp is not None:
                    b = s.mlp
                    reached(pe, dve_xn, b + 1)
                    if s.attn is not None:
                        reached(pe, dve_aT[1], s.attn + 1)
                    turn(xT_ps, xn).then_inc(pe_xT, 1)
                if s.ffn is not None:
                    b = s.ffn
                    reached(pe, dve_hn, b + 1)
                    if s.attn is not None:
                        reached(pe, act_k01, s.attn + 1)
                        reached(pe, dve_v01, s.attn + 1)
                    else:
                        reached(pe, dve_x1, BATCHES)
                        reached(pe, dve_g_means, s.finish)
                    if s.finish is not None and s.attn is not None:
                        sums()
                    turn(hT_ps, hn).then_inc(pe_hT, 1)
                if s.attn is not None:
                    b = s.attn
                    reached(pe, act_h, b + 1)
                    if s.ffn is not None:
                        for t in range(2):
                            reached(pe, act_product[t], s.ffn)
                    for c in range(GROUPS):
                        w = slice(c * P, (c + 1) * P)
                        last = three(q_ps[:, c, :], [((qkv_hi[:, d, w], qkv_lo[:, d, w]),
                                                            (aT_hi[:, d, :], aT_lo[:, d, :])) for d in range(GROUPS)])
                    last.then_inc(pe_q, 1)
                if s.mlp is not None:
                    b = s.mlp
                    reached(pe, dve_xT, b + 1)
                    for n, (ps, done) in enumerate(((hid01_ps, pe_hid01), (hid23_ps, pe_hid23))):
                        if n and s.attn is not None:
                            reached(pe, act_q_square, s.attn + 1)
                        elif n and s.ffn is not None:
                            for t in range(2):
                                reached(pe, act_product[t], s.ffn)
                        for m in range(2):
                            w = slice((2 * n + m) * P, (2 * n + m + 1) * P)
                            last = three(ps[:, m, :], [((conv1_hi[:, c, w], conv1_lo[:, c, w]),
                                                              (xT_hi[:, c, :], xT_lo[:, c, :])) for c in range(GROUPS)])
                        last.then_inc(done, 1)
                if s.ffn is not None:
                    b = s.ffn
                    reached(pe, dve_hT, b + 1)
                    if s.attn is not None:
                        reached(pe, act_k2, s.attn + 1)
                        reached(pe, dve_v2, s.attn + 1)
                    reached(pe, act_product[2], b)
                    wide(0)
                if s.attn is not None:
                    b = s.attn
                    reached(pe, act_k, b + 1)
                    reached(pe, dve_v2, b + 1)
                    reached(pe, dve_v01, b + 1)
                    if s.ffn is not None:
                        reached(pe, dve_hT, s.ffn + 1)
                    if s.finish is not None:
                        reached(pe, dve_g_means, s.finish + 1)
                    for n in range(GROUPS):
                        for t in range(TILES):
                            last = T.matmul(kv_ps[:, n, :], k[:, t, n * P:(n + 1) * P], v[:, t, n, :],
                                            start=t == 0, stop=t == TILES - 1)
                    last.then_inc(pe_kv, 1)
                    if not s.looped and s.attn == 0:
                        mean_absolute()
                if s.ffn is not None:
                    if s.mlp is not None:
                        reached(pe, act_hid01, s.mlp + 1)
                    wide(1)
                if s.mlp is not None:
                    b = s.mlp
                    reached(pe, dve_hid01, b + 1)
                    reached(pe, dve_hid23, b + 1)
                    for t in range(TILES):
                        last = three(mlp_ps[:, t, :],
                                     [((tile(hid_hi, n, t), tile(hid_lo, n, t)), (conv2_hi[:, n, :], conv2_lo[:, n, :]))
                                      for n in range(HIDDEN_TILES)])
                    last.then_inc(pe_mlp, 1)
                if s.ffn is not None:
                    if s.attn is not None:
                        reached(pe, dve_kv, s.attn + 1)
                    wide(2)
                if s.attn is not None:
                    b = s.attn
                    reached(pe, dve_kv, b + 1)
                    reached(pe, dve_q, b + 1)
                    if s.ffn is not None:
                        reached(pe, act_g[0], s.ffn + 1)
                    elif b == 0:
                        pe.wait_ge(absolute_taken, 1)
                    for t in range(TILES):
                        for n in range(GROUPS):
                            last = three(read_ps[:, n, t, :],
                                         [((tile(q_hi, n, t), tile(q_lo, n, t)), (kv_hi[:, n, :], kv_lo[:, n, :]))])
                    last.then_inc(pe_read, 1)
                if s.ffn is not None:
                    reached(pe, act_g[1], s.ffn + 1)
                    wide(3)
                if s.finish is not None and s.attn is None:
                    reached(pe, act_g[2], (s.ffn if s.ffn is not None else s.finish) + 1)
                    sums()
                if s.embed is not None:
                    b, p = s.embed, 1 - s.parity
                    reached(pe, dve_pixels, b + 1)
                    if s.mlp is not None:
                        reached(pe, dve_h2, s.mlp + 1)
                    elif s.attn is not None:
                        reached(pe, act_q_square, s.attn + 1)
                    for t in range(IMAGE_TILES):
                        last = three(tok_ps[:, t, :],
                                     [tuple(tuple(x[0:P if n < FULL else REST + 1, n, cut] for x in pair)
                                            for pair, cut in (((pixels_hi, pixels_lo), slice(t * P, (t + 1) * P)),
                                                              ((tok_hi, tok_lo), slice(0, DIM))))
                                      for n in range(FULL + 1)])
                    last.then_inc(pe_tok, 1)
                if s.attn is not None:
                    b = s.attn
                    reached(pe, dve_read, b + 1)
                    turn(readT_ps, read).then_inc(pe_readT, 1)
                if s.ffn is not None:
                    if s.mlp is not None:
                        reached(pe, dve_h2, s.mlp + 1)
                    if s.attn is not None:
                        narrow(0)
                        if s.embed is not None:
                            reached(pe, act_h, s.embed + 1)
                        narrow(1)
                    else:
                        reached(pe, act_g[0], s.ffn + 1)
                        narrow_together()
                if s.attn is not None:
                    b = s.attn
                    reached(pe, dve_readT, b + 1)
                    if not s.looped and b == 0:
                        pe.wait_ge(bias_ready, 3)
                    if s.ffn is not None:
                        reached(pe, act_g[2], s.ffn + 1)
                    for t in range(TILES):
                        last = three(attn_ps[:, t, :],
                                     [((tile(readT_hi, c, t), tile(readT_lo, c, t)), (proj_hi[:, c, :], proj_lo[:, c, :]))
                                      for c in range(GROUPS)], bias=attn_bias[:, :])
                    last.then_inc(pe_attn, 1)
                if s.embed is not None:
                    b, p = s.embed, 1 - s.parity
                    reached(pe, dve_a, b + 1)
                    if s.ffn is not None:
                        reached(pe, act_g[3], s.ffn + 1)
                    elif s.mlp is not None:
                        reached(pe, act_hid01, s.mlp + 1)
                    turn(aT_ps, a[p], pe_aT)
                if s.ffn is not None and s.attn is not None:
                    reached(pe, dve_readT, s.attn + 1)
                    narrow(2)

            run(pe, body, {-1: ahead_of_embedding, 0: ahead_of_attention, 2: ahead_of_ffn})


_INS = ["image", "text", "tok_w", "tok_b", "columns", "rows", "qkv_w", "proj_w", "conv1_w", "conv2_w",
        "fc_w", "ffn_w"]


def kernel(x, txt, L0_tok_W, L0_tok_b, L0_attn_scale1, L0_attn_scale2, L0_attn_gamma, L0_attn_qkv_w,
           L0_attn_proj_w, L0_attn_proj_b, L0_attn_conv1_w, L0_attn_conv1_b, L0_attn_conv2_w,
           L0_attn_conv2_b, L0_ffn_W_fc, L0_ffn_ln_w, L0_ffn_ln_b, L0_ffn_W_proj):
    import concourse.bacc as _bacc
    from concourse.bass_utils import run_bass_kernel_spmd as _run

    image = np.asarray(x).reshape(BATCHES, CHANNELS, GRID, PATCH, GRID, PATCH).transpose(0, 1, 3, 5, 2, 4)
    image = image.reshape(BATCHES, PIXELS, PATCHES)
    columns = np.concatenate([np.asarray(c).reshape(-1, P).T for c in (
        L0_attn_scale1, L0_attn_scale2, L0_attn_conv1_b, L0_ffn_ln_b, L0_ffn_ln_w)], axis=1)
    rows = np.concatenate([np.asarray(r)[None] for r in (
        L0_attn_gamma, L0_attn_proj_b, L0_attn_conv2_b)], axis=1)
    given = [image, txt, np.asarray(L0_tok_W).T, L0_tok_b, columns, rows,
             np.asarray(L0_attn_qkv_w).T, np.asarray(L0_attn_proj_w).T, np.asarray(L0_attn_conv1_w).T,
             np.asarray(L0_attn_conv2_w).T, np.asarray(L0_ffn_W_fc).T, np.asarray(L0_ffn_W_proj).T]
    nc = _bacc.Bacc("TRN2", target_bir_lowering=False, num_devices=1)
    arrays, args = {}, []
    for name, array in zip(_INS, given):
        array = np.ascontiguousarray(array)
        arrays[f"in_{name}"] = array
        args.append(nc.dram_tensor(f"in_{name}", array.shape, mybir.dt.from_np(array.dtype),
                                   kind="ExternalInput").ap())
    out = nc.dram_tensor("out", (BATCHES, TOKENS, DIM), mybir.dt.float32, kind="ExternalOutput").ap()
    build(nc, *args, out)
    r = _run(nc, [arrays], core_ids=[0])
    return r.results[0]["out"]
```
